# Optimizing a Trainium2 kernel written in Bass

```python
import numpy as np
import jax
import jax.numpy as jnp

def _softmax(x, axis=-1):
    return jax.nn.softmax(x, axis=axis)

def _gelu(x):
    return jax.nn.gelu(x, approximate=True)

def _silu(x):
    return jax.nn.silu(x)

def _sigmoid(x):
    return jax.nn.sigmoid(x)

def _layernorm(x, axis=-1, eps=1e-05):
    m = jnp.mean(x, axis=axis, keepdims=True)
    v = jnp.var(x, axis=axis, keepdims=True)
    return (x - m) / jnp.sqrt(v + eps)

def _scatter_add(tgt, idx, src, axis=0):
    return tgt.at[idx].add(src)

def _segment_sum(src, seg, n):
    return jax.ops.segment_sum(src, seg, n)
kernel_name = 'mk_adaln_d2_jaxref_r8_286448'

def setup_inputs(seed: int=0):
    np.random.seed(seed)
    _w = jnp.asarray

    def _L0_attn_setup():
        import jax, jax.numpy as jnp
        import numpy as np
        D_MODEL = 128
        N_LAYER = 4
        EXPAND = 2
        HEADDIM = 32
        D_STATE = 128
        D_CONV = 4
        NGROUPS = 1
        D_INNER = EXPAND * D_MODEL
        NHEADS = D_INNER // HEADDIM
        CONV_DIM = D_INNER + 2 * NGROUPS * D_STATE
        D_IN_PROJ = 2 * D_INNER + 2 * NGROUPS * D_STATE + NHEADS
        BATCH, SEQLEN = (4, 256)

        def _rmsnorm(x, w, eps=1e-05):
            return x * jax.lax.rsqrt(jnp.mean(x * x, axis=-1, keepdims=True) + eps) * w

        def _mamba2_layer(h, Wi, cw, cb, dtb, Alog, Dh, gw, Wo):
            B, L, _ = h.shape
            zxbcdt = h @ Wi
            z, xBC, dt = jnp.split(zxbcdt, [D_INNER, D_INNER + CONV_DIM], axis=-1)
            xp = jnp.pad(xBC, ((0, 0), (D_CONV - 1, 0), (0, 0)))
            conv = cb + sum((xp[:, k:k + L, :] * cw[:, k] for k in range(D_CONV)))
            xBC = jax.nn.silu(conv)
            xs, Bm, Cm = jnp.split(xBC, [D_INNER, D_INNER + D_STATE], axis=-1)
            xs = xs.reshape(B, L, NHEADS, HEADDIM)
            dt = jax.nn.softplus(dt + dtb)
            A = -jnp.exp(Alog)
            dA = jnp.exp(dt * A)
            dtx = dt[..., None] * xs

            def step(hs, inp):
                dA_t, dtx_t, B_t, C_t = inp
                hs = hs * dA_t[:, :, None, None] + dtx_t[..., None] * B_t[:, None, None, :]
                y = jnp.einsum('bhpn,bn->bhp', hs, C_t)
                return (hs, y)
            h0 = jnp.zeros((B, NHEADS, HEADDIM, D_STATE), h.dtype)
            _, ys = jax.lax.scan(step, h0, (dA.swapaxes(0, 1), dtx.swapaxes(0, 1), Bm.swapaxes(0, 1), Cm.swapaxes(0, 1)))
            y = ys.swapaxes(0, 1) + Dh[None, None, :, None] * xs
            y = y.reshape(B, L, D_INNER)
            y = _rmsnorm(y * jax.nn.silu(z), gw)
            return y @ Wo
        key = jax.random.key(seed)
        ks = jax.random.split(key, 8)
        x = jax.random.normal(ks[0], (BATCH, SEQLEN, D_MODEL), jnp.float32)
        s_in = 1.0 / np.sqrt(D_MODEL)
        s_out = 1.0 / np.sqrt(D_INNER)
        W_in = jax.random.normal(ks[1], (N_LAYER, D_MODEL, D_IN_PROJ), jnp.float32) * s_in
        conv_w = jax.random.normal(ks[2], (N_LAYER, CONV_DIM, D_CONV), jnp.float32) * 0.5
        conv_b = jnp.zeros((N_LAYER, CONV_DIM), jnp.float32)
        dt = jax.random.uniform(ks[3], (N_LAYER, NHEADS), jnp.float32, 0.001, 0.1)
        dt_bias = jnp.log(jnp.expm1(dt))
        A_log = jnp.log(jax.random.uniform(ks[4], (N_LAYER, NHEADS), jnp.float32, 1.0, 16.0))
        D = jnp.ones((N_LAYER, NHEADS), jnp.float32)
        gate_norm_w = jnp.ones((N_LAYER, D_INNER), jnp.float32)
        W_out = jax.random.normal(ks[5], (N_LAYER, D_INNER, D_MODEL), jnp.float32) * s_out
        block_norm_w = jnp.ones((N_LAYER, D_MODEL), jnp.float32)
        final_norm_w = jnp.ones((D_MODEL,), jnp.float32)
        return dict(x=x, W_in=W_in, conv_w=conv_w, conv_b=conv_b, dt_bias=dt_bias, A_log=A_log, D=D, gate_norm_w=gate_norm_w, W_out=W_out, block_norm_w=block_norm_w, final_norm_w=final_norm_w)
    _L0_attn_in = _L0_attn_setup()

    def _L0_ffn_setup():
        import jax, jax.numpy as jnp
        import numpy as np
        B, S, H = (2, 256, 128)
        E, K, F_EXP, F_SHARED = (16, 2, 64, 128)
        key = jax.random.key(seed)
        ks = jax.random.split(key, 9)
        sc = 1.0 / np.sqrt(H)
        scf = 1.0 / np.sqrt(F_EXP)
        scfs = 1.0 / np.sqrt(F_SHARED)
        return {'x': jax.random.normal(ks[0], (B, S, H), dtype=jnp.float32), 'router_w': jax.random.normal(ks[1], (H, E), dtype=jnp.float32) * sc, 'gate_w': jax.random.normal(ks[2], (E, H, F_EXP), dtype=jnp.float32) * sc, 'up_w': jax.random.normal(ks[3], (E, H, F_EXP), dtype=jnp.float32) * sc, 'down_w': jax.random.normal(ks[4], (E, F_EXP, H), dtype=jnp.float32) * scf, 'shared_gate_w': jax.random.normal(ks[5], (H, F_SHARED), dtype=jnp.float32) * sc, 'shared_up_w': jax.random.normal(ks[6], (H, F_SHARED), dtype=jnp.float32) * sc, 'shared_down_w': jax.random.normal(ks[7], (F_SHARED, H), dtype=jnp.float32) * scfs}
    _L0_ffn_in = _L0_ffn_setup()
    _L0_c = _w((lambda *s: np.random.randn(*s).astype(np.float32) * 0.05)(8, 128))
    _L0_wmod = _w((lambda *s: np.random.randn(*s).astype(np.float32) * 0.05)(128, 6 * 128) * 128 ** (-0.5))

    def _L1_attn_setup():
        import jax, jax.numpy as jnp
        import numpy as np
        DIM = 128
        NUM_HEADS = 16
        HEAD_DIM = DIM // NUM_HEADS
        SCALE = 1.0 / float(np.sqrt(HEAD_DIM))
        key = jax.random.key(seed)
        kx, kw1, kb1, kw2, kb2 = jax.random.split(key, 5)
        b, l = (2, 256)
        s = 1.0 / np.sqrt(DIM)
        return {'x': jax.random.normal(kx, (b, l, DIM), dtype=jnp.float32), 'w_qkv': jax.random.uniform(kw1, (DIM, 3 * DIM), jnp.float32, -s, s), 'b_qkv': jax.random.uniform(kb1, (3 * DIM,), jnp.float32, -s, s), 'w_proj': jax.random.uniform(kw2, (DIM, DIM), jnp.float32, -s, s), 'b_proj': jax.random.uniform(kb2, (DIM,), jnp.float32, -s, s)}
    _L1_attn_in = _L1_attn_setup()

    def _L1_ffn_setup():
        import jax, jax.numpy as jnp
        import numpy as np
        HIDDEN = 128
        N_ROUTED = 16
        N_SHARED = 2
        TOP_K = 2
        MID_R = HIDDEN // 4
        MID_S = HIDDEN // 2
        key = jax.random.key(seed)
        ks = jax.random.split(key, 8)
        s = 0.02
        return {'x': jax.random.normal(ks[0], (2, 128, HIDDEN), dtype=jnp.float32), 'router_w': jax.random.normal(ks[1], (HIDDEN, N_ROUTED), dtype=jnp.float32) * s, 'wg_r': jax.random.normal(ks[2], (N_ROUTED, HIDDEN, MID_R), dtype=jnp.float32) * s, 'wu_r': jax.random.normal(ks[3], (N_ROUTED, HIDDEN, MID_R), dtype=jnp.float32) * s, 'wd_r': jax.random.normal(ks[4], (N_ROUTED, MID_R, HIDDEN), dtype=jnp.float32) * s, 'wg_s': jax.random.normal(ks[5], (N_SHARED, HIDDEN, MID_S), dtype=jnp.float32) * s, 'wu_s': jax.random.normal(ks[6], (N_SHARED, HIDDEN, MID_S), dtype=jnp.float32) * s, 'wd_s': jax.random.normal(ks[7], (N_SHARED, MID_S, HIDDEN), dtype=jnp.float32) * s}
    _L1_ffn_in = _L1_ffn_setup()
    _L1_c = _w((lambda *s: np.random.randn(*s).astype(np.float32) * 0.05)(8, 128))
    _L1_wmod = _w((lambda *s: np.random.randn(*s).astype(np.float32) * 0.05)(128, 6 * 128) * 128 ** (-0.5))
    _d = {'L0_attn_x': _L0_attn_in['x'], 'L0_attn_W_in': _L0_attn_in['W_in'], 'L0_attn_conv_w': _L0_attn_in['conv_w'], 'L0_attn_conv_b': _L0_attn_in['conv_b'], 'L0_attn_dt_bias': _L0_attn_in['dt_bias'], 'L0_attn_A_log': _L0_attn_in['A_log'], 'L0_attn_D': _L0_attn_in['D'], 'L0_attn_gate_norm_w': _L0_attn_in['gate_norm_w'], 'L0_attn_W_out': _L0_attn_in['W_out'], 'L0_attn_block_norm_w': _L0_attn_in['block_norm_w'], 'L0_attn_final_norm_w': _L0_attn_in['final_norm_w'], 'L0_ffn_router_w': _L0_ffn_in['router_w'], 'L0_ffn_gate_w': _L0_ffn_in['gate_w'], 'L0_ffn_up_w': _L0_ffn_in['up_w'], 'L0_ffn_down_w': _L0_ffn_in['down_w'], 'L0_ffn_shared_gate_w': _L0_ffn_in['shared_gate_w'], 'L0_ffn_shared_up_w': _L0_ffn_in['shared_up_w'], 'L0_ffn_shared_down_w': _L0_ffn_in['shared_down_w'], 'L0_c': _L0_c, 'L0_wmod': _L0_wmod, 'L1_attn_w_qkv': _L1_attn_in['w_qkv'], 'L1_attn_b_qkv': _L1_attn_in['b_qkv'], 'L1_attn_w_proj': _L1_attn_in['w_proj'], 'L1_attn_b_proj': _L1_attn_in['b_proj'], 'L1_ffn_router_w': _L1_ffn_in['router_w'], 'L1_ffn_wg_r': _L1_ffn_in['wg_r'], 'L1_ffn_wu_r': _L1_ffn_in['wu_r'], 'L1_ffn_wd_r': _L1_ffn_in['wd_r'], 'L1_ffn_wg_s': _L1_ffn_in['wg_s'], 'L1_ffn_wu_s': _L1_ffn_in['wu_s'], 'L1_ffn_wd_s': _L1_ffn_in['wd_s'], 'L1_c': _L1_c, 'L1_wmod': _L1_wmod}
    _x0 = _d['L0_attn_x']
    _d['L0_attn_x'] = jax.random.normal(jax.random.fold_in(jax.random.key(seed), 1), (8, 256, 128), dtype=_x0.dtype)
    del _x0
    return _d

def reference(L0_attn_x, L0_attn_W_in, L0_attn_conv_w, L0_attn_conv_b, L0_attn_dt_bias, L0_attn_A_log, L0_attn_D, L0_attn_gate_norm_w, L0_attn_W_out, L0_attn_block_norm_w, L0_attn_final_norm_w, L0_ffn_router_w, L0_ffn_gate_w, L0_ffn_up_w, L0_ffn_down_w, L0_ffn_shared_gate_w, L0_ffn_shared_up_w, L0_ffn_shared_down_w, L0_c, L0_wmod, L1_attn_w_qkv, L1_attn_b_qkv, L1_attn_w_proj, L1_attn_b_proj, L1_ffn_router_w, L1_ffn_wg_r, L1_ffn_wu_r, L1_ffn_wd_r, L1_ffn_wg_s, L1_ffn_wu_s, L1_ffn_wd_s, L1_c, L1_wmod):

    def _L0_attn_ref(x, W_in, conv_w, conv_b, dt_bias, A_log, D, gate_norm_w, W_out, block_norm_w, final_norm_w):
        import jax, jax.numpy as jnp
        import numpy as np
        D_MODEL = 128
        N_LAYER = 4
        EXPAND = 2
        HEADDIM = 32
        D_STATE = 128
        D_CONV = 4
        NGROUPS = 1
        D_INNER = EXPAND * D_MODEL
        NHEADS = D_INNER // HEADDIM
        CONV_DIM = D_INNER + 2 * NGROUPS * D_STATE
        D_IN_PROJ = 2 * D_INNER + 2 * NGROUPS * D_STATE + NHEADS
        BATCH, SEQLEN = (4, 256)

        def _rmsnorm(x, w, eps=1e-05):
            return x * jax.lax.rsqrt(jnp.mean(x * x, axis=-1, keepdims=True) + eps) * w

        def _mamba2_layer(h, Wi, cw, cb, dtb, Alog, Dh, gw, Wo):
            B, L, _ = h.shape
            zxbcdt = h @ Wi
            z, xBC, dt = jnp.split(zxbcdt, [D_INNER, D_INNER + CONV_DIM], axis=-1)
            xp = jnp.pad(xBC, ((0, 0), (D_CONV - 1, 0), (0, 0)))
            conv = cb + sum((xp[:, k:k + L, :] * cw[:, k] for k in range(D_CONV)))
            xBC = jax.nn.silu(conv)
            xs, Bm, Cm = jnp.split(xBC, [D_INNER, D_INNER + D_STATE], axis=-1)
            xs = xs.reshape(B, L, NHEADS, HEADDIM)
            dt = jax.nn.softplus(dt + dtb)
            A = -jnp.exp(Alog)
            dA = jnp.exp(dt * A)
            dtx = dt[..., None] * xs

            def step(hs, inp):
                dA_t, dtx_t, B_t, C_t = inp
                hs = hs * dA_t[:, :, None, None] + dtx_t[..., None] * B_t[:, None, None, :]
                y = jnp.einsum('bhpn,bn->bhp', hs, C_t)
                return (hs, y)
            h0 = jnp.zeros((B, NHEADS, HEADDIM, D_STATE), h.dtype)
            _, ys = jax.lax.scan(step, h0, (dA.swapaxes(0, 1), dtx.swapaxes(0, 1), Bm.swapaxes(0, 1), Cm.swapaxes(0, 1)))
            y = ys.swapaxes(0, 1) + Dh[None, None, :, None] * xs
            y = y.reshape(B, L, D_INNER)
            y = _rmsnorm(y * jax.nn.silu(z), gw)
            return y @ Wo
        h = x
        for l in range(N_LAYER):
            h = h + _mamba2_layer(_rmsnorm(h, block_norm_w[l]), W_in[l], conv_w[l], conv_b[l], dt_bias[l], A_log[l], D[l], gate_norm_w[l], W_out[l])
        return _rmsnorm(h, final_norm_w)

    def _L0_ffn_ref(x, router_w, gate_w, up_w, down_w, shared_gate_w, shared_up_w, shared_down_w):
        import jax, jax.numpy as jnp
        import numpy as np
        B, S, H = (2, 256, 128)
        E, K, F_EXP, F_SHARED = (16, 2, 64, 128)
        b, s, h = x.shape
        T = b * s
        x_flat = x.reshape(T, h)
        shared_out = jax.nn.silu(x @ shared_gate_w) * (x @ shared_up_w) @ shared_down_w
        router_probs = jax.nn.softmax(x_flat @ router_w, axis=-1)
        topk_probs, topk_idx = jax.lax.top_k(router_probs, K)
        coeff = jnp.einsum('tk,tke->te', topk_probs, jax.nn.one_hot(topk_idx, E, dtype=x.dtype))

        def expert_step(acc, ws):
            g, u, d, c = ws
            inter = jax.nn.silu(x_flat @ g) * (x_flat @ u)
            return (acc + inter @ d * c[:, None], None)
        routed, _ = jax.lax.scan(expert_step, jnp.zeros((T, h), dtype=x.dtype), (gate_w, up_w, down_w, coeff.T))
        return routed.reshape(b, s, h) + shared_out

    def _L1_attn_ref(x, w_qkv, b_qkv, w_proj, b_proj):
        import jax, jax.numpy as jnp
        import numpy as np
        DIM = 128
        NUM_HEADS = 16
        HEAD_DIM = DIM // NUM_HEADS
        SCALE = 1.0 / float(np.sqrt(HEAD_DIM))
        b, l, c = x.shape
        n, d = (NUM_HEADS, HEAD_DIM)
        qkv = x @ w_qkv + b_qkv
        qkv = qkv.reshape(b, l, 3 * n, d)
        q, k, v = (qkv[:, :, :n], qkv[:, :, n:2 * n], qkv[:, :, 2 * n:])
        attn = SCALE * jnp.einsum('binc,bjnc->bnij', q, k)
        attn = jax.nn.softmax(attn.astype(jnp.float32), axis=-1).astype(q.dtype)
        out = jnp.einsum('bnij,bjnc->binc', attn, v)
        out = out.reshape(b, l, c)
        return out @ w_proj + b_proj

    def _L1_ffn_ref(x, router_w, wg_r, wu_r, wd_r, wg_s, wu_s, wd_s):
        import jax, jax.numpy as jnp
        import numpy as np
        HIDDEN = 128
        N_ROUTED = 16
        N_SHARED = 2
        TOP_K = 2
        MID_R = HIDDEN // 4
        MID_S = HIDDEN // 2
        orig_shape = x.shape
        flat = x.reshape(-1, orig_shape[-1])
        gs = jnp.einsum('td,ndm->tnm', flat, wg_s)
        us = jnp.einsum('td,ndm->tnm', flat, wu_s)
        out = jnp.einsum('tnm,nmd->td', jax.nn.silu(gs) * us, wd_s)
        logits = (flat @ router_w).astype(jnp.float32)
        probs = jax.nn.softmax(logits, axis=-1)
        weights, indices = jax.lax.top_k(probs, TOP_K)
        weights = weights / (weights.sum(axis=-1, keepdims=True) + 1e-09)
        weights = weights.astype(x.dtype)
        comb = jnp.sum(jax.nn.one_hot(indices, N_ROUTED, dtype=x.dtype) * weights[..., None], axis=1)
        g = jnp.einsum('td,edm->tem', flat, wg_r)
        u = jnp.einsum('td,edm->tem', flat, wu_r)
        h = jax.nn.silu(g) * u
        h = h * comb[:, :, None]
        out = out + jnp.einsum('tem,emd->td', h, wd_r)
        return out.reshape(orig_shape)
    x = L0_attn_x
    mod = (_silu(L0_c) @ L0_wmod).reshape(L0_c.shape[0], 6, 1, -1)
    sa, ca, ga, sb, cb, gb = (mod[:, 0], mod[:, 1], mod[:, 2], mod[:, 3], mod[:, 4], mod[:, 5])
    ga = (2 * (ga >= 0) - 1) * jnp.maximum(jnp.abs(ga), 0.25)
    gb = (2 * (gb >= 0) - 1) * jnp.maximum(jnp.abs(gb), 0.25)
    h = _layernorm(x, axis=-1) * (1 + ca) + sa
    x = x + ga * _L0_attn_ref(h, L0_attn_W_in, L0_attn_conv_w, L0_attn_conv_b, L0_attn_dt_bias, L0_attn_A_log, L0_attn_D, L0_attn_gate_norm_w, L0_attn_W_out, L0_attn_block_norm_w, L0_attn_final_norm_w)
    h = _layernorm(x, axis=-1) * (1 + cb) + sb
    x = x + gb * _L0_ffn_ref(h, L0_ffn_router_w, L0_ffn_gate_w, L0_ffn_up_w, L0_ffn_down_w, L0_ffn_shared_gate_w, L0_ffn_shared_up_w, L0_ffn_shared_down_w)
    mod = (_silu(L1_c) @ L1_wmod).reshape(L1_c.shape[0], 6, 1, -1)
    sa, ca, ga, sb, cb, gb = (mod[:, 0], mod[:, 1], mod[:, 2], mod[:, 3], mod[:, 4], mod[:, 5])
    ga = (2 * (ga >= 0) - 1) * jnp.maximum(jnp.abs(ga), 0.25)
    gb = (2 * (gb >= 0) - 1) * jnp.maximum(jnp.abs(gb), 0.25)
    h = _layernorm(x, axis=-1) * (1 + ca) + sa
    x = x + ga * _L1_attn_ref(h, L1_attn_w_qkv, L1_attn_b_qkv, L1_attn_w_proj, L1_attn_b_proj)
    h = _layernorm(x, axis=-1) * (1 + cb) + sb
    x = x + gb * _L1_ffn_ref(h, L1_ffn_router_w, L1_ffn_wg_r, L1_ffn_wu_r, L1_ffn_wd_r, L1_ffn_wg_s, L1_ffn_wu_s, L1_ffn_wd_s)
    return x

_drawn_inputs = setup_inputs


def setup_inputs(seed=0):
    import zlib

    import numpy as np

    out = dict(_drawn_inputs(seed))
    spreads = {'L0_attn_conv_b': (0.0, 0.1),
     'L0_attn_D': (1.0, 0.2),
     'L0_attn_gate_norm_w': (1.0, 0.2),
     'L0_attn_block_norm_w': (1.0, 0.2),
     'L0_attn_final_norm_w': (1.0, 0.2)}
    factors = {'L1_attn_w_qkv': 8.0,
     'L1_attn_b_qkv': 7.558,
     'L1_attn_w_proj': 5.844,
     'L1_attn_b_proj': 13.902,
     'L1_ffn_router_w': 8.0,
     'L1_ffn_wg_r': 8.0,
     'L1_ffn_wu_r': 8.0,
     'L1_ffn_wd_r': 8.0,
     'L1_ffn_wg_s': 8.0,
     'L1_ffn_wu_s': 8.0,
     'L1_ffn_wd_s': 8.0,
     'L1_c': 3.887,
     'L1_wmod': 3.667}
    for name, (base, spread) in spreads.items():
        noise = np.random.default_rng([zlib.crc32(name.encode()), seed]).standard_normal(out[name].shape)
        drawn = base * np.exp(spread * noise) if base else spread * noise
        out[name] = jnp.asarray(drawn.astype(out[name].dtype))
    for name, factor in factors.items():
        out[name] = (out[name] * factor).astype(out[name].dtype)
    return out
```

```python
from contextlib import ExitStack

import concourse.bass as bass
from concourse import mybir

P = 128
F32 = mybir.dt.float32
BF16 = mybir.dt.bfloat16
U32 = mybir.dt.uint32
ALU = mybir.AluOpType
ACT = mybir.ActivationFunctionType
AX = mybir.AxisListType

BATCH, SEQ, DM = 8, 256, 128
CHUNK = 128
CHUNKS = BATCH * SEQ // CHUNK
UNIT = 512
UC = UNIT // CHUNK
UNITS = BATCH * SEQ // UNIT
LAYERS = 4
DI, HEADS, HD, NS, TAPS = 256, 8, 32, 128, 4
ZOFF, XOFF, DTOFF, DPROJ = 0, 256, 768, 776
PARTS = 3
PH = PARTS * HEADS
EPS = 1e-5
FREE = 1
EXPERTS, AH, AD = 16, 16, 8
PCW, PCB, PGW, PBN, PD_, PDTB, PA_, PLEN = 0, 16, 20, 22, 23, 25, 33, 41


def program(nc, x, W_in, conv_w, conv_b, dt_bias, A_log, D, gate_norm_w, W_out, block_norm_w, final_norm_w,
            c0, wmod0, c1, wmod1, router0, gate0, up0, down0, sgate0, sup0, sdown0, w_qkv, b_qkv, w_proj, b_proj,
            router1, gate1, up1, down1, sgate1, sup1, sdown1, out):
    with ExitStack() as whole:
        sb, sem = allocators(nc, whole)
        bank = [whole.enter_context(nc.psum_tensor(f"bank{i}", [P, 512], F32)) for i in range(8)]
        shared = Shared(sb, sem)
        with ExitStack() as ctx:
            mamba(nc, ctx, bank, shared, x, W_in, conv_w, conv_b, dt_bias, A_log, D, gate_norm_w, W_out,
                  block_norm_w, final_norm_w, c0, wmod0, c1, wmod1,
                  (router0, gate0, up0, down0, sgate0, sup0, sdown0, w_qkv, b_qkv, w_proj, b_proj,
                   router1, gate1, up1, down1, sgate1, sup1, sdown1))
        with ExitStack() as ctx:
            mixture(nc, ctx, bank, shared, shared.moe0, "f0")
        with ExitStack() as ctx:
            attention(nc, ctx, bank, shared)
        with ExitStack() as ctx:
            mixture(nc, ctx, bank, shared, shared.moe1, "f1")
        with ExitStack() as ctx:
            store(nc, ctx, shared, out)


def allocators(nc, ctx):
    def sb(name, shape, dt=F32):
        return ctx.enter_context(nc.sbuf_tensor(name, shape, dt))

    def sem(name):
        return ctx.enter_context(nc.semaphore(name))

    return sb, sem


class Moe:

    def __init__(self, sb, name, f, norm, mod, gate_bc):
        self.f, self.norm, self.mod, self.gate_bc = f, norm, mod, gate_bc
        self.per = P // f
        self.routed = EXPERTS // self.per
        self.groups = self.routed + 1
        self.router = sb(f"{name}_router", [P, EXPERTS])
        self.gate = sb(f"{name}_gate", [P, self.groups, P])
        self.up = sb(f"{name}_up", [P, self.groups, P])
        self.down = sb(f"{name}_down", [P, self.groups, DM])
        self.sel = sb(f"{name}_sel", [PARTS * EXPERTS, self.routed, P], BF16)


class Shared:

    def __init__(self, sb, sem):
        self.ident = sb("ident", [P, P])
        self.identb = sb("identb", [P, P], BF16)
        self.mhalf = sb("mhalf", [P, CHUNKS])
        self.iota = sb("iota", [P, EXPERTS])
        self.x_tok = sb("x_tok", [P, CHUNKS, DM])
        self.mod = [sb(f"mod{i}", [P, 6, BATCH]) for i in range(2)]
        self.bc = [sb(f"bc{i}", [P, BATCH, DM]) for i in range(6)]
        self.moe0 = Moe(sb, "moe0", 64, False, self.mod[0], self.bc[3])
        self.moe1 = Moe(sb, "moe1", 32, True, self.mod[1], self.bc[5])
        self.wqkv = sb("wqkv", [P, 3 * DM])
        self.wproj = sb("wproj", [P, DM])
        self.bqk = sb("bqk", [P, 2])
        self.bv = sb("bv", [P, DM])
        self.bp = sb("bp", [P, DM])
        self.headsel = sb("headsel", [P, 4, 4])
        self.headmask = sb("headmask", [P, 4])
        self.selm = sb("selm", [PARTS * AH, AH, P], BF16)
        self.s_w2 = sem("s_w2")


def mamba(nc, ctx, bank, shared, x, W_in, conv_w, conv_b, dt_bias, A_log, D, gate_norm_w, W_out, block_norm_w,
          final_norm_w, c0, wmod0, c1, wmod1, later):
    if True:
        sb, sem = allocators(nc, ctx)
        PA, PDk, PG, PM, PY = bank[0:2], bank[2:4], bank[4], bank[5], bank[6:8]

        ident, identb, mhalf, x_tok, mod, bc = (shared.ident, shared.identb, shared.mhalf, shared.x_tok, shared.mod,
                                                shared.bc)
        ones = sb("ones", [P, P])
        triu = sb("triu", [P, P])
        maskneg = sb("maskneg", [P, 4, CHUNK], BF16)
        selh = sb("selh", [PH, HEADS, P], BF16)
        negsel = sb("negsel", [PH, HEADS, P], BF16)
        selq = sb("selq", [PH, 2, P], BF16)

        wi_all = sb("wi_all", [P, LAYERS, DPROJ])
        wo_all = sb("wo_all", [P, LAYERS, 2, DM])
        par = sb("par", [P, LAYERS, PLEN])
        fnw = sb("fnw", [P, 1])
        cT = [sb(f"cT{i}", [P, BATCH]) for i in range(2)]
        wmod = [sb(f"wmod{i}", [P, 6, P]) for i in range(2)]
        wi = sb("wi", [P, DPROJ])
        wo = sb("wo", [P, 2, DM])
        pla = sb("pla", [P, PLEN])
        plb = sb("plb", [P, PLEN])

        h_tok = sb("h_tok", [P, CHUNKS, DM])
        modt = sb("modt", [P, 2, BATCH])

        sq = sb("sq", [P, UC, DM])
        ss = sb("ss", [P, UC])
        ms = sb("ms", [P, UC])
        rs = sb("rs", [P, UC])
        hn = sb("hn", [P, UC, DM])
        hnT = sb("hnT", [P, UNIT])
        cv = [sb(f"cv{g}", [P, UNIT]) for g in range(4)]
        feat = [[sb(f"feat{p}_{g}", [P, UNIT]) for g in range(4)] for p in range(2)]
        sz = [sb(f"sz{p}", [P, 2, UNIT]) for p in range(2)]
        va = [sb(f"va{i}", [P, UC * HEADS]) for i in range(8)]
        dts = sb("dts", [P, UC, HEADS])
        av = sb("av", [P, UC * HEADS])
        ct = sb("ct", [P, 2, UC * HEADS])
        cp = sb("cp", [P, UC, PARTS, HEADS], BF16)
        edec = sb("edec", [P, UC, HEADS])
        cTs = [sb(f"cTs{p}", [PH, UNIT], BF16) for p in range(2)]
        dtx = [sb(f"dtx{p}", [P, UC, DI]) for p in range(2)]
        dtxd = [sb(f"dtxd{p}", [P, 2, DI]) for p in range(2)]
        Btok = [sb(f"Btok{p}", [P, 2, NS]) for p in range(2)]
        Gs = [sb(f"Gs{p}", [P, UC, CHUNK]) for p in range(2)]
        Ssb = sb("Ssb", [P, 2, DI])
        Ei = sb("Ei", [P, 2, 2, CHUNK])
        yi = sb("yi", [P, 2, 2, CHUNK])
        eb = [sb(f"eb{i}", [P, 4, CHUNK]) for i in range(2)]
        yt = sb("yt", [P, 2, UNIT])
        gsq = sb("gsq", [P, 2, UNIT])
        ms2 = sb("ms2", [P, UC])
        rs2 = sb("rs2", [P, UC])

        pa_w, pa_r = [sem("pa_w0"), sem("pa_w1")], [sem("pa_r0"), sem("pa_r1")]
        pd_w, pd_r = [sem("pd_w0"), sem("pd_w1")], [sem("pd_r0"), sem("pd_r1")]
        pg_w, pg_r = sem("pg_w"), sem("pg_r")
        pm_w, pm_r = sem("pm_w"), sem("pm_r")
        (s_ld, s_x, s_const, s_setup, s_par, s_mod, s_modps, s_h0, s_ms, s_rs, s_hn, s_acc, s_feat, s_v, s_e,
         s_a, s_cp, s_diff, s_edec, s_dtxd, s_y, s_M, s_g, s_gsq, s_ssq, s_ms2, s_rs2, s_wa, s_wb, s_hend, s_out) = (
            sem(n) for n in ("s_ld s_x s_const s_setup s_par s_mod s_modps s_h0 s_ms s_rs s_hn s_acc s_feat s_v "
                             "s_e s_a s_cp s_diff s_edec s_dtxd s_y s_M s_g s_gsq s_ssq s_ms2 s_rs2 s_wa s_wb s_hend "
                             "s_out").split())
        dchA, dchB, dchS = sem("dchA"), sem("dchB"), sem("dchS")
        BASE = 6

        def at(eng, s, per, n, m):
            eng.wait_ge(s, n * per + m)

        lnv = sb("lnv", [P, CHUNKS])
        bns = sb("bns", [P, CHUNKS, 6])
        bna = sb("bna", [P, CHUNKS, 2])
        lnt = sb("lnt", [P, CHUNKS, DM])
        gtmp = sb("gtmp", [P, 4, BATCH])

        def bcsrc(j):
            return (modt[:, 0, :], mod[0][:, 0, :], modt[:, 1, :], mod[0][:, 5, :], mod[1][:, 2, :], mod[1][:, 5, :])[j]

        NPAR = 5 * LAYERS + 2 + HEADS
        LOADS = 4 + 2 * LAYERS + NPAR

        ctx.enter_context(nc.allow_non_contiguous_dma(reason="a few small vectors, laid over partitions"))
        block = ctx.enter_context(nc.Block())

        @block.sync
        def _(sp):
            for free in (*pd_r, s_ms2, s_y):
                sp.sem_inc(free, FREE)
            sp.dma_start(cT[0][:], c0.rearrange("b k -> k b")).then_inc(s_ld, 16)
            sp.dma_start(wmod[0][:], wmod0.rearrange("k (j d) -> k j d", j=6)).then_inc(s_ld, 16)
            sp.dma_start(cT[1][:], c1.rearrange("b k -> k b")).then_inc(s_ld, 16)
            sp.dma_start(wmod[1][:], wmod1.rearrange("k (j d) -> k j d", j=6)).then_inc(s_ld, 16)
            sp.dma_start(x_tok[:], x.rearrange("b (i p) d -> p (b i) d", p=P)).then_inc(s_x, 16)
            for l in range(LAYERS):
                sp.dma_start(wi_all[:, l, :], W_in[l]).then_inc(s_ld, 16)
                sp.dma_start(wo_all[:, l, :, :], W_out[l].rearrange("(q p) d -> p q d", q=2)).then_inc(s_ld, 16)
            for l in range(LAYERS):
                sp.dma_start(par[:, l, PCW:PCW + 16].rearrange("p (g k) -> p g k", g=4),
                            conv_w[l].rearrange("(g p) k -> p g k", p=P)).then_inc(s_ld, 16)
                sp.dma_start(par[:, l, PCB:PCB + 4], conv_b[l].rearrange("(g p) -> p g", p=P),
                            ).then_inc(s_ld, 16)
                sp.dma_start(par[:, l, PGW:PGW + 2], gate_norm_w[l].rearrange("(g p) -> p g", p=P)).then_inc(s_ld, 16)
                sp.dma_start(par[:, l, PBN:PBN + 1], block_norm_w[l:l + 1, :].rearrange("o p -> p o")).then_inc(s_ld, 16)
                sp.dma_start(par[:, l, PDTB:PDTB + 8], dt_bias[l:l + 1, :].partition_broadcast(P)).then_inc(s_ld, 16)
            sp.dma_start(par[:, :, PA_:PA_ + 8], A_log.partition_broadcast(P)).then_inc(s_ld, 16)
            sp.dma_start(fnw[:], final_norm_w.rearrange("(p o) -> p o", o=1)).then_inc(s_ld, 16)
            for h in range(HEADS):
                sp.dma_start(par[32 * (h % 4):32 * (h % 4) + 32, :, PD_ + h // 4],
                            D[:, h].partition_broadcast(32)).then_inc(s_ld, 16)
            (router0, gate0, up0, down0, sgate0, sup0, sdown0, w_qkv, b_qkv, w_proj, b_proj,
             router1, gate1, up1, down1, sgate1, sup1, sdown1) = later
            m0, m1, r0, r1 = shared.moe0, shared.moe1, shared.moe0.routed, shared.moe1.routed
            late = [
                (m0.router[:], router0), (m1.router[:], router1),
                (m0.gate[:, 0:r0, :].rearrange("p g (e f) -> p (g e) f", f=m0.f), gate0.rearrange("e h f -> h e f")),
                (m0.up[:, 0:r0, :].rearrange("p g (e f) -> p (g e) f", f=m0.f), up0.rearrange("e h f -> h e f")),
                (m0.down[:, 0:r0, :], down0.rearrange("(g e) f d -> (e f) g d", g=r0)),
                (m0.gate[:, r0, :], sgate0), (m0.up[:, r0, :], sup0), (m0.down[:, r0, :], sdown0),
                (shared.wqkv[:], w_qkv), (shared.wproj[:], w_proj),
                (shared.bqk[:], b_qkv[0:2 * DM].rearrange("(k p) -> p k", k=2)),
                (shared.bv[:], b_qkv[2 * DM:3 * DM].partition_broadcast(P)),
                (shared.bp[:], b_proj.partition_broadcast(P)),
                (m1.gate[:, 0:r1, :].rearrange("p g (e f) -> p (g e) f", f=m1.f), gate1.rearrange("e h f -> h e f")),
                (m1.up[:, 0:r1, :].rearrange("p g (e f) -> p (g e) f", f=m1.f), up1.rearrange("e h f -> h e f")),
                (m1.down[:, 0:r1, :], down1.rearrange("(g e) f d -> (e f) g d", g=r1)),
                (m1.gate[:, r1, :].rearrange("p (n f) -> p n f", n=2), sgate1.rearrange("n h f -> h n f")),
                (m1.up[:, r1, :].rearrange("p (n f) -> p n f", n=2), sup1.rearrange("n h f -> h n f")),
                (m1.down[:, r1, :], sdown1.rearrange("n f d -> (n f) d")),
            ]
            for dst, src in late:
                sp.dma_start(dst, src).then_inc(shared.s_w2, 16)
            sp.wait_ge(shared.s_w2, 16 * len(late))

        @block.gpsimd
        def _(g):
            for t, v in ((ident, 0.0), (identb, 0.0), (ones, 1.0), (triu, 1.0), (maskneg, 0.0), (selh, 0.0),
                         (selq, 0.0), (mhalf, -0.5), (shared.moe0.sel, 0.0), (shared.moe1.sel, 0.0),
                         (shared.selm, 0.0), (shared.headsel, 1.0)):
                last = nc.gpsimd.memset(t[:], v)
            last.then_inc(s_setup, 1)
            g.wait_ge(s_setup, 1)
            nc.gpsimd.affine_select(out=ident[:], in_=ident[:], compare_op=ALU.not_equal, fill=1.0, base=0,
                                    pattern=[[-1, P]], channel_multiplier=1)
            nc.gpsimd.affine_select(out=identb[:], in_=identb[:], compare_op=ALU.not_equal, fill=1.0, base=0,
                                    pattern=[[-1, P]], channel_multiplier=1)
            nc.gpsimd.affine_select(out=triu[:], in_=triu[:], compare_op=ALU.is_ge, fill=0.0, base=0,
                                    pattern=[[1, P]], channel_multiplier=-1)
            nc.gpsimd.affine_select(out=maskneg[:], in_=maskneg[:], compare_op=ALU.is_ge, fill=-1e30, base=0,
                                    pattern=[[0, 4], [1, CHUNK]], channel_multiplier=-1)
            for k in range(PARTS):
                nc.gpsimd.affine_select(out=selh[:], in_=selh[:], compare_op=ALU.not_equal, fill=1.0, base=-HEADS * k,
                                        pattern=[[-1, HEADS], [0, P]], channel_multiplier=1)
                last = nc.gpsimd.affine_select(out=selq[:], in_=selq[:], compare_op=ALU.not_equal, fill=1.0,
                                               base=-HEADS * k, pattern=[[-4, 2], [-1, 4], [0, HD]],
                                               channel_multiplier=1)
                for mo in (shared.moe0, shared.moe1):
                    nc.gpsimd.affine_select(out=mo.sel[:], in_=mo.sel[:], compare_op=ALU.not_equal, fill=1.0,
                                            base=-EXPERTS * k, pattern=[[-mo.per, mo.routed], [-1, mo.per], [0, mo.f]],
                                            channel_multiplier=1)
                last = nc.gpsimd.affine_select(out=shared.selm[:], in_=shared.selm[:], compare_op=ALU.not_equal,
                                               fill=1.0, base=-AH * k, pattern=[[-1, AH], [0, P]],
                                               channel_multiplier=1)
                last.then_inc(s_setup, 1)
                g.wait_ge(s_setup, 2 + k)
            nc.gpsimd.affine_select(out=shared.headsel[:], in_=shared.headsel[:], compare_op=ALU.is_ge, fill=0.0,
                                    base=0, pattern=[[-AD, 4], [-32, 4]], channel_multiplier=1).then_inc(s_setup, 1)
            g.wait_ge(s_setup, 5)
            nc.gpsimd.affine_select(out=shared.headsel[:], in_=shared.headsel[:], compare_op=ALU.is_ge, fill=0.0,
                                    base=AD - 1, pattern=[[AD, 4], [32, 4]], channel_multiplier=-1)
            nc.gpsimd.iota(shared.iota[:], pattern=[[1, EXPERTS]], base=0, channel_multiplier=0,
                           allow_small_or_imprecise_dtypes=True)
            nc.gpsimd.tensor_scalar(negsel[:], selh[:], -1.0, 0.0, ALU.mult, ALU.add).then_inc(s_const, 1)

            g.wait_ge(s_h0, 1)
            nc.gpsimd.tensor_tensor(lnv[:], lnv[:], mhalf[:], ALU.pow).then_inc(s_h0, 1)

            def A(m):
                at(g, s_ms, 1, m, 1)
                nc.gpsimd.tensor_tensor(rs[:], ms[:], mhalf[:, 0:UC], ALU.pow).then_inc(s_rs, 1)

            def A2(m, p):
                g.wait_ge(pa_r[0], m * 5 + BASE + 5)
                at(g, s_edec, 1, m, 1)
                src = dtx[p][:].rearrange("p (b i) (h d) -> p b i h d", i=2, h=HEADS)[:, :, 0]
                dst = dtxd[p][:].rearrange("p b (h d) -> p b h d", h=HEADS)
                e = edec[:].rearrange("p (b i) h -> p b i h", i=2)[:, :, 0]
                for b in range(2):
                    ins = nc.gpsimd.tensor_tensor(dst[:, b], src[:, b], e[:, b, :, None].to_broadcast([P, HEADS, HD]),
                                                  ALU.mult)
                ins.then_inc(s_dtxd, 1)

            def B(n):
                at(g, s_ms2, 1, n, 1 + FREE)
                nc.gpsimd.tensor_tensor(rs2[:], ms2[:], mhalf[:, 0:UC], ALU.pow).then_inc(s_rs2, 1)

            A(0)
            A2(0, 0)

            def layer(l, last):
                for u in range(UNITS):
                    n = l * UNITS + u
                    more = not (last and u == UNITS - 1)
                    if more:
                        A(n + 1)
                    B(n)
                    if more:
                        A2(n + 1, (u + 1) % 2)

            with g.Fori(0, LAYERS - 1) as l:
                layer(l, False)
            layer(LAYERS - 1, True)
            g.wait_ge(s_h0, 5)
            nc.gpsimd.tensor_tensor(lnv[:], lnv[:], mhalf[:], ALU.pow).then_inc(s_h0, 1)

        @block.tensor
        def _(pe):
            pe.wait_ge(s_mod, 1)
            for i in range(2):
                for j in range(6):
                    ins = pe.matmul(PY[i][:, j * BATCH:(j + 1) * BATCH], wmod[i][:, j, :], cT[i][:],
                                    start=True, stop=True)
                ins.then_inc(s_modps, 1)
            pe.wait_ge(s_const, 1)
            pe.wait_ge(s_mod, 2)
            for j in range(6):
                for half in range(2):
                    k = 2 * j + half
                    if k >= 2:
                        pe.wait_ge(pa_r[half], j)
                    for b in range(4):
                        src = bcsrc(j)[:, 4 * half + b:4 * half + b + 1]
                        ins = pe.matmul(PA[half][:, b * DM:(b + 1) * DM], src.to_broadcast([P, P]), ident[:],
                                        start=True, stop=True)
                    ins.then_inc(pa_w[half], 1)

            def pa_turn(m, k):
                b = k % 2
                pe.wait_ge(pa_r[b], m * 5 + k // 2 + BASE)
                return PA[b], pa_w[b]

            def A1(m):
                bk, w = pa_turn(m, 0)
                at(pe, s_hn, 1, m, 1)
                for c in range(UC):
                    ins = pe.transpose(bk[:, c * P:(c + 1) * P], hn[:, c, :], ident[:])
                ins.then_inc(w, 1)

            def dt(m):
                pe.wait_ge(pa_r[0], m * 5 + BASE + 1)
                at(pe, pm_r, 3, m, 0)
                for c in range(UC):
                    ins = pe.matmul(PM[:, c * HEADS:(c + 1) * HEADS], hnT[:, c * P:(c + 1) * P],
                                    wi[:, DTOFF:DPROJ], start=True, stop=True)
                ins.then_inc(pm_w, 1)

            def proj(m, k, off):
                bk, w = pa_turn(m, k)
                pe.matmul(bk[:], wi[:, off:off + P], hnT[:], start=True, stop=True).then_inc(w, 1)

            def xproj(m, g):
                proj(m, 1 + g, XOFF + g * P)

            def zproj(m, q):
                proj(m, 5 + q, ZOFF + q * P)

            def cum(m):
                at(pe, s_a, 1, m, 1)
                at(pe, pm_r, 3, m, 1)
                pe.matmul(PM[:, 0:UC * HEADS], triu[:], av[:], start=True, stop=True)
                pe.matmul(PM[:, UC * HEADS:2 * UC * HEADS], ones[:], av[:], start=True, stop=True).then_inc(pm_w, 1)

            def cTr(m):
                at(pe, s_cp, 1, m, 1)
                at(pe, pm_r, 3, m, 2)
                dst = PM[0:PH, 0:UNIT // 2].bitcast(BF16)
                for c in range(UC):
                    ins = pe.transpose(dst[:, c * P:(c + 1) * P], cp[:, c, :, :].rearrange("p k h -> p (k h)"),
                                       identb[:])
                ins.then_inc(pm_w, 1)

            def A3(m, p):
                f = feat[p]
                at(pe, s_feat, 4, m, 4)
                for j in range(2):
                    bk, w = pa_turn(m, 7 + j)
                    for i in range(2):
                        for q in range(2):
                            c = 2 * j + i
                            ins = pe.transpose(bk[:, i * DI + q * P:i * DI + (q + 1) * P],
                                               f[q][:, c * P:(c + 1) * P], ident[:])
                    ins.then_inc(w, 1)
                bk, w = pa_turn(m, 9)
                for b in range(2):
                    ins = pe.transpose(bk[:, b * P:(b + 1) * P], f[2][:, 2 * b * P:(2 * b + 1) * P], ident[:])
                ins.then_inc(w, 1)
                at(pe, pg_r, 4, m, 0)
                for c in range(UC):
                    cs = slice(c * P, (c + 1) * P)
                    ins = pe.matmul(PG[:, cs], f[2][:, cs], f[3][:, cs], start=True, stop=True)
                ins.then_inc(pg_w, 1)

            def S(n, p):
                pe.wait_ge(pa_r[1], n * 5 + BASE + 5)
                at(pe, s_dtxd, 1, n, 1)
                at(pe, pg_r, 4, n, 1)
                for b in range(2):
                    ins = pe.matmul(PG[:, b * DI:(b + 1) * DI], Btok[p][:, b, :], dtxd[p][:, b, :],
                                    start=True, stop=True)
                ins.then_inc(pg_w, 1)

            def inter(n, p):
                at(pe, pg_r, 4, n, 2)
                for b in range(2):
                    cs = slice((2 * b + 1) * P, (2 * b + 2) * P)
                    for q in range(2):
                        k = 2 * b + q
                        ins = pe.matmul(PG[:, k * P:(k + 1) * P], Ssb[:, b, q * P:(q + 1) * P], feat[p][3][:, cs],
                                        start=True, stop=True)
                ins.then_inc(pg_w, 1)

            def Einter(n, p):
                at(pe, pm_r, 3, n, 3)
                at(pe, pd_r[0], 5, n, 0 + FREE)
                for b in range(2):
                    cs = slice((2 * b + 1) * P, (2 * b + 2) * P)
                    for q in range(2):
                        k = 2 * b + q
                        ins = pe.matmul(PDk[0][:, k * P:(k + 1) * P], selq[:, q, :], cTs[p][:, cs],
                                        start=True, stop=True)
                ins.then_inc(pd_w[0], 1)

            def decay(n, p, i):
                c, q = i // 2, i % 2
                cs = slice(c * P, (c + 1) * P)
                if q == 0:
                    at(pe, pd_r[0], 5, n, 1 + c + FREE)
                else:
                    at(pe, pd_r[1], 4, n, c + FREE)
                bk = PDk[q]
                pe.matmul(bk[:], identb[:], maskneg[:].rearrange("p h t -> p (h t)"), start=True, stop=False)
                for r in range(4):
                    pe.matmul(bk[:, r * P:(r + 1) * P], selh[:, 4 * q + r, :], cTs[p][:, cs],
                              start=False, stop=False, skip_group_check=True)
                ins = pe.matmul(bk[:], cTs[p][:, cs], negsel[:, 4 * q:4 * q + 4, :].rearrange("k h t -> k (h t)"),
                                start=False, stop=True)
                ins.then_inc(pd_w[q], 1)

            def y(n, p, i):
                c, q = i // 2, i % 2
                at(pe, s_M, 8, n, i + 1)
                if c == 0:
                    at(pe, s_ms2, 1, n, 0 + FREE)
                for r in range(4):
                    h = 4 * q + r
                    ins = pe.matmul(PY[q][32 * r:32 * r + 32, c * P:(c + 1) * P],
                                    dtx[p][:, c, h * HD:(h + 1) * HD], eb[q][:, r, :], start=True, stop=True)
                ins.then_inc(s_y, 1)

            def outp(n):
                at(pe, s_g, 1, n, 1)
                at(pe, pg_r, 4, n, 3)
                at(pe, s_wb, 1, l_of[0], 1)
                for c in range(UC):
                    cs = slice(c * P, (c + 1) * P)
                    for q in range(2):
                        ins = pe.matmul(PG[:, cs], yt[:, q, cs], wo[:, q, :], start=(q == 0), stop=(q == 1))
                ins.then_inc(pg_w, 1)

            def sumsq(n):
                at(pe, s_gsq, 1, n, 1)
                for c in range(UC):
                    cs = slice(c * P, (c + 1) * P)
                    for q in range(2):
                        ins = pe.matmul(PY[0][:, c:c + 1], gsq[:, q, cs], ones[:, 0:1],
                                        start=(q == 0), stop=(q == 1))
                ins.then_inc(s_ssq, 1)

            l_of = [0]
            pe.wait_ge(s_wa, 1)
            A1(0)
            dt(0)
            for g in range(4):
                xproj(0, g)
            cum(0)
            cTr(0)
            zproj(0, 0)
            zproj(0, 1)
            A3(0, 0)

            def layer(l, last):
                l_of[0] = l
                for u in range(UNITS):
                    n, p = l * UNITS + u, u % 2
                    more = not (last and u == UNITS - 1)
                    if more:
                        A1(n + 1)
                    Einter(n, p)
                    S(n, p)
                    if more:
                        if u == UNITS - 1:
                            pe.wait_ge(s_wa, l + 2)
                        dt(n + 1)
                    for i in range(8):
                        decay(n, p, i)
                        if i == 0:
                            inter(n, p)
                        if more and i in (0, 2, 4, 6):
                            xproj(n + 1, i // 2)
                        if i >= 1:
                            y(n, p, i - 1)
                        if more and i == 5:
                            cum(n + 1)
                        if more and i == 7:
                            cTr(n + 1)
                    y(n, p, 7)
                    if more:
                        zproj(n + 1, 0)
                        zproj(n + 1, 1)
                    outp(n)
                    sumsq(n)
                    if more:
                        A3(n + 1, 1 - p)

            with pe.Fori(0, LAYERS - 1) as l:
                layer(l, False)
            layer(LAYERS - 1, True)

        @block.scalar
        def _(act):
            act.wait_ge(s_ld, 16 * LOADS)
            for i in range(2):
                ins = nc.scalar.activation(cT[i][:], cT[i][:], ACT.Silu)
            ins.then_inc(s_mod, 1)
            nc.scalar.activation(par[:, :, PA_:PA_ + 8], par[:, :, PA_:PA_ + 8], ACT.Exp).then_inc(s_par, 1)
            for k in range(12):
                half = k % 2
                act.wait_ge(pa_w[half], k // 2 + 1)
                nc.scalar.activation(bc[k // 2][:, 4 * half:4 * half + 4, :].rearrange("p b d -> p (b d)"),
                                     PA[half][:], ACT.Identity).then_inc(pa_r[half], 1)

            def hnT_copy(m):
                act.wait_ge(pa_w[0], m * 5 + BASE + 1)
                nc.scalar.activation(hnT[:], PA[0][:], ACT.Identity).then_inc(pa_r[0], 1)

            def tap(m, g):
                b, k = (1 + g) % 2, (1 + g) // 2
                if not first(m):
                    at(act, s_feat, 4, m - 1, g + 1)
                if g == 0:
                    act.wait_ge(s_wa, layer_of[0] + 1)
                act.wait_ge(pa_w[b], m * 5 + k + BASE + 1)
                nc.scalar.activation(cv[g][:], PA[b][:], ACT.Identity, bias=pla[:, PCB + g:PCB + g + 1],
                                     scale=pla[:, PCW + 4 * g + 3:PCW + 4 * g + 4]).then_inc(s_acc, 1)

            def silus(m, p):
                for g in range(4):
                    b, k = (1 + g) % 2, (1 + g) // 2
                    act.wait_ge(pa_r[b], m * 5 + k + BASE + 1)
                    nc.scalar.activation(feat[p][g][:], cv[g][:], ACT.Silu).then_inc(s_feat, 1)
                for q in range(2):
                    b, k = (5 + q) % 2, (5 + q) // 2
                    act.wait_ge(pa_w[b], m * 5 + k + BASE + 1)
                    nc.scalar.activation(sz[p][:, q, :], PA[b][:], ACT.Silu).then_inc(pa_r[b], 1)

            def tail(m, p):
                act.wait_ge(pa_w[1], m * 5 + 5 + BASE)
                nc.scalar.activation(Btok[p][:].rearrange("p b n -> p (b n)"), PA[1][:, 0:2 * NS],
                                     ACT.Identity).then_inc(pa_r[1], 1)
                at(act, pg_w, 4, m, 1)
                nc.scalar.activation(Gs[p][:].rearrange("p c t -> p (c t)"), PG[:], ACT.Identity).then_inc(pg_r, 1)

            def expv(m):
                at(act, s_v, 1, m, 1)
                nc.scalar.activation(va[2][:], va[1][:], ACT.Exp, scale=-1.0).then_inc(s_e, 1)

            def expd(m):
                at(act, s_dtxd, 1, m, 0)
                at(act, s_diff, 1, m, 1)
                nc.scalar.activation(edec[:].rearrange("p c h -> p (c h)"), va[7][:], ACT.Exp).then_inc(s_edec, 1)

            def Eint(n):
                at(act, pd_w[0], 5, n, 1)
                nc.scalar.activation(Ei[:].rearrange("p b q t -> p (b q t)"), PDk[0][:], ACT.Exp).then_inc(pd_r[0], 1)

            def Scopy(n):
                at(act, pg_w, 4, n, 2)
                nc.scalar.activation(Ssb[:].rearrange("p b d -> p (b d)"), PG[:], ACT.Identity).then_inc(pg_r, 1)

            def E(n, i):
                c, q = i // 2, i % 2
                if q == 0:
                    at(act, pd_w[0], 5, n, 2 + c)
                else:
                    at(act, pd_w[1], 4, n, 1 + c)
                at(act, s_y, 8, n, max(i - 1, 0) + FREE)
                nc.scalar.activation(eb[q][:].rearrange("p h t -> p (h t)"), PDk[q][:], ACT.Exp).then_inc(pd_r[q], 1)

            def square(n):
                at(act, s_g, 1, n, 1)
                nc.scalar.activation(gsq[:], yt[:], ACT.Square).then_inc(s_gsq, 1)

            layer_of = [0]
            hnT_copy(0)
            expv(0)
            for g in range(4):
                tap(0, g)
            expd(0)
            silus(0, 0)
            tail(0, 0)

            def layer(l, last):
                for u in range(UNITS):
                    n, p = l * UNITS + u, u % 2
                    layer_of[0] = l + 1 if u == UNITS - 1 else l
                    more = not (last and u == UNITS - 1)
                    if more:
                        hnT_copy(n + 1)
                    Eint(n)
                    Scopy(n)
                    for i in range(8):
                        E(n, i)
                        if more and i % 2 == 1:
                            tap(n + 1, i // 2)
                        if more and i == 2:
                            expv(n + 1)
                    if more:
                        expd(n + 1)
                        silus(n + 1, 1 - p)
                    square(n)
                    if more:
                        tail(n + 1, 1 - p)

            with act.Fori(0, LAYERS - 1) as l:
                layer(l, False)
            layer(LAYERS - 1, True)

        @block.vector
        def _(v):
            V = nc.vector
            cA, cB, cS = Chain(v, dchA, KA), Chain(v, dchB, KB), Chain(v, dchS, 0)
            cS.start(0)
            for i in range(2):
                v.wait_ge(s_modps, i + 1)
                cS.link(V.tensor_copy(mod[i][:].rearrange("p j b -> p (j b)"), PY[i][:, 0:6 * BATCH]))
            for i in range(2):
                for j in (2, 5):
                    cS.link(V.tensor_scalar(gtmp[:, 0, :], mod[i][:, j, :], 0.0, 2.0, ALU.is_ge, ALU.mult))
                    cS.link(V.scalar_tensor_tensor(gtmp[:, 1, :], mod[i][:, j, :], -1.0, mod[i][:, j, :],
                                                   ALU.mult, ALU.max))
                    cS.link(V.tensor_scalar(gtmp[:, 1, :], gtmp[:, 1, :], 0.25, None, ALU.max))
                    cS.link(V.scalar_tensor_tensor(mod[i][:, j, :], gtmp[:, 0, :], -1.0, gtmp[:, 1, :],
                                                   ALU.add, ALU.mult))
            cS.link(V.tensor_scalar(modt[:, 0, :], mod[0][:, 1, :], 1.0, None, ALU.add))
            v.wait_ge(s_ld, 16 * LOADS)
            V.tensor_scalar(modt[:, 1, :], mod[0][:, 2, :], fnw[:, 0:1], None, ALU.mult).then_inc(s_mod, 1)

            v.wait_ge(s_const, 1)
            cS.link(V.tensor_reduce(shared.headmask[:], shared.headsel[:], AX.X, ALU.add))

            def layer_norm(k):
                for c in range(CHUNKS):
                    ins = V.bn_stats(bns[:, c, :], x_tok[:, c, :])
                cS.link(ins)
                for c in range(CHUNKS):
                    ins = V.bn_aggr(bna[:, c, :], bns[:, c, :])
                cS.link(ins)
                V.tensor_scalar(lnv[:], bna[:, :, 1], EPS, None, ALU.add).then_inc(s_h0, 1)
                v.wait_ge(s_h0, k + 2)
                for c in range(CHUNKS):
                    ins = V.tensor_scalar(lnt[:, c, :], x_tok[:, c, :], bna[:, c, 0:1], lnv[:, c:c + 1],
                                          ALU.subtract, ALU.mult)
                cS.link(ins)

            v.wait_ge(s_x, 16)
            layer_norm(0)
            v.wait_ge(pa_r[1], 2)
            v4 = lambda t: t[:].rearrange("p (b i) d -> p b i d", i=2)
            def brow(t, n=2):
                return t[:, :, None, :].to_broadcast([P, BATCH, n, DM])
            cS.link(V.tensor_tensor(v4(h_tok), v4(lnt), brow(bc[0]), ALU.mult))
            cS.link(V.tensor_tensor(v4(h_tok), v4(h_tok), brow(bc[1]), ALU.add))

            def fold_a(l):
                if not first(l):
                    v.wait_ge(pa_w[0], l * UNITS * 5 - 1 + BASE)
                    at(v, s_acc, 16, l, 0)
                V.tensor_copy(pla[:], par[:, l, :]).then_inc(s_par, 1)
                v.wait_ge(s_par, 2 * l + 2)
                V.tensor_scalar(wi[:], wi_all[:, l, :], pla[:, PBN:PBN + 1], None, ALU.mult).then_inc(s_wa, 1)

            def fold_b(l):
                V.tensor_copy(plb[:], par[:, l, :]).then_inc(s_par, 1)
                v.wait_ge(s_par, 2 * l + 3)
                for q in range(2):
                    ins = V.tensor_scalar(wo[:, q, :], wo_all[:, l, q, :], plb[:, PGW + q:PGW + q + 1], None, ALU.mult)
                ins.then_inc(s_wb, 1)
                v.wait_ge(s_wb, l + 1)

            def A1(m, hs):
                cA.start(m)
                for c in range(UC):
                    ins = V.tensor_tensor_reduce(out=sq[:, c, :], in0=h_tok[:, hs + c, :], in1=h_tok[:, hs + c, :],
                                                 scale=1.0, scalar=0.0, op0=ALU.mult, op1=ALU.add,
                                                 accum_out=ss[:, c:c + 1])
                cA.link(ins)
                V.tensor_scalar(ms[:], ss[:], 1.0 / DM, EPS, ALU.mult, ALU.add).then_inc(s_ms, 1)
                if not first(m):
                    v.wait_ge(pa_w[0], m * 5 - 4 + BASE)
                at(v, s_rs, 1, m, 1)
                for c in range(UC):
                    ins = V.tensor_scalar(hn[:, c, :], h_tok[:, hs + c, :], rs[:, c:c + 1], None, ALU.mult)
                ins.then_inc(s_hn, 1)

            ch = lambda t: t.rearrange("p (c h) -> p c h", h=HEADS)

            def dt_bias_add(m):
                at(v, pm_w, 3, m, 1)
                V.tensor_tensor(ch(va[0][:]), ch(PM[:, 0:UC * HEADS]),
                                pla[:, None, PDTB:PDTB + 8].to_broadcast([P, UC, HEADS]), ALU.add).then_inc(pm_r, 1)
                at(v, pm_r, 3, m, 1)
                V.scalar_tensor_tensor(va[1][:], va[0][:], -1.0, va[0][:], ALU.mult, ALU.max).then_inc(s_v, 1)

            def softplus(m):
                e, s, s2, p = va[2][:], va[4][:], va[5][:], va[6][:]
                at(v, s_e, 1, m, 1)
                cA.link(V.tensor_scalar(va[3][:], e, 2.0, None, ALU.add))
                cA.link(V.reciprocal(va[3][:], va[3][:]))
                cA.link(V.tensor_tensor(s, e, va[3][:], ALU.mult))
                cA.link(V.tensor_tensor(s2, s, s, ALU.mult))
                cA.link(V.tensor_scalar(p, s2, 1.0 / 15, None, ALU.mult))
                for k in (13, 11, 9, 7, 5, 3):
                    cA.link(V.scalar_tensor_tensor(p, p, 1.0 / k, s2, ALU.add, ALU.mult))
                cA.link(V.scalar_tensor_tensor(p, p, 1.0, s, ALU.add, ALU.mult))
                cA.link(V.tensor_scalar(va[0][:], va[0][:], 0.0, None, ALU.max))
                cA.link(V.scalar_tensor_tensor(dts[:].rearrange("p c h -> p (c h)"), p, 2.0, va[0][:],
                                               ALU.mult, ALU.add))
                V.scalar_tensor_tensor(ch(av[:]), dts[:], -1.0,
                                       pla[:, None, PA_:PA_ + 8].to_broadcast([P, UC, HEADS]),
                                       ALU.mult, ALU.mult).then_inc(s_a, 1)

            def split(m):
                at(v, pm_w, 3, m, 2)
                cA.link(V.tensor_copy(ct[:].rearrange("p k c -> p (k c)"), PM[:, 0:2 * UC * HEADS]))
                v.sem_inc(pm_r, 1)
                r = va[3][:]
                cA.link(V.tensor_copy(cp[:, :, 0, :], ch(ct[:, 0, :])))
                cA.link(V.tensor_tensor(ch(r), ch(ct[:, 0, :]), cp[:, :, 0, :], ALU.subtract))
                cA.link(V.tensor_copy(cp[:, :, 1, :], ch(r)))
                cA.link(V.tensor_tensor(ch(r), ch(r), cp[:, :, 1, :], ALU.subtract))
                V.tensor_copy(cp[:, :, 2, :], ch(r)).then_inc(s_cp, 1)
                V.tensor_tensor(va[7][:], ct[:, 1, :], ct[:, 0, :], ALU.subtract).then_inc(s_diff, 1)

            def cT_copy(m, p):
                at(v, pm_w, 3, m, 3)
                V.tensor_copy(cTs[p][:], PM[0:PH, 0:UNIT // 2].bitcast(BF16)).then_inc(pm_r, 1)

            def taps(m, g):
                b, k = (1 + g) % 2, (1 + g) // 2
                at(v, s_acc, 4, m, g + 1)
                src = PA[b][:].rearrange("p (b t) -> p b t", b=2)
                acc = cv[g][:].rearrange("p (b t) -> p b t", b=2)
                for s in (1, 2, 3):
                    j = PCW + 4 * g + 3 - s
                    ins = V.scalar_tensor_tensor(acc[:, :, s:], src[:, :, :SEQ - s], pla[:, j:j + 1], acc[:, :, s:],
                                                 ALU.mult, ALU.add)
                    if s < 3:
                        cA.link(ins)
                    else:
                        ins.then_inc(pa_r[b], 1)

            def dtx_(m, p):
                for j in range(2):
                    b, k = (7 + j) % 2, (7 + j) // 2
                    v.wait_ge(pa_w[b], m * 5 + k + BASE + 1)
                    V.tensor_tensor(dtx[p][:, 2 * j:2 * j + 2, :].rearrange("p c (h d) -> p (c h) d", h=HEADS),
                                    PA[b][:].rearrange("p (c d) -> p c d", d=HD),
                                    dts[:, 2 * j:2 * j + 2, :].rearrange("p c h -> p (c h)")[:, :, None]
                                    .to_broadcast([P, 2 * HEADS, HD]), ALU.mult).then_inc(pa_r[b], 1)
                cA.end()

            def M(n, p, i):
                c, q = i // 2, i % 2
                if i == 0:
                    at(v, pg_r, 4, n, 1)
                if q == 0:
                    at(v, pd_r[0], 5, n, 2 + c + FREE)
                else:
                    at(v, pd_r[1], 4, n, 1 + c + FREE)
                V.tensor_tensor(eb[q][:], eb[q][:], Gs[p][:, c, None, :].to_broadcast([P, 4, CHUNK]),
                                ALU.mult).then_inc(s_M, 1)

            def yinter(n):
                cB.start(n)
                at(v, pg_w, 4, n, 3)
                at(v, pd_r[0], 5, n, 1 + FREE)
                V.tensor_tensor(yi[:].rearrange("p b q t -> p (b q t)"), PG[:], Ei[:].rearrange("p b q t -> p (b q t)"),
                                ALU.mult).then_inc(pg_r, 1)

            def gate(n, p):
                for q in range(2):
                    at(v, s_y, 8, n, 7 + q + FREE)
                    cB.link(V.scalar_tensor_tensor(yt[:, q, :], feat[p][q][:], plb[:, PD_ + q:PD_ + q + 1], PY[q][:],
                                                   ALU.mult, ALU.add))
                at(v, pg_r, 4, n, 3)
                odd = yt[:].rearrange("p q (b i t) -> p q b i t", b=2, i=2)[:, :, :, 1, :]
                cB.link(V.tensor_tensor(odd, odd, yi[:].rearrange("p b q t -> p q b t"), ALU.add))
                v.wait_ge(pa_r[0], n * 5 + 4 + BASE)
                V.tensor_tensor(yt[:], yt[:], sz[p][:], ALU.mult).then_inc(s_g, 1)

            def meansq(n):
                at(v, s_ssq, 1, n, 1)
                V.tensor_scalar(ms2[:], PY[0][:, 0:UC], 1.0 / DI, EPS, ALU.mult, ALU.add).then_inc(s_ms2, 1)

            def residual(n, hs):
                at(v, s_rs2, 1, n, 1)
                at(v, pg_w, 4, n, 4)
                for c in range(UC):
                    ins = V.scalar_tensor_tensor(h_tok[:, hs + c, :], PG[:, c * P:(c + 1) * P], rs2[:, c:c + 1],
                                                 h_tok[:, hs + c, :], ALU.mult, ALU.add)
                cB.link(ins)
                v.sem_inc(pg_r, 1)
                cB.end()

            fold_a(0)
            A1(0, 0)
            dt_bias_add(0)
            softplus(0)
            for g in range(4):
                taps(0, g)
            split(0)
            cT_copy(0, 0)
            dtx_(0, 0)

            def layer(l, last):
                fold_b(l)
                for u in range(UNITS):
                    n, p = l * UNITS + u, u % 2
                    more = not (last and u == UNITS - 1)
                    if more:
                        if u == UNITS - 1:
                            fold_a(l + 1)
                        A1(n + 1, (u + 1) % UNITS * UC)
                        dt_bias_add(n + 1)
                    for i in range(8):
                        M(n, p, i)
                        if i == 0:
                            yinter(n)
                        if more and i % 2 == 1:
                            taps(n + 1, i // 2)
                        if more and i == 2:
                            softplus(n + 1)
                        if more and i == 5:
                            split(n + 1)
                    if more:
                        cT_copy(n + 1, 1 - p)
                    gate(n, p)
                    meansq(n)
                    if more:
                        dtx_(n + 1, 1 - p)
                    residual(n, u * UC)

            with v.Fori(0, LAYERS - 1) as l:
                layer(l, False)
            layer(LAYERS - 1, True)

            cS.link(V.tensor_tensor(lnt[:], h_tok[:], h_tok[:], ALU.mult))
            cS.link(V.tensor_reduce(lnv[:], lnt[:], AX.X, ALU.add))
            v.wait_ge(s_h0, 2)
            cS.link(V.tensor_scalar(lnv[:], lnv[:], 1.0 / DM, EPS, ALU.mult, ALU.add))
            v.sem_inc(s_h0, 3)
            v.wait_ge(s_h0, 6)
            for c in range(CHUNKS):
                ins = V.scalar_tensor_tensor(lnt[:, c, :], h_tok[:, c, :], lnv[:, c:c + 1], bc[2][:, c // 2, :],
                                             ALU.mult, ALU.mult)
            cS.link(ins)
            V.tensor_tensor(x_tok[:], x_tok[:], lnt[:], ALU.add).then_inc(s_out, 1)
            v.wait_ge(s_out, 1)


class Norm:

    def __init__(self, nc, sb, sem, shared, mod, j, bk, w, r, per, tag):
        self.nc, self.shared, self.mod, self.j = nc, shared, mod, j
        self.bk, self.w, self.r, self.per = bk, w, r, per
        self.bns, self.bna = sb(f"{tag}_bns", [P, UC, 6]), sb(f"{tag}_bna", [P, UC, 2])
        self.var, self.rstd = sb(f"{tag}_var", [P, UC]), sb(f"{tag}_rstd", [P, UC])
        self.xn, self.hT = sb(f"{tag}_xn", [P, UC, DM]), sb(f"{tag}_hT", [P, UNIT])
        self.modu = sb(f"{tag}_modu", [P, 2, 2])
        self.s_var, self.s_rstd, self.s_xn, self.s_mod = (sem(f"{tag}_{n}") for n in ("var", "rstd", "xn", "mod"))

    def vector(self, v, u, link):
        V, x = self.nc.vector, self.shared.x_tok
        for c in range(UC):
            ins = V.bn_stats(self.bns[:, c, :], x[:, u * UC + c, :])
        link(ins)
        V.tensor_scalar(self.modu[:, 0, :], self.mod[:, self.j + 1, bass.ds(2 * u, 2)], 1.0, None, ALU.add)
        V.tensor_scalar(self.modu[:, 1, :], self.mod[:, self.j, bass.ds(2 * u, 2)], 0.0, None,
                        ALU.add).then_inc(self.s_mod, 1)
        for c in range(UC):
            ins = V.bn_aggr(self.bna[:, c, :], self.bns[:, c, :])
        link(ins)
        V.tensor_scalar(self.var[:], self.bna[:, :, 1], EPS, None, ALU.add).then_inc(self.s_var, 1)
        v.wait_ge(self.s_rstd, u + 1)
        for c in range(UC):
            ins = V.tensor_scalar(self.xn[:, c, :], x[:, u * UC + c, :], self.bna[:, c, 0:1], self.rstd[:, c:c + 1],
                                  ALU.subtract, ALU.mult)
        ins.then_inc(self.s_xn, 1)

    def gpsimd(self, g, u):
        g.wait_ge(self.s_var, u + 1)
        self.nc.gpsimd.tensor_tensor(self.rstd[:], self.var[:], self.shared.mhalf[:, 0:UC],
                                     ALU.pow).then_inc(self.s_rstd, 1)

    def tensor(self, pe, u):
        pe.wait_ge(self.s_xn, u + 1)
        pe.wait_ge(self.r, u * self.per + FREE)
        for c in range(UC):
            ins = pe.transpose(self.bk[:, c * P:(c + 1) * P], self.xn[:, c, :], self.shared.ident[:])
        ins.then_inc(self.w, 1)

    def scalar(self, act, u):
        act.wait_ge(self.s_mod, u + 1)
        act.wait_ge(self.w, u * self.per + 1)
        for b in range(2):
            ins = self.nc.scalar.activation(self.hT[:, b * SEQ:(b + 1) * SEQ], self.bk[:, b * SEQ:(b + 1) * SEQ],
                                            ACT.Identity, bias=self.modu[:, 1, b:b + 1],
                                            scale=self.modu[:, 0, b:b + 1])
        ins.then_inc(self.r, 1)


def split3(V, link, parts, src, tmp):
    link(V.tensor_copy(parts[0], src))
    link(V.tensor_tensor(tmp, src, parts[0], ALU.subtract))
    link(V.tensor_copy(parts[1], tmp))
    link(V.tensor_tensor(tmp, tmp, parts[1], ALU.subtract))
    return V.tensor_copy(parts[2], tmp)


def mixture(nc, ctx, bank, shared, mo, tag):
    sb, sem0 = allocators(nc, ctx)
    sem = lambda n: sem0(f"{tag}_{n}")
    PGate, PUp, PCo, PAcc, PM = bank[0:2], bank[2:4], bank[4:6], bank[6], bank[7]
    s_mix, s_down, s_lg, s_ex, s_co, s_chain, s_end = (sem(n) for n in "s_mix s_down s_lg s_ex s_co s_chain s_end".split())
    gate_w, gate_r = [sem("gate_w0"), sem("gate_w1")], [sem("gate_r0"), sem("gate_r1")]
    up_w, up_r = [sem("up_w0"), sem("up_w1")], [sem("up_r0"), sem("up_r1")]
    co_w, co_r = [sem("co_w0"), sem("co_w1")], [sem("co_r0"), sem("co_r1")]
    acc_w, acc_r, pm_w, pm_r = sem("acc_w"), sem("acc_r"), sem("pm_w"), sem("pm_r")
    G, R = mo.groups, mo.routed
    turns = [(G + 1) // 2, G // 2]
    cturns = [(R + 1) // 2, R // 2]
    PMT = 3
    norm = Norm(nc, sb, sem, shared, mo.mod, 3, PM, pm_w, pm_r, PMT, tag)
    hT = norm.hT
    lg = sb(f"{tag}_lg", [P, UC, EXPERTS])
    top = sb(f"{tag}_top", [P, UC, 8])
    idx = sb(f"{tag}_idx", [P, UC, 8], U32)
    idf = sb(f"{tag}_idf", [P, UC, 8])
    ex = sb(f"{tag}_ex", [P, UC, EXPERTS + 1])
    z, z2, z3 = (sb(f"{tag}_z{i}", [P, UC]) for i in range(3))
    wt = [sb(f"{tag}_wt{i}", [P, UC]) for i in range(2)]
    oh = [sb(f"{tag}_oh{i}", [P, UC, EXPERTS]) for i in range(2)]
    cop = sb(f"{tag}_cop", [P, UC, P], BF16)
    copk = [cop[:, :, k * EXPERTS:(k + 1) * EXPERTS] for k in range(PARTS)]
    coT = sb(f"{tag}_coT", [PARTS * EXPERTS, UNIT], BF16)
    sg = [sb(f"{tag}_sg{i}", [P, UNIT]) for i in range(2)]
    it = [sb(f"{tag}_it{i}", [P, UNIT]) for i in range(2)]
    res = sb(f"{tag}_res", [P, UC, DM])
    block = ctx.enter_context(nc.Block())

    @block.sync
    def _(sp):
        for free in (*gate_r, *up_r, *co_r, acc_r, pm_r, s_down):
            sp.sem_inc(free, FREE)

    @block.gpsimd
    def _(g):
        with g.Fori(0, UNITS) as u:
            norm.gpsimd(g, u)

    @block.tensor
    def _(pe):
        def gate_up(u, g):
            b = g % 2
            for bk, w, r, wt_ in ((PGate[b], gate_w[b], gate_r[b], mo.gate), (PUp[b], up_w[b], up_r[b], mo.up)):
                pe.wait_ge(r, u * turns[b] + g // 2 + FREE)
                pe.matmul(bk[:], wt_[:, g, :], hT[:], start=True, stop=True).then_inc(w, 1)

        def coefficients(u, g):
            b = g % 2
            pe.wait_ge(co_r[b], u * cturns[b] + g // 2 + FREE)
            pe.matmul(PCo[b][:], mo.sel[:, g, :], coT[:], start=True, stop=True).then_inc(co_w[b], 1)

        def down(u, g):
            pe.wait_ge(s_mix, u * G + g + 1)
            if g == 0:
                pe.wait_ge(acc_r, u + FREE)
            for c in range(UC):
                ins = pe.matmul(PAcc[:, c * P:(c + 1) * P], it[g % 2][:, c * P:(c + 1) * P], mo.down[:, g, :],
                                start=(g == 0 and c == 0), stop=(g == G - 1), skip_group_check=True)
            ins.then_inc(s_down, 1)

        with pe.Fori(0, UNITS) as u:
            norm.tensor(pe, u)
            pe.wait_ge(pm_r, u * PMT + 1 + FREE)
            for c in range(UC):
                ins = pe.matmul(PM[:, c * EXPERTS:(c + 1) * EXPERTS], hT[:, c * P:(c + 1) * P], mo.router[:],
                                start=True, stop=True)
            ins.then_inc(pm_w, 1)
            gate_up(u, 0)
            gate_up(u, 1)
            pe.wait_ge(s_co, u + 2)
            pe.wait_ge(pm_r, u * PMT + 2 + FREE)
            dst = PM[:, 0:UNIT // 2].bitcast(BF16)
            for c in range(UC):
                ins = pe.transpose(dst[:, c * P:(c + 1) * P], cop[:, c, :],
                                   shared.identb[:])
            ins.then_inc(pm_w, 1)
            pe.wait_ge(pm_r, u * PMT + 3 + FREE)
            for g in range(G):
                if g < R:
                    coefficients(u, g)
                if g >= 1:
                    down(u, g - 1)
                if g >= 1 and g + 1 < G:
                    gate_up(u, g + 1)
            down(u, G - 1)

    @block.scalar
    def _(act):
        with act.Fori(0, UNITS) as u:
            norm.scalar(act, u)
            act.wait_ge(s_lg, u + 1)
            nc.scalar.activation(ex[:], ex[:], ACT.Exp).then_inc(s_ex, 1)
            for g in range(G):
                b = g % 2
                act.wait_ge(gate_w[b], u * turns[b] + g // 2 + 1)
                act.wait_ge(up_r[b], u * turns[b] + g // 2 + FREE)
                nc.scalar.activation(sg[b][:], PGate[b][:], ACT.Silu).then_inc(gate_r[b], 1)

    @block.vector
    def _(v):
        V = nc.vector
        V.memset(cop[:], 0.0).then_inc(s_co, 1)
        v.wait_ge(s_co, 1)
        ch = Chain(v, s_chain, LN_LINKS + 16 + (4 if mo.norm else 0) + R + 1)
        link = ch.link
        v.wait_ge(shared.s_w2, 16 * 19)
        with v.Fori(0, UNITS) as u:
            ch.start(u)
            norm.vector(v, u, link)
            v.wait_ge(pm_w, u * PMT + 2)
            link(V.tensor_copy(lg[:].rearrange("p c e -> p (c e)"), PM[:, 0:UC * EXPERTS]))
            v.sem_inc(pm_r, 1)
            for c in range(UC):
                ins = V.max(top[:, c, :], lg[:, c, :])
            link(ins)
            V.tensor_tensor(ex[:, :, EXPERTS], top[:, :, 1], top[:, :, 0], ALU.subtract)
            for c in range(UC):
                ins = V.max_index(idx[:, c, :], top[:, c, :], lg[:, c, :])
            link(ins)
            V.tensor_tensor(ex[:, :, 0:EXPERTS], lg[:], top[:, :, 0:1].to_broadcast([P, UC, EXPERTS]),
                            ALU.subtract).then_inc(s_lg, 1)
            link(V.tensor_copy(idf[:], idx[:]))
            for k in range(2):
                link(V.tensor_tensor(oh[k][:], shared.iota[:, None, :].to_broadcast([P, UC, EXPERTS]),
                                     idf[:, :, k:k + 1].to_broadcast([P, UC, EXPERTS]), ALU.is_equal))
            v.wait_ge(s_ex, u + 1)
            link(V.tensor_reduce(z[:], ex[:, :, 0:EXPERTS], AX.X, ALU.add))
            link(V.reciprocal(wt[0][:], z[:]))
            link(V.tensor_tensor(wt[1][:], wt[0][:], ex[:, :, EXPERTS], ALU.mult))
            if mo.norm:
                link(V.scalar_tensor_tensor(z2[:], wt[0][:], 1e-9, wt[1][:], ALU.add, ALU.add))
                link(V.reciprocal(z3[:], z2[:]))
                for k in range(2):
                    link(V.tensor_tensor(wt[k][:], wt[k][:], z3[:], ALU.mult))
            for k in range(2):
                link(V.tensor_tensor(oh[k][:], oh[k][:], wt[k][:, :, None].to_broadcast([P, UC, EXPERTS]), ALU.mult))
            link(V.tensor_tensor(oh[0][:], oh[0][:], oh[1][:], ALU.add))
            split3(V, link, copk, oh[0][:], oh[1][:]).then_inc(s_co, 1)
            v.wait_ge(pm_w, u * PMT + 3)
            V.tensor_copy(coT[:], PM[0:PARTS * EXPERTS, 0:UNIT // 2].bitcast(BF16)).then_inc(pm_r, 1)
            for g in range(G):
                b = g % 2
                v.wait_ge(up_w[b], u * turns[b] + g // 2 + 1)
                v.wait_ge(gate_r[b], u * turns[b] + g // 2 + 1 + FREE)
                v.wait_ge(s_down, u * G + max(g - 1, 0) + FREE)
                if g < R:
                    V.tensor_tensor(it[b][:], sg[b][:], PUp[b][:], ALU.mult).then_inc(up_r[b], 1)
                    v.wait_ge(up_r[b], u * turns[b] + g // 2 + 1 + FREE)
                    v.wait_ge(co_w[b], u * cturns[b] + g // 2 + 1)
                    link(V.tensor_tensor(it[b][:], it[b][:], PCo[b][:], ALU.mult))
                    v.sem_inc(co_r[b], 1)
                    v.sem_inc(s_mix, 1)
                else:
                    V.tensor_tensor(it[b][:], sg[b][:], PUp[b][:], ALU.mult).then_inc(up_r[b], 1)
                    v.wait_ge(up_r[b], u * turns[b] + g // 2 + 1 + FREE)
                    v.sem_inc(s_mix, 1)
            residual(v, V, link, u, shared, mo.gate_bc, res, PAcc, s_down, (u + 1) * G + FREE, acc_r, u + 1)
            ch.end()


def residual(v, V, link, u, shared, gate_bc, res, bk, s_done, value, r, r_value, bias=None):
    v.wait_ge(s_done, value)
    acc = bk[:].rearrange("p (c d) -> p c d", d=DM)
    if bias is not None:
        link(V.tensor_tensor(res[:], acc, bias[:, None, :].to_broadcast([P, UC, DM]), ALU.add))
        acc = res[:]
    for b in range(2):
        ins = V.tensor_tensor(res[:, 2 * b:2 * b + 2, :], acc[:, 2 * b:2 * b + 2, :],
                              gate_bc[:, 2 * u + b, None, :].to_broadcast([P, 2, DM]), ALU.mult)
    ins.then_inc(r, 1)
    v.wait_ge(r, r_value + FREE)
    x = shared.x_tok[:, bass.ds(u * UC, UC), :]
    link(V.tensor_tensor(x, x, res[:], ALU.add))


def attention(nc, ctx, bank, shared):
    sb, sem = allocators(nc, ctx)
    PS, PT, PO, PX, PZ = bank[0:2], bank[2:4], bank[4:6], bank[6], bank[7]
    ps_w, ps_r = [sem("ps_w0"), sem("ps_w1")], [sem("ps_r0"), sem("ps_r1")]
    pt_w, pt_r = [sem("pt_w0"), sem("pt_w1")], [sem("pt_r0"), sem("pt_r1")]
    px_w, px_r, pz_w, pz_r, po_r = sem("px_w"), sem("px_r"), sem("pz_w"), sem("pz_r"), sem("po_r")
    s_qm, s_v, s_mp, s_pv, s_on, s_chain = (sem(f"at_{n}") for n in "qm v mp pv on chain".split())
    XT = 8
    SCALE = float(AD) ** -0.5
    GH = 4
    norm = Norm(nc, sb, sem, shared, shared.mod[1], 0, PX, px_w, px_r, XT, "at")
    hT = norm.hT
    qT, kT = sb("qT", [P, UNIT]), sb("kT", [P, UNIT])
    qm = [sb(f"qm{r}", [P, UNIT]) for r in range(GH)]
    bq = sb("bq", [P, 1])
    Vp = sb("Vp", [P, UC, AH, 32])
    mx = sb("mx", [P, UC, AH])
    mt = sb("mt", [P, UC, AH])
    mp = sb("mp", [P, UC, P], BF16)
    mT = [sb(f"mT{i}", [PARTS * AH, SEQ], BF16) for i in range(2)]
    Pt = [sb(f"Pt{i}", [P, 2, SEQ]) for i in range(8)]
    OT = sb("OT", [P, 4, SEQ])
    rec = sb("rec", [P, AH])
    on = sb("on", [P, UC, DM])
    oT = sb("oT", [P, UNIT])
    res = sb("at_res", [P, UC, DM])
    block = ctx.enter_context(nc.Block())

    @block.sync
    def _(sp):
        for free in (*ps_r, *pt_r, po_r, px_r, pz_r, s_pv):
            sp.sem_inc(free, FREE)

    @block.gpsimd
    def _(g):
        with g.Fori(0, UNITS) as u:
            norm.gpsimd(g, u)

    @block.tensor
    def _(pe):
        def scores(u, b, h):
            i = b * AH + h
            g, r, bk = h // GH, h % GH, i % 2
            pe.wait_ge(ps_r[bk], u * AH + i // 2 + FREE)
            for c in range(2):
                at0 = b * SEQ + c * P
                ins = pe.matmul(PS[bk][:, c * SEQ:(c + 1) * SEQ], qm[r][32 * g:32 * g + 32, at0:at0 + P],
                                kT[32 * g:32 * g + 32, b * SEQ:(b + 1) * SEQ], start=True, stop=True)
            ins.then_inc(ps_w[bk], 1)

        def maxima(u, b):
            pe.wait_ge(s_mp, u * 2 + b + 1)
            pe.wait_ge(px_r, u * XT + 4 + b + FREE)
            dst = PX[:, 0:P].bitcast(BF16)
            for c in range(2):
                ins = pe.transpose(dst[:, c * P:(c + 1) * P], mp[:, 2 * b + c, :],
                                   shared.identb[:])
            ins.then_inc(px_w, 1)

        def scores_T(u, b, h):
            i = b * AH + h
            g, r, bk = h // GH, h % GH, i % 2
            pe.wait_ge(pt_r[bk], u * AH + i // 2 + FREE)
            for c in range(2):
                at0, half = b * SEQ + c * P, slice(c * SEQ, (c + 1) * SEQ)
                pe.matmul(PT[bk][:, half], shared.selm[:, h, :], mT[b][:], start=True, stop=False)
                ins = pe.matmul(PT[bk][:, half], kT[32 * g:32 * g + 32, at0:at0 + P],
                                qm[r][32 * g:32 * g + 32, b * SEQ:(b + 1) * SEQ], start=False, stop=True)
            ins.then_inc(pt_w[bk], 1)

        def values(u, b, g):
            i = b * AH + GH * g
            for bk in range(2):
                pe.wait_ge(pt_r[bk], u * AH + i // 2 + 2 + FREE)
            if g % 2 == 0:
                pe.wait_ge(po_r, (u * 2 + b) * 2 + FREE)
            for c in range(2):
                for r in range(GH):
                    ins = pe.matmul(PO[g // 2][32 * r:32 * r + 32, (g % 2) * SEQ:(g % 2 + 1) * SEQ],
                                    Vp[:, 2 * b + c, GH * g + r, :], Pt[(i + r) % 8][:, c, :],
                                    start=(c == 0), stop=(c == 1))
            ins.then_inc(s_pv, 1)

        def turn_o(u, b):
            pe.wait_ge(po_r, (u * 2 + b + 1) * 2 + FREE)
            for c in range(2):
                pe.wait_ge(pz_r, u * 4 + 2 * b + c + FREE)
                for g in range(4):
                    ins = pe.transpose(PZ[:, g * P:(g + 1) * P], OT[:, g, c * P:(c + 1) * P], shared.ident[:])
                ins.then_inc(pz_w, 1)

        with pe.Fori(0, UNITS) as u:
            norm.tensor(pe, u)
            for k in range(2):
                pe.wait_ge(px_r, u * XT + 1 + k + FREE)
                pe.matmul(PX[:], shared.wqkv[:, k * DM:(k + 1) * DM], hT[:], start=True, stop=True).then_inc(px_w, 1)
            pe.wait_ge(px_r, u * XT + 3 + FREE)
            for c in range(UC):
                ins = pe.matmul(PX[:, c * DM:(c + 1) * DM], hT[:, c * P:(c + 1) * P], shared.wqkv[:, 2 * DM:3 * DM],
                                start=True, stop=True)
            ins.then_inc(px_w, 1)
            pe.wait_ge(s_qm, u + 1)
            for h in range(AH):
                scores(u, 0, h)
            maxima(u, 0)
            pe.wait_ge(px_r, u * XT + 5 + FREE)
            for h in range(AH):
                scores_T(u, 0, h)
                scores(u, 1, h)
                if h % GH == 1 and h > GH:
                    values(u, 0, h // GH - 1)
            values(u, 0, 3)
            maxima(u, 1)
            pe.wait_ge(px_r, u * XT + 6 + FREE)
            for h in range(AH):
                scores_T(u, 1, h)
                if h % GH == 1 and h > GH:
                    values(u, 1, h // GH - 1)
                if h == 2:
                    turn_o(u, 0)
            values(u, 1, 3)
            turn_o(u, 1)
            pe.wait_ge(s_on, u * 4 + 4)
            pe.wait_ge(px_r, u * XT + 6 + FREE)
            for c in range(UC):
                ins = pe.transpose(PX[:, c * P:(c + 1) * P], on[:, c, :], shared.ident[:])
            ins.then_inc(px_w, 1)
            pe.wait_ge(px_r, u * XT + 7 + FREE)
            for c in range(UC):
                ins = pe.matmul(PX[:, c * DM:(c + 1) * DM], oT[:, c * P:(c + 1) * P], shared.wproj[:],
                                start=True, stop=True)
            ins.then_inc(px_w, 1)

    @block.scalar
    def _(act):
        with act.Fori(0, UNITS) as u:
            norm.scalar(act, u)
            for k, dst, bias, scale in ((0, qT, bq[:, 0:1], SCALE), (1, kT, shared.bqk[:, 1:2], 1.0)):
                act.wait_ge(px_w, u * XT + 2 + k)
                nc.scalar.activation(dst[:], PX[:], ACT.Identity, bias=bias, scale=scale).then_inc(px_r, 1)
            for b in range(2):
                for h in range(AH):
                    i = b * AH + h
                    act.wait_ge(pt_w[i % 2], u * AH + i // 2 + 1)
                    act.wait_ge(s_pv, u * 8 + max(i // GH - 1, 0) + FREE)
                    nc.scalar.activation(Pt[i % 8][:].rearrange("p c t -> p (c t)"), PT[i % 2][:],
                                         ACT.Exp).then_inc(pt_r[i % 2], 1)
                act.wait_ge(s_pv, u * 8 + b * 4 + 4 + FREE)
                if b == 1:
                    act.wait_ge(pz_w, u * 4 + 2)
                for k in range(2):
                    nc.scalar.activation(OT[:, 2 * k:2 * k + 2, :].rearrange("p g t -> p (g t)"), PO[k][:],
                                         ACT.Identity).then_inc(po_r, 1)
            act.wait_ge(px_w, u * XT + 7)
            nc.scalar.activation(oT[:], PX[:], ACT.Identity).then_inc(px_r, 1)

    @block.vector
    def _(v):
        V = nc.vector
        ch = Chain(v, s_chain, LN_LINKS + 2 * 5 + 4 + 2)
        link = ch.link
        V.memset(mp[:], 0.0)
        V.memset(Vp[:], 0.0).then_inc(s_v, 1)
        v.wait_ge(s_v, 1)
        V.memset(Vp[:, :, :, AD], 1.0)
        V.tensor_scalar(bq[:], shared.bqk[:, 0:1], SCALE, None, ALU.mult).then_inc(s_v, 1)
        v.wait_ge(s_v, 2)
        with v.Fori(0, UNITS) as u:
            ch.start(u)
            norm.vector(v, u, link)
            v.wait_ge(px_r, u * XT + 2 + FREE)
            for r in range(GH):
                ins = V.tensor_scalar(qm[r][:], qT[:], shared.headmask[:, r:r + 1], None, ALU.mult)
            ins.then_inc(s_qm, 1)
            v.wait_ge(px_w, u * XT + 4)
            for c in range(UC):
                ins = V.tensor_tensor(Vp[:, c, :, 0:AD], PX[:, c * DM:(c + 1) * DM].rearrange("p (h d) -> p h d", d=AD),
                                      shared.bv[:].rearrange("p (h d) -> p h d", d=AD), ALU.add)
            ins.then_inc(px_r, 1)
            for b in range(2):
                for h in range(AH):
                    i = b * AH + h
                    v.wait_ge(ps_w[i % 2], u * AH + i // 2 + 1)
                    V.tensor_reduce(mx[:, 2 * b:2 * b + 2, h], PS[i % 2][:].rearrange("p (c t) -> p c t", c=2), AX.X,
                                    ALU.max).then_inc(ps_r[i % 2], 1)
                v.wait_ge(ps_r[1], u * AH + (b + 1) * AH // 2 + FREE)
                two = slice(2 * b, 2 * b + 2)
                link(V.tensor_scalar(mx[:, two, :], mx[:, two, :], -1.0, None, ALU.mult))
                split3(V, link, [mp[:, two, k * AH:(k + 1) * AH] for k in range(PARTS)], mx[:, two, :],
                       mt[:, two, :]).then_inc(s_mp, 1)
                v.wait_ge(px_w, u * XT + 5 + b)
                V.tensor_copy(mT[b][:], PX[0:PARTS * AH, 0:P].bitcast(BF16)).then_inc(px_r, 1)
            for k in range(4):
                o = PZ[:].rearrange("p (h d) -> p h d", d=32)
                v.wait_ge(pz_w, u * 4 + k + 1)
                link(V.reciprocal(rec[:], o[:, :, AD]))
                V.tensor_tensor(on[:, k, :].rearrange("p (h d) -> p h d", d=AD), o[:, :, 0:AD],
                                rec[:, :, None].to_broadcast([P, AH, AD]), ALU.mult).then_inc(pz_r, 1)
                v.wait_ge(pz_r, u * 4 + k + 1 + FREE)
                v.sem_inc(s_on, 1)
            residual(v, V, link, u, shared, shared.bc[4], res, PX, px_w, (u + 1) * XT, px_r, (u + 1) * XT,
                     bias=shared.bp)
            ch.end()


def store(nc, ctx, shared, out):
    s_out = ctx.enter_context(nc.semaphore("s_store"))
    block = ctx.enter_context(nc.Block())

    @block.sync
    def _(sp):
        sp.dma_start(out.rearrange("b (i p) d -> p (b i) d", p=P), shared.x_tok[:]).then_inc(s_out, 16)
        sp.wait_ge(s_out, 16)


LN_LINKS = 2

def first(m):
    return isinstance(m, int) and m == 0


KA, KB = 1 + 14 + 5 + 8, 4


class Chain:

    def __init__(self, eng, sem, per):
        self.eng, self.sem, self.per = eng, sem, per

    def start(self, n):
        self.n, self.k = n, 0

    def link(self, ins):
        self.k += 1
        ins.then_inc(self.sem, 1)
        self.eng.wait_ge(self.sem, self.n * self.per + self.k)

    def end(self):
        assert self.k == self.per, self.k


_INS = {"x": "L0_attn_x", "W_in": "L0_attn_W_in", "conv_w": "L0_attn_conv_w", "conv_b": "L0_attn_conv_b",
        "dt_bias": "L0_attn_dt_bias", "A_log": "L0_attn_A_log", "D": "L0_attn_D",
        "gate_norm_w": "L0_attn_gate_norm_w", "W_out": "L0_attn_W_out", "block_norm_w": "L0_attn_block_norm_w",
        "final_norm_w": "L0_attn_final_norm_w", "c0": "L0_c", "wmod0": "L0_wmod", "c1": "L1_c", "wmod1": "L1_wmod"}


_INS.update({
    "router0": "L0_ffn_router_w", "gate0": "L0_ffn_gate_w", "up0": "L0_ffn_up_w", "down0": "L0_ffn_down_w",
    "sgate0": "L0_ffn_shared_gate_w", "sup0": "L0_ffn_shared_up_w", "sdown0": "L0_ffn_shared_down_w",
    "w_qkv": "L1_attn_w_qkv", "b_qkv": "L1_attn_b_qkv", "w_proj": "L1_attn_w_proj", "b_proj": "L1_attn_b_proj",
    "router1": "L1_ffn_router_w", "gate1": "L1_ffn_wg_r", "up1": "L1_ffn_wu_r", "down1": "L1_ffn_wd_r",
    "sgate1": "L1_ffn_wg_s", "sup1": "L1_ffn_wu_s", "sdown1": "L1_ffn_wd_s"})


def kernel(**inputs):
    import numpy as np
    import concourse.bacc as bacc
    from concourse.bass_utils import run_bass_kernel_spmd

    nc = bacc.Bacc("TRN2", target_bir_lowering=False, num_devices=1)
    arrays, args = {}, {}
    for arg, name in _INS.items():
        a = np.ascontiguousarray(inputs[name])
        arrays[f"in_{arg}"] = a
        args[arg] = nc.dram_tensor(f"in_{arg}", a.shape, mybir.dt.from_np(a.dtype), kind="ExternalInput").ap()
    args["out"] = nc.dram_tensor("out_x", (BATCH, SEQ, DM), F32, kind="ExternalOutput").ap()
    program(nc, **args)
    r = run_bass_kernel_spmd(nc, [arrays], core_ids=[0])
    return r.results[0]["out_x"]
```

```python
from contextlib import ExitStack

import concourse.bass as bass
from concourse import mybir

P = 128
F32 = mybir.dt.float32
BF16 = mybir.dt.bfloat16
U32 = mybir.dt.uint32
ALU = mybir.AluOpType
ACT = mybir.ActivationFunctionType
AX = mybir.AxisListType

BATCH, SEQ, DM = 8, 256, 128
CHUNK = 128
CHUNKS = BATCH * SEQ // CHUNK
UNIT = 512
UC = UNIT // CHUNK
UNITS = BATCH * SEQ // UNIT
LAYERS = 4
DI, HEADS, HD, NS, TAPS = 256, 8, 32, 128, 4
ZOFF, XOFF, DTOFF, DPROJ = 0, 256, 768, 776
PARTS = 3
PH = PARTS * HEADS
EPS = 1e-5
FREE = 1
EXPERTS, AH, AD = 16, 16, 8
PCW, PCB, PGW, PBN, PD_, PDTB, PA_, PLEN = 0, 16, 20, 22, 23, 25, 33, 41


def program(nc, x, W_in, conv_w, conv_b, dt_bias, A_log, D, gate_norm_w, W_out, block_norm_w, final_norm_w,
            c0, wmod0, c1, wmod1, router0, gate0, up0, down0, sgate0, sup0, sdown0, w_qkv, b_qkv, w_proj, b_proj,
            router1, gate1, up1, down1, sgate1, sup1, sdown1, out):
    with ExitStack() as whole:
        sb, sem = allocators(nc, whole)
        bank = [whole.enter_context(nc.psum_tensor(f"bank{i}", [P, 512], F32)) for i in range(8)]
        shared = Shared(sb, sem)
        with ExitStack() as ctx:
            mamba(nc, ctx, bank, shared, x, W_in, conv_w, conv_b, dt_bias, A_log, D, gate_norm_w, W_out,
                  block_norm_w, final_norm_w, c0, wmod0, c1, wmod1,
                  (router0, gate0, up0, down0, sgate0, sup0, sdown0, w_qkv, b_qkv, w_proj, b_proj,
                   router1, gate1, up1, down1, sgate1, sup1, sdown1))
        with ExitStack() as ctx:
            mixture(nc, ctx, bank, shared, shared.moe0, "f0")
        with ExitStack() as ctx:
            attention(nc, ctx, bank, shared)
        with ExitStack() as ctx:
            mixture(nc, ctx, bank, shared, shared.moe1, "f1")
        with ExitStack() as ctx:
            store(nc, ctx, shared, out)


def allocators(nc, ctx):
    def sb(name, shape, dt=F32):
        return ctx.enter_context(nc.sbuf_tensor(name, shape, dt))

    def sem(name):
        return ctx.enter_context(nc.semaphore(name))

    return sb, sem


class Moe:

    def __init__(self, sb, name, f, norm, mod, gate_bc):
        self.f, self.norm, self.mod, self.gate_bc = f, norm, mod, gate_bc
        self.per = P // f
        self.routed = EXPERTS // self.per
        self.groups = self.routed + 1
        self.router = sb(f"{name}_router", [P, EXPERTS])
        self.gate = sb(f"{name}_gate", [P, self.groups, P])
        self.up = sb(f"{name}_up", [P, self.groups, P])
        self.down = sb(f"{name}_down", [P, self.groups, DM])
        self.sel = sb(f"{name}_sel", [P, self.routed, P], BF16)


class Shared:

    def __init__(self, sb, sem):
        self.ident = sb("ident", [P, P])
        self.identb = sb("identb", [P, P], BF16)
        self.mhalf = sb("mhalf", [P, CHUNKS])
        self.iota = sb("iota", [P, EXPERTS])
        self.x_tok = sb("x_tok", [P, CHUNKS, DM])
        self.mod = [sb(f"mod{i}", [P, 6, BATCH]) for i in range(2)]
        self.bc = [sb(f"bc{i}", [P, BATCH, DM]) for i in range(6)]
        self.moe0 = Moe(sb, "moe0", 64, False, self.mod[0], self.bc[3])
        self.moe1 = Moe(sb, "moe1", 32, True, self.mod[1], self.bc[5])
        self.wqkv = sb("wqkv", [P, 3 * DM])
        self.wproj = sb("wproj", [P, DM])
        self.bqk = sb("bqk", [P, 2])
        self.bv = sb("bv", [P, DM])
        self.bp = sb("bp", [P, DM])
        self.selm = sb("selm", [P, AH // 4, P], BF16)
        self.s_w2 = sem("s_w2")


def mamba(nc, ctx, bank, shared, x, W_in, conv_w, conv_b, dt_bias, A_log, D, gate_norm_w, W_out, block_norm_w,
          final_norm_w, c0, wmod0, c1, wmod1, later):
    if True:
        sb, sem = allocators(nc, ctx)
        PA, PDk, PG, PM, PY = bank[0:2], bank[2:4], bank[4], bank[5], bank[6:8]

        ident, identb, mhalf, x_tok, mod, bc = (shared.ident, shared.identb, shared.mhalf, shared.x_tok, shared.mod,
                                                shared.bc)
        ones = sb("ones", [P, P])
        triu = sb("triu", [P, P])
        maskneg = sb("maskneg", [P, 4, CHUNK], BF16)
        selh = sb("selh", [P, HEADS, P], BF16)
        negsel = sb("negsel", [P, HEADS, P], BF16)
        selq = sb("selq", [P, 2, P], BF16)

        wi_all = sb("wi_all", [P, LAYERS, DPROJ])
        wo_all = sb("wo_all", [P, LAYERS, 2, DM])
        par = sb("par", [P, LAYERS, PLEN])
        fnw = sb("fnw", [P, 1])
        cT = [sb(f"cT{i}", [P, BATCH]) for i in range(2)]
        wmod = [sb(f"wmod{i}", [P, 6, P]) for i in range(2)]
        wi = sb("wi", [P, DPROJ])
        wo = sb("wo", [P, 2, DM])
        pla = sb("pla", [P, PLEN])
        plb = sb("plb", [P, PLEN])

        h_tok = sb("h_tok", [P, CHUNKS, DM])
        modt = sb("modt", [P, 2, BATCH])

        sq = sb("sq", [P, UC, DM])
        ss = sb("ss", [P, UC])
        ms = sb("ms", [P, UC])
        rs = sb("rs", [P, UC])
        hn = sb("hn", [P, UC, DM])
        hnT = sb("hnT", [P, UNIT])
        cv = [sb(f"cv{g}", [P, UNIT]) for g in range(4)]
        feat = [[sb(f"feat{p}_{g}", [P, UNIT]) for g in range(4)] for p in range(2)]
        sz = [sb(f"sz{p}", [P, 2, UNIT]) for p in range(2)]
        va = [sb(f"va{i}", [P, UC * HEADS]) for i in range(8)]
        dts = sb("dts", [P, UC, HEADS])
        av = sb("av", [P, UC * HEADS])
        ct = sb("ct", [P, 2, UC * HEADS])
        cp = sb("cp", [P, UC, P], BF16)
        edec = sb("edec", [P, UC, HEADS])
        cTs = [sb(f"cTs{p}", [P, UNIT], BF16) for p in range(2)]
        dtx = [sb(f"dtx{p}", [P, UC, DI]) for p in range(2)]
        dtxd = [sb(f"dtxd{p}", [P, 2, DI]) for p in range(2)]
        Btok = [sb(f"Btok{p}", [P, 2, NS]) for p in range(2)]
        Gs = [sb(f"Gs{p}", [P, UC, CHUNK]) for p in range(2)]
        Ssb = sb("Ssb", [P, 2, DI])
        Ei = sb("Ei", [P, 2, 2, CHUNK])
        yi = sb("yi", [P, 2, 2, CHUNK])
        eb = [sb(f"eb{i}", [P, 4, CHUNK]) for i in range(2)]
        yts = [sb(f"yt{p}", [P, 2, UNIT]) for p in range(2)]
        gsq = sb("gsq", [P, 2, UNIT])
        ms2 = sb("ms2", [P, UC])
        rs2 = sb("rs2", [P, UC])

        pa_w, pa_r = [sem("pa_w0"), sem("pa_w1")], [sem("pa_r0"), sem("pa_r1")]
        pd_w, pd_r = [sem("pd_w0"), sem("pd_w1")], [sem("pd_r0"), sem("pd_r1")]
        pg_w, pg_r = sem("pg_w"), sem("pg_r")
        pm_w, pm_r = sem("pm_w"), sem("pm_r")
        (s_ld, s_x, s_const, s_setup, s_par, s_mod, s_modps, s_h0, s_ms, s_rs, s_hn, s_acc, s_feat, s_v, s_e,
         s_a, s_cp, s_diff, s_edec, s_dtxd, s_y, s_M, s_yt, s_yo, s_g, s_gsq, s_ssq, s_ms2, s_rs2, s_wa, s_wb, s_hend, s_out) = (
            sem(n) for n in ("s_ld s_x s_const s_setup s_par s_mod s_modps s_h0 s_ms s_rs s_hn s_acc s_feat s_v "
                             "s_e s_a s_cp s_diff s_edec s_dtxd s_y s_M s_yt s_yo s_g s_gsq s_ssq s_ms2 s_rs2 s_wa s_wb s_hend "
                             "s_out").split())
        dchA, dchB, dchP, dchS = sem("dchA"), sem("dchB"), sem("dchP"), sem("dchS")
        BASE = 6

        def pd_turn(i):
            c, q = i // 2, i % 2
            return c if q == 1 or c == 0 else c + 1

        def at(eng, s, per, n, m):
            eng.wait_ge(s, n * per + m)

        lnv = sb("lnv", [P, CHUNKS])
        bns = sb("bns", [P, CHUNKS, 6])
        bna = sb("bna", [P, CHUNKS, 2])
        lnt = sb("lnt", [P, CHUNKS, DM])
        gtmp = sb("gtmp", [P, 4, BATCH])

        def bcsrc(j):
            return (modt[:, 0, :], mod[0][:, 0, :], modt[:, 1, :], mod[0][:, 5, :], mod[1][:, 2, :], mod[1][:, 5, :])[j]

        NPAR = 5 * LAYERS + 2 + HEADS
        LOADS = 4 + 2 * LAYERS + NPAR

        ctx.enter_context(nc.allow_non_contiguous_dma(reason="a few small vectors, laid over partitions"))
        block = ctx.enter_context(nc.Block())

        @block.sync
        def _(sp):
            for free in (*pd_r, s_y):
                sp.sem_inc(free, FREE)
            sp.dma_start(cT[0][:], c0.rearrange("b k -> k b")).then_inc(s_ld, 16)
            sp.dma_start(wmod[0][:], wmod0.rearrange("k (j d) -> k j d", j=6)).then_inc(s_ld, 16)
            sp.dma_start(cT[1][:], c1.rearrange("b k -> k b")).then_inc(s_ld, 16)
            sp.dma_start(wmod[1][:], wmod1.rearrange("k (j d) -> k j d", j=6)).then_inc(s_ld, 16)
            sp.dma_start(x_tok[:], x.rearrange("b (i p) d -> p (b i) d", p=P)).then_inc(s_x, 16)
            for l in range(LAYERS):
                sp.dma_start(wi_all[:, l, :], W_in[l]).then_inc(s_ld, 16)
                sp.dma_start(wo_all[:, l, :, :], W_out[l].rearrange("(q p) d -> p q d", q=2)).then_inc(s_ld, 16)
            for l in range(LAYERS):
                sp.dma_start(par[:, l, PCW:PCW + 16].rearrange("p (g k) -> p g k", g=4),
                            conv_w[l].rearrange("(g p) k -> p g k", p=P)).then_inc(s_ld, 16)
                sp.dma_start(par[:, l, PCB:PCB + 4], conv_b[l].rearrange("(g p) -> p g", p=P),
                            ).then_inc(s_ld, 16)
                sp.dma_start(par[:, l, PGW:PGW + 2], gate_norm_w[l].rearrange("(g p) -> p g", p=P)).then_inc(s_ld, 16)
                sp.dma_start(par[:, l, PBN:PBN + 1], block_norm_w[l:l + 1, :].rearrange("o p -> p o")).then_inc(s_ld, 16)
                sp.dma_start(par[:, l, PDTB:PDTB + 8], dt_bias[l:l + 1, :].partition_broadcast(P)).then_inc(s_ld, 16)
            sp.dma_start(par[:, :, PA_:PA_ + 8], A_log.partition_broadcast(P)).then_inc(s_ld, 16)
            sp.dma_start(fnw[:], final_norm_w.rearrange("(p o) -> p o", o=1)).then_inc(s_ld, 16)
            for h in range(HEADS):
                sp.dma_start(par[32 * (h % 4):32 * (h % 4) + 32, :, PD_ + h // 4],
                            D[:, h].partition_broadcast(32)).then_inc(s_ld, 16)
            (router0, gate0, up0, down0, sgate0, sup0, sdown0, w_qkv, b_qkv, w_proj, b_proj,
             router1, gate1, up1, down1, sgate1, sup1, sdown1) = later
            m0, m1, r0, r1 = shared.moe0, shared.moe1, shared.moe0.routed, shared.moe1.routed
            late = [
                (m0.router[:], router0), (m1.router[:], router1),
                (m0.gate[:, 0:r0, :].rearrange("p g (e f) -> p (g e) f", f=m0.f), gate0.rearrange("e h f -> h e f")),
                (m0.up[:, 0:r0, :].rearrange("p g (e f) -> p (g e) f", f=m0.f), up0.rearrange("e h f -> h e f")),
                (m0.down[:, 0:r0, :], down0.rearrange("(g e) f d -> (e f) g d", g=r0)),
                (m0.gate[:, r0, :], sgate0), (m0.up[:, r0, :], sup0), (m0.down[:, r0, :], sdown0),
                (shared.wqkv[:], w_qkv), (shared.wproj[:], w_proj),
                *((shared.bqk[AH * c:AH * c + AH, :], b_qkv[0:2 * DM].rearrange("(k h c) -> c h k", k=2, c=AD)[c])
                  for c in range(AD)),
                (shared.bv[:], b_qkv[2 * DM:3 * DM].partition_broadcast(P)),
                (shared.bp[:], b_proj.partition_broadcast(P)),
                (m1.gate[:, 0:r1, :].rearrange("p g (e f) -> p (g e) f", f=m1.f), gate1.rearrange("e h f -> h e f")),
                (m1.up[:, 0:r1, :].rearrange("p g (e f) -> p (g e) f", f=m1.f), up1.rearrange("e h f -> h e f")),
                (m1.down[:, 0:r1, :], down1.rearrange("(g e) f d -> (e f) g d", g=r1)),
                (m1.gate[:, r1, :].rearrange("p (n f) -> p n f", n=2), sgate1.rearrange("n h f -> h n f")),
                (m1.up[:, r1, :].rearrange("p (n f) -> p n f", n=2), sup1.rearrange("n h f -> h n f")),
                (m1.down[:, r1, :], sdown1.rearrange("n f d -> (n f) d")),
            ]
            shared.late = len(late)
            for dst, src in late:
                sp.dma_start(dst, src).then_inc(shared.s_w2, 16)
            sp.wait_ge(shared.s_w2, 16 * len(late))

        @block.gpsimd
        def _(g):
            for t, v in ((ident, 0.0), (identb, 0.0), (ones, 1.0), (triu, 1.0), (maskneg, 0.0), (selh, 0.0),
                         (selq, 0.0), (mhalf, -0.5), (cp, 0.0), (shared.moe0.sel, 0.0), (shared.moe1.sel, 0.0),
                         (shared.selm, 0.0)):
                last = nc.gpsimd.memset(t[:], v)
            last.then_inc(s_setup, 1)
            g.wait_ge(s_setup, 1)
            nc.gpsimd.affine_select(out=ident[:], in_=ident[:], compare_op=ALU.not_equal, fill=1.0, base=0,
                                    pattern=[[-1, P]], channel_multiplier=1)
            nc.gpsimd.affine_select(out=identb[:], in_=identb[:], compare_op=ALU.not_equal, fill=1.0, base=0,
                                    pattern=[[-1, P]], channel_multiplier=1)
            nc.gpsimd.affine_select(out=triu[:], in_=triu[:], compare_op=ALU.is_ge, fill=0.0, base=0,
                                    pattern=[[1, P]], channel_multiplier=-1)
            nc.gpsimd.affine_select(out=maskneg[:], in_=maskneg[:], compare_op=ALU.is_ge, fill=-1e30, base=0,
                                    pattern=[[0, 4], [1, CHUNK]], channel_multiplier=-1)
            for k in range(PARTS):
                nc.gpsimd.affine_select(out=selh[:], in_=selh[:], compare_op=ALU.not_equal, fill=1.0, base=-HEADS * k,
                                        pattern=[[-1, HEADS], [0, P]], channel_multiplier=1)
                last = nc.gpsimd.affine_select(out=selq[:], in_=selq[:], compare_op=ALU.not_equal, fill=1.0,
                                               base=-HEADS * k, pattern=[[-4, 2], [-1, 4], [0, HD]],
                                               channel_multiplier=1)
                for mo in (shared.moe0, shared.moe1):
                    nc.gpsimd.affine_select(out=mo.sel[:], in_=mo.sel[:], compare_op=ALU.not_equal, fill=1.0,
                                            base=-EXPERTS * k, pattern=[[-mo.per, mo.routed], [-1, mo.per], [0, mo.f]],
                                            channel_multiplier=1)
                last = nc.gpsimd.affine_select(out=shared.selm[:], in_=shared.selm[:], compare_op=ALU.not_equal,
                                               fill=-1.0, base=-(AH // 4) * k, pattern=[[-1, AH // 4], [0, P]],
                                               channel_multiplier=1)
                last.then_inc(s_setup, 1)
                g.wait_ge(s_setup, 2 + k)
            nc.gpsimd.iota(shared.iota[:], pattern=[[1, EXPERTS]], base=0, channel_multiplier=0,
                           allow_small_or_imprecise_dtypes=True)
            nc.gpsimd.tensor_scalar(negsel[:], selh[:], -1.0, 0.0, ALU.mult, ALU.add).then_inc(s_const, 1)

            g.wait_ge(s_h0, 1)
            nc.gpsimd.tensor_tensor(lnv[:], lnv[:], mhalf[:], ALU.pow).then_inc(s_h0, 1)

            def A(m):
                at(g, s_ms, 1, m, 1)
                nc.gpsimd.tensor_tensor(rs[:], ms[:], mhalf[:, 0:UC], ALU.pow).then_inc(s_rs, 1)

            def A2(m, p):
                g.wait_ge(pa_r[0], m * 5 + BASE + 5)
                at(g, s_edec, 1, m, 1)
                src = dtx[p][:].rearrange("p (b i) (h d) -> p b i h d", i=2, h=HEADS)[:, :, 0]
                dst = dtxd[p][:].rearrange("p b (h d) -> p b h d", h=HEADS)
                e = edec[:].rearrange("p (b i) h -> p b i h", i=2)[:, :, 0]
                for b in range(2):
                    ins = nc.gpsimd.tensor_tensor(dst[:, b], src[:, b], e[:, b, :, None].to_broadcast([P, HEADS, HD]),
                                                  ALU.mult)
                ins.then_inc(s_dtxd, 1)

            def gate(n, p):
                yt = yts[p]
                """what came in with the sequence's first chunk, for the second; and silu(z)"""
                at(g, s_yt, 1, n, 1)
                odd = yt[:].rearrange("p q (b i t) -> p q b i t", b=2, i=2)[:, :, :, 1, :]
                nc.gpsimd.tensor_tensor(odd, odd, yi[:].rearrange("p b q t -> p q b t"), ALU.add).then_inc(s_yo, 1)
                at(g, s_yo, 1, n, 1)
                g.wait_ge(pa_r[0], n * 5 + 4 + BASE)
                nc.gpsimd.tensor_tensor(yt[:], yt[:], sz[p][:], ALU.mult).then_inc(s_g, 1)

            def C(n):
                at(g, s_ms2, 1, n, 1)
                nc.gpsimd.tensor_tensor(rs2[:], ms2[:], mhalf[:, 0:UC], ALU.pow).then_inc(s_rs2, 1)

            def step(n, p, more=True, more2=True):
                if more2:
                    A(n + 2)
                if not first(n):
                    C(n - 1)
                gate(n, p)
                if more:
                    A2(n + 1, 1 - p)

            A(0)
            A(1)
            A2(0, 0)
            step(0, 0)
            with g.Fori(0, LAYERS - 1) as l:
                for u in range(1, UNITS + 1):
                    step(l * UNITS + u, u % 2)
            for u in range(1, UNITS):
                step((LAYERS - 1) * UNITS + u, u % 2, u < UNITS - 1, u < UNITS - 2)
            C(LAYERS * UNITS - 1)
            g.wait_ge(s_h0, 5)
            nc.gpsimd.tensor_tensor(lnv[:], lnv[:], mhalf[:], ALU.pow).then_inc(s_h0, 1)

        @block.tensor
        def _(pe):
            pe.wait_ge(s_mod, 1)
            for i in range(2):
                for j in range(6):
                    ins = pe.matmul(PY[i][:, j * BATCH:(j + 1) * BATCH], wmod[i][:, j, :], cT[i][:],
                                    start=True, stop=True)
                ins.then_inc(s_modps, 1)
            pe.wait_ge(s_const, 1)
            pe.wait_ge(s_mod, 2)
            for j in range(6):
                for half in range(2):
                    k = 2 * j + half
                    if k >= 2:
                        pe.wait_ge(pa_r[half], j)
                    for b in range(4):
                        src = bcsrc(j)[:, 4 * half + b:4 * half + b + 1]
                        ins = pe.matmul(PA[half][:, b * DM:(b + 1) * DM], src.to_broadcast([P, P]), ident[:],
                                        start=True, stop=True)
                    ins.then_inc(pa_w[half], 1)

            def pa_turn(m, k):
                b = k % 2
                pe.wait_ge(pa_r[b], m * 5 + k // 2 + BASE)
                return PA[b], pa_w[b]

            def A1(m):
                bk, w = pa_turn(m, 0)
                at(pe, s_hn, 1, m, 1)
                for c in range(UC):
                    ins = pe.transpose(bk[:, c * P:(c + 1) * P], hn[:, c, :], ident[:])
                ins.then_inc(w, 1)

            def dt(m):
                pe.wait_ge(pa_r[0], m * 5 + BASE + 1)
                at(pe, pm_r, 3, m, 0)
                for c in range(UC):
                    ins = pe.matmul(PM[:, c * HEADS:(c + 1) * HEADS], hnT[:, c * P:(c + 1) * P],
                                    wi[:, DTOFF:DPROJ], start=True, stop=True)
                ins.then_inc(pm_w, 1)

            def proj(m, k, off):
                bk, w = pa_turn(m, k)
                pe.matmul(bk[:], wi[:, off:off + P], hnT[:], start=True, stop=True).then_inc(w, 1)

            def xproj(m, g):
                proj(m, 1 + g, XOFF + g * P)

            def zproj(m, q):
                proj(m, 5 + q, ZOFF + q * P)

            def cum(m):
                at(pe, s_a, 1, m, 1)
                at(pe, pm_r, 3, m, 1)
                if not (isinstance(m, int) and m < 2):
                    at(pe, s_ms2, 1, m - 2, 1)
                pe.matmul(PM[:, 0:UC * HEADS], triu[:], av[:], start=True, stop=True)
                pe.matmul(PM[:, UC * HEADS:2 * UC * HEADS], ones[:], av[:], start=True, stop=True).then_inc(pm_w, 1)

            def cTr(m):
                at(pe, s_cp, 1, m, 1)
                at(pe, pm_r, 3, m, 2)
                dst = PM[:, 0:UNIT // 2].bitcast(BF16)
                for c in range(UC):
                    ins = pe.transpose(dst[:, c * P:(c + 1) * P], cp[:, c, :], identb[:])
                ins.then_inc(pm_w, 1)

            def A3(m, p):
                f = feat[p]
                at(pe, s_feat, 4, m, 4)
                for j in range(2):
                    bk, w = pa_turn(m, 7 + j)
                    for i in range(2):
                        for q in range(2):
                            c = 2 * j + i
                            ins = pe.transpose(bk[:, i * DI + q * P:i * DI + (q + 1) * P],
                                               f[q][:, c * P:(c + 1) * P], ident[:])
                    ins.then_inc(w, 1)
                bk, w = pa_turn(m, 9)
                for b in range(2):
                    ins = pe.transpose(bk[:, b * P:(b + 1) * P], f[2][:, 2 * b * P:(2 * b + 1) * P], ident[:])
                ins.then_inc(w, 1)
                at(pe, pg_r, 4, m, 0)
                for c in range(UC):
                    cs = slice(c * P, (c + 1) * P)
                    ins = pe.matmul(PG[:, cs], f[2][:, cs], f[3][:, cs], start=True, stop=True)
                ins.then_inc(pg_w, 1)

            def S(n, p):
                pe.wait_ge(pa_r[1], n * 5 + BASE + 5)
                at(pe, s_dtxd, 1, n, 1)
                at(pe, pg_r, 4, n, 1)
                for b in range(2):
                    ins = pe.matmul(PG[:, b * DI:(b + 1) * DI], Btok[p][:, b, :], dtxd[p][:, b, :],
                                    start=True, stop=True)
                ins.then_inc(pg_w, 1)

            def inter(n, p):
                at(pe, pg_r, 4, n, 2)
                for b in range(2):
                    cs = slice((2 * b + 1) * P, (2 * b + 2) * P)
                    for q in range(2):
                        k = 2 * b + q
                        ins = pe.matmul(PG[:, k * P:(k + 1) * P], Ssb[:, b, q * P:(q + 1) * P], feat[p][3][:, cs],
                                        start=True, stop=True)
                ins.then_inc(pg_w, 1)

            def Einter(n, p):
                at(pe, pd_r[0], 5, n, 1 + FREE)
                for b in range(2):
                    cs = slice((2 * b + 1) * P, (2 * b + 2) * P)
                    for q in range(2):
                        k = 2 * b + q
                        ins = pe.matmul(PDk[0][:, k * P:(k + 1) * P], selq[:, q, :], cTs[p][:, cs],
                                        start=True, stop=True)
                ins.then_inc(pd_w[0], 1)

            def decay(n, p, i):
                c, q = i // 2, i % 2
                cs = slice(c * P, (c + 1) * P)
                if i == 0:
                    at(pe, pm_r, 3, n, 3)
                at(pe, pd_r[q], 5 - q, n, pd_turn(i) + FREE)
                bk = PDk[q]
                pe.matmul(bk[:], identb[:], maskneg[:].rearrange("p h t -> p (h t)"), start=True, stop=False)
                for r in range(4):
                    pe.matmul(bk[:, r * P:(r + 1) * P], selh[:, 4 * q + r, :], cTs[p][:, cs],
                              start=False, stop=False, skip_group_check=True)
                ins = pe.matmul(bk[:], cTs[p][:, cs], negsel[:, 4 * q:4 * q + 4, :].rearrange("k h t -> k (h t)"),
                                start=False, stop=True)
                ins.then_inc(pd_w[q], 1)

            def y(n, p, i):
                c, q = i // 2, i % 2
                at(pe, s_M, 8, n, i + 1)
                if i == 0 and not first(n):
                    at(pe, s_yt, 1, n - 1, 1)
                for r in range(4):
                    h = 4 * q + r
                    ins = pe.matmul(PY[q][32 * r:32 * r + 32, c * P:(c + 1) * P],
                                    dtx[p][:, c, h * HD:(h + 1) * HD], eb[q][:, r, :], start=True, stop=True)
                ins.then_inc(s_y, 1)

            def outp(n, p, l, turn):
                yt = yts[p]
                at(pe, s_g, 1, n, 1)
                pe.wait_ge(pg_r, turn)
                at(pe, s_wb, 1, l, 1)
                for c in range(UC):
                    cs = slice(c * P, (c + 1) * P)
                    for q in range(2):
                        ins = pe.matmul(PG[:, cs], yt[:, q, cs], wo[:, q, :], start=(q == 0), stop=(q == 1))
                ins.then_inc(pg_w, 1)

            def sumsq(n, turn):
                at(pe, s_gsq, 1, n, 1)
                pe.wait_ge(pm_r, turn)
                for c in range(UC):
                    cs = slice(c * P, (c + 1) * P)
                    for q in range(2):
                        ins = pe.matmul(PM[:, c:c + 1], gsq[:, q, cs], ones[:, 0:1],
                                        start=(q == 0), stop=(q == 1))
                ins.then_inc(s_ssq, 1)

            pe.wait_ge(s_wa, 1)
            A1(0)
            dt(0)
            for g in range(4):
                xproj(0, g)
            cum(0)
            cTr(0)
            zproj(0, 0)
            zproj(0, 1)
            decay(0, 0, 0)
            decay(0, 0, 1)
            A3(0, 0)
            A1(1)

            def step(l, u, more=True, more2=True):
                n, p = l * UNITS + u, u % 2
                for i in range(8):
                    if i == 0:
                        S(n, p)
                        Einter(n, p)
                        if more:
                            if u == UNITS - 1:
                                pe.wait_ge(s_wa, l + 2)
                            dt(n + 1)
                    if i == 1:
                        inter(n, p)
                    if i == 2:
                        if first(n):
                            pe.wait_ge(pg_r, 3)
                            pe.sem_inc(pg_w, 1)
                        else:
                            outp(n - 1, 1 - p, l if u > 0 else l - 1, n * 4 + 3)
                    if i == 3 and not first(n):
                        sumsq(n - 1, (n + 1) * 3 + 1 if more else n * 3 + 3)
                    if more:
                        if i in [1, 2, 3, 4]:
                            xproj(n + 1, [1, 2, 3, 4].index(i))
                        if i == 5:
                            cum(n + 1)
                        if i == 6:
                            zproj(n + 1, 0)
                        if i == 7:
                            cTr(n + 1)
                        if i == 7:
                            zproj(n + 1, 1)
                    y(n, p, i)
                    if i < 6:
                        decay(n, p, i + 2)
                if more:
                    decay(n + 1, 1 - p, 0)
                    decay(n + 1, 1 - p, 1)
                    A3(n + 1, 1 - p)
                if more2:
                    A1(n + 2)

            step(0, 0)
            with pe.Fori(0, LAYERS - 1) as l:
                for u in range(1, UNITS):
                    step(l, u)
                step(l + 1, 0)
            for u in range(1, UNITS):
                step(LAYERS - 1, u, u < UNITS - 1, u < UNITS - 2)
            outp(LAYERS * UNITS - 1, 1, LAYERS - 1, LAYERS * UNITS * 4)
            pe.wait_ge(s_ms2, LAYERS * UNITS - 1)
            sumsq(LAYERS * UNITS - 1, LAYERS * UNITS * 3)

        @block.scalar
        def _(act):
            act.wait_ge(s_ld, 16 * LOADS)
            for i in range(2):
                ins = nc.scalar.activation(cT[i][:], cT[i][:], ACT.Silu)
            ins.then_inc(s_mod, 1)
            nc.scalar.activation(par[:, :, PA_:PA_ + 8], par[:, :, PA_:PA_ + 8], ACT.Exp).then_inc(s_par, 1)
            for k in range(12):
                half = k % 2
                act.wait_ge(pa_w[half], k // 2 + 1)
                nc.scalar.activation(bc[k // 2][:, 4 * half:4 * half + 4, :].rearrange("p b d -> p (b d)"),
                                     PA[half][:], ACT.Identity).then_inc(pa_r[half], 1)

            def hnT_copy(m):
                act.wait_ge(pa_w[0], m * 5 + BASE + 1)
                nc.scalar.activation(hnT[:], PA[0][:], ACT.Identity).then_inc(pa_r[0], 1)

            def tap(m, g):
                b, k = (1 + g) % 2, (1 + g) // 2
                if not first(m):
                    at(act, s_feat, 4, m - 1, g + 1)
                if g == 0:
                    act.wait_ge(s_wa, layer_of[0] + 1)
                act.wait_ge(pa_w[b], m * 5 + k + BASE + 1)
                nc.scalar.activation(cv[g][:], PA[b][:], ACT.Identity, bias=pla[:, PCB + g:PCB + g + 1],
                                     scale=pla[:, PCW + 4 * g + 3:PCW + 4 * g + 4]).then_inc(s_acc, 1)

            def silus(m, p):
                for g in range(4):
                    b, k = (1 + g) % 2, (1 + g) // 2
                    act.wait_ge(pa_r[b], m * 5 + k + BASE + 1)
                    nc.scalar.activation(feat[p][g][:], cv[g][:], ACT.Silu).then_inc(s_feat, 1)
                for q in range(2):
                    b, k = (5 + q) % 2, (5 + q) // 2
                    act.wait_ge(pa_w[b], m * 5 + k + BASE + 1)
                    nc.scalar.activation(sz[p][:, q, :], PA[b][:], ACT.Silu).then_inc(pa_r[b], 1)

            def tail(m, p):
                act.wait_ge(pa_w[1], m * 5 + 5 + BASE)
                nc.scalar.activation(Btok[p][:].rearrange("p b n -> p (b n)"), PA[1][:, 0:2 * NS],
                                     ACT.Identity).then_inc(pa_r[1], 1)
                at(act, pg_w, 4, m, 1)
                nc.scalar.activation(Gs[p][:].rearrange("p c t -> p (c t)"), PG[:], ACT.Identity).then_inc(pg_r, 1)

            def expv(m):
                at(act, s_v, 1, m, 1)
                nc.scalar.activation(va[2][:], va[1][:], ACT.Exp, scale=-1.0).then_inc(s_e, 1)

            def expd(m):
                at(act, s_dtxd, 1, m, 0)
                at(act, s_diff, 1, m, 1)
                nc.scalar.activation(edec[:].rearrange("p c h -> p (c h)"), va[7][:], ACT.Exp).then_inc(s_edec, 1)

            def Eint(n):
                at(act, pd_w[0], 5, n, 2)
                nc.scalar.activation(Ei[:].rearrange("p b q t -> p (b q t)"), PDk[0][:], ACT.Exp).then_inc(pd_r[0], 1)

            def Scopy(n):
                at(act, pg_w, 4, n, 2)
                nc.scalar.activation(Ssb[:].rearrange("p b d -> p (b d)"), PG[:], ACT.Identity).then_inc(pg_r, 1)

            def E(n, i):
                c, q = i // 2, i % 2
                at(act, pd_w[q], 5 - q, n, pd_turn(i) + 1)
                at(act, s_y, 8, n, max(i - 1, 0) + FREE)
                nc.scalar.activation(eb[q][:].rearrange("p h t -> p (h t)"), PDk[q][:], ACT.Exp).then_inc(pd_r[q], 1)

            def square(n, p):
                yt = yts[p]
                at(act, s_g, 1, n, 1)
                nc.scalar.activation(gsq[:], yt[:], ACT.Square).then_inc(s_gsq, 1)

            layer_of = [0]
            hnT_copy(0)
            expv(0)
            for g in range(4):
                tap(0, g)
            expd(0)
            silus(0, 0)
            E(0, 0)
            E(0, 1)
            tail(0, 0)
            hnT_copy(1)

            def step(l, u, more=True, more2=True):
                n, p = l * UNITS + u, u % 2
                layer_of[0] = l + 1 if u == UNITS - 1 else l
                for i in range(8):
                    if i == 0:
                        Scopy(n)
                        Eint(n)
                    if i == 2 and not first(n):
                        square(n - 1, 1 - p)
                    if more:
                        if i == 1:
                            expv(n + 1)
                        if i in [1, 2, 3, 4]:
                            tap(n + 1, [1, 2, 3, 4].index(i))
                    if i < 6:
                        E(n, i + 2)
                if more:
                    expd(n + 1)
                    silus(n + 1, 1 - p)
                    E(n + 1, 0)
                    E(n + 1, 1)
                    tail(n + 1, 1 - p)
                if more2:
                    hnT_copy(n + 2)

            step(0, 0)
            with act.Fori(0, LAYERS - 1) as l:
                for u in range(1, UNITS):
                    step(l, u)
                step(l + 1, 0)
            for u in range(1, UNITS):
                step(LAYERS - 1, u, u < UNITS - 1, u < UNITS - 2)
            square(LAYERS * UNITS - 1, 1)

        @block.vector
        def _(v):
            V = nc.vector
            cA, cB, cP, cS = Chain(v, dchA, KA), Chain(v, dchB, KB), Chain(v, dchP, KP), Chain(v, dchS, 0)
            cS.start(0)
            for i in range(2):
                v.wait_ge(s_modps, i + 1)
                cS.link(V.tensor_copy(mod[i][:].rearrange("p j b -> p (j b)"), PY[i][:, 0:6 * BATCH]))
            for i in range(2):
                for j in (2, 5):
                    cS.link(V.tensor_scalar(gtmp[:, 0, :], mod[i][:, j, :], 0.0, 2.0, ALU.is_ge, ALU.mult))
                    cS.link(V.scalar_tensor_tensor(gtmp[:, 1, :], mod[i][:, j, :], -1.0, mod[i][:, j, :],
                                                   ALU.mult, ALU.max))
                    cS.link(V.tensor_scalar(gtmp[:, 1, :], gtmp[:, 1, :], 0.25, None, ALU.max))
                    cS.link(V.scalar_tensor_tensor(mod[i][:, j, :], gtmp[:, 0, :], -1.0, gtmp[:, 1, :],
                                                   ALU.add, ALU.mult))
            cS.link(V.tensor_scalar(modt[:, 0, :], mod[0][:, 1, :], 1.0, None, ALU.add))
            v.wait_ge(s_ld, 16 * LOADS)
            V.tensor_scalar(modt[:, 1, :], mod[0][:, 2, :], fnw[:, 0:1], None, ALU.mult).then_inc(s_mod, 1)

            v.wait_ge(s_const, 1)

            def layer_norm(k):
                for c in range(CHUNKS):
                    ins = V.bn_stats(bns[:, c, :], x_tok[:, c, :])
                cS.link(ins)
                for c in range(CHUNKS):
                    ins = V.bn_aggr(bna[:, c, :], bns[:, c, :])
                cS.link(ins)
                V.tensor_scalar(lnv[:], bna[:, :, 1], EPS, None, ALU.add).then_inc(s_h0, 1)
                v.wait_ge(s_h0, k + 2)
                for c in range(CHUNKS):
                    ins = V.tensor_scalar(lnt[:, c, :], x_tok[:, c, :], bna[:, c, 0:1], lnv[:, c:c + 1],
                                          ALU.subtract, ALU.mult)
                cS.link(ins)

            v.wait_ge(s_x, 16)
            layer_norm(0)
            v.wait_ge(pa_r[1], 2)
            v4 = lambda t: t[:].rearrange("p (b i) d -> p b i d", i=2)
            def brow(t, n=2):
                return t[:, :, None, :].to_broadcast([P, BATCH, n, DM])
            cS.link(V.tensor_tensor(v4(h_tok), v4(lnt), brow(bc[0]), ALU.mult))
            cS.link(V.tensor_tensor(v4(h_tok), v4(h_tok), brow(bc[1]), ALU.add))

            def fold_a(l):
                if not first(l):
                    v.wait_ge(pa_w[0], l * UNITS * 5 - 1 + BASE)
                    at(v, s_acc, 16, l, 0)
                V.tensor_copy(pla[:], par[:, l, :]).then_inc(s_par, 1)
                v.wait_ge(s_par, 2 * l + 2)
                V.tensor_scalar(wi[:], wi_all[:, l, :], pla[:, PBN:PBN + 1], None, ALU.mult).then_inc(s_wa, 1)

            def fold_b(l):
                V.tensor_copy(plb[:], par[:, l, :]).then_inc(s_par, 1)
                v.wait_ge(s_par, 2 * l + 3)
                for q in range(2):
                    ins = V.tensor_scalar(wo[:, q, :], wo_all[:, l, q, :], plb[:, PGW + q:PGW + q + 1], None, ALU.mult)
                ins.then_inc(s_wb, 1)
                v.wait_ge(s_wb, l + 1)

            def A1a(m, hs):
                cP.start(m)
                for c in range(UC):
                    ins = V.tensor_tensor_reduce(out=sq[:, c, :], in0=h_tok[:, hs + c, :], in1=h_tok[:, hs + c, :],
                                                 scale=1.0, scalar=0.0, op0=ALU.mult, op1=ALU.add,
                                                 accum_out=ss[:, c:c + 1])
                cP.link(ins)
                V.tensor_scalar(ms[:], ss[:], 1.0 / DM, EPS, ALU.mult, ALU.add).then_inc(s_ms, 1)

            def A1b(m, hs):
                if not first(m):
                    v.wait_ge(pa_w[0], m * 5 - 4 + BASE)
                at(v, s_rs, 1, m, 1)
                for c in range(UC):
                    ins = V.tensor_scalar(hn[:, c, :], h_tok[:, hs + c, :], rs[:, c:c + 1], None, ALU.mult)
                ins.then_inc(s_hn, 1)

            ch = lambda t: t.rearrange("p (c h) -> p c h", h=HEADS)

            def dt_bias_add(m):
                cA.start(m)
                at(v, pm_w, 3, m, 1)
                V.tensor_tensor(ch(va[0][:]), ch(PM[:, 0:UC * HEADS]),
                                pla[:, None, PDTB:PDTB + 8].to_broadcast([P, UC, HEADS]), ALU.add).then_inc(pm_r, 1)
                at(v, pm_r, 3, m, 1)
                V.scalar_tensor_tensor(va[1][:], va[0][:], -1.0, va[0][:], ALU.mult, ALU.max).then_inc(s_v, 1)

            def softplus(m):
                e, s, s2, p = va[2][:], va[4][:], va[5][:], va[6][:]
                at(v, s_e, 1, m, 1)
                cA.link(V.tensor_scalar(va[3][:], e, 2.0, None, ALU.add))
                cA.link(V.reciprocal(va[3][:], va[3][:]))
                cA.link(V.tensor_tensor(s, e, va[3][:], ALU.mult))
                cA.link(V.tensor_tensor(s2, s, s, ALU.mult))
                cA.link(V.tensor_scalar(p, s2, 1.0 / 15, None, ALU.mult))
                for k in (13, 11, 9, 7, 5, 3):
                    cA.link(V.scalar_tensor_tensor(p, p, 1.0 / k, s2, ALU.add, ALU.mult))
                cA.link(V.scalar_tensor_tensor(p, p, 1.0, s, ALU.add, ALU.mult))
                cA.link(V.tensor_scalar(va[0][:], va[0][:], 0.0, None, ALU.max))
                cA.link(V.scalar_tensor_tensor(dts[:].rearrange("p c h -> p (c h)"), p, 2.0, va[0][:],
                                               ALU.mult, ALU.add))
                V.scalar_tensor_tensor(ch(av[:]), dts[:], -1.0,
                                       pla[:, None, PA_:PA_ + 8].to_broadcast([P, UC, HEADS]),
                                       ALU.mult, ALU.mult).then_inc(s_a, 1)

            def split(m):
                at(v, pm_w, 3, m, 2)
                cA.link(V.tensor_copy(ct[:].rearrange("p k c -> p (k c)"), PM[:, 0:2 * UC * HEADS]))
                v.sem_inc(pm_r, 1)
                r = va[3][:]
                split3(V, cA.link, [cp[:, :, k * HEADS:(k + 1) * HEADS] for k in range(PARTS)], ch(ct[:, 0, :]),
                       ch(r)).then_inc(s_cp, 1)
                V.tensor_tensor(va[7][:], ct[:, 1, :], ct[:, 0, :], ALU.subtract).then_inc(s_diff, 1)

            def cT_copy(m, p):
                at(v, pm_w, 3, m, 3)
                V.tensor_copy(cTs[p][:], PM[:, 0:UNIT // 2].bitcast(BF16)).then_inc(pm_r, 1)

            def taps(m, g):
                b, k = (1 + g) % 2, (1 + g) // 2
                at(v, s_acc, 4, m, g + 1)
                src = PA[b][:].rearrange("p (b t) -> p b t", b=2)
                acc = cv[g][:].rearrange("p (b t) -> p b t", b=2)
                for s in (1, 2, 3):
                    j = PCW + 4 * g + 3 - s
                    ins = V.scalar_tensor_tensor(acc[:, :, s:], src[:, :, :SEQ - s], pla[:, j:j + 1], acc[:, :, s:],
                                                 ALU.mult, ALU.add)
                    if s < 3:
                        cA.link(ins)
                    else:
                        ins.then_inc(pa_r[b], 1)

            def dtx_(m, p):
                for j in range(2):
                    b, k = (7 + j) % 2, (7 + j) // 2
                    v.wait_ge(pa_w[b], m * 5 + k + BASE + 1)
                    V.tensor_tensor(dtx[p][:, 2 * j:2 * j + 2, :].rearrange("p c (h d) -> p (c h) d", h=HEADS),
                                    PA[b][:].rearrange("p (c d) -> p c d", d=HD),
                                    dts[:, 2 * j:2 * j + 2, :].rearrange("p c h -> p (c h)")[:, :, None]
                                    .to_broadcast([P, 2 * HEADS, HD]), ALU.mult).then_inc(pa_r[b], 1)
                cA.end()

            def M(n, p, i):
                c, q = i // 2, i % 2
                if i == 0:
                    at(v, pg_r, 4, n, 1)
                at(v, pd_r[q], 5 - q, n, pd_turn(i) + 1 + FREE)
                V.tensor_tensor(eb[q][:], eb[q][:], Gs[p][:, c, None, :].to_broadcast([P, 4, CHUNK]),
                                ALU.mult).then_inc(s_M, 1)

            def yinter(n):
                if not first(n):
                    at(v, s_yo, 1, n - 1, 1)
                at(v, pg_w, 4, n, 3)
                at(v, pd_r[0], 5, n, 2 + FREE)
                V.tensor_tensor(yi[:].rearrange("p b q t -> p (b q t)"), PG[:], Ei[:].rearrange("p b q t -> p (b q t)"),
                                ALU.mult).then_inc(pg_r, 1)

            def gate(n, p):
                yt = yts[p]
                """y with D x added; GpSimd goes on with it"""
                for q in range(2):
                    at(v, s_y, 8, n, 7 + q + FREE)
                    ins = V.scalar_tensor_tensor(yt[:, q, :], feat[p][q][:], plb[:, PD_ + q:PD_ + q + 1], PY[q][:],
                                                 ALU.mult, ALU.add)
                ins.then_inc(s_yt, 1)

            def meansq(n):
                at(v, s_ssq, 1, n, 1)
                V.tensor_scalar(ms2[:], PM[:, 0:UC], 1.0 / DI, EPS, ALU.mult, ALU.add).then_inc(s_ms2, 1)

            def residual(n, hs, turn):
                cB.start(n)
                at(v, s_rs2, 1, n, 1)
                v.wait_ge(pg_w, turn + 1)
                for c in range(UC):
                    ins = V.scalar_tensor_tensor(h_tok[:, hs + c, :], PG[:, c * P:(c + 1) * P], rs2[:, c:c + 1],
                                                 h_tok[:, hs + c, :], ALU.mult, ALU.add)
                cB.link(ins)
                v.sem_inc(pg_r, 1)
                cB.end()

            fold_a(0)
            A1a(0, 0)
            A1b(0, 0)
            A1a(1, UC)
            dt_bias_add(0)
            softplus(0)
            for g in range(4):
                taps(0, g)
            split(0)
            cT_copy(0, 0)
            dtx_(0, 0)
            fold_b(0)
            A1b(1, UC)

            def step(l, u, more=True, more2=True):
                n, p = l * UNITS + u, u % 2
                if more and u == UNITS - 1:
                    fold_a(l + 1)
                for i in range(8):
                    M(n, p, i)
                    if i == 1:
                        yinter(n)
                    if i == 5:
                        if first(n):
                            v.sem_inc(pg_r, 1)
                        else:
                            meansq(n - 1)
                    if more:
                        if i == 0:
                            dt_bias_add(n + 1)
                        if i == 1:
                            softplus(n + 1)
                        if i == 6:
                            split(n + 1)
                        if i in [2, 3, 4, 5]:
                            taps(n + 1, [2, 3, 4, 5].index(i))
                        if i == 7:
                            cT_copy(n + 1, 1 - p)
                    if more2:
                        if i == 0:
                            A1a(n + 2, (u + 2) % UNITS * UC)
                        if i == 2:
                            A1b(n + 2, (u + 2) % UNITS * UC)
                    if i == 6 and not first(n):
                        residual(n - 1, (u - 1) % UNITS * UC, n * 4 + 3)
                        if u == 0:
                            fold_b(l)
                gate(n, p)
                if more:
                    dtx_(n + 1, 1 - p)

            step(0, 0)
            with v.Fori(0, LAYERS - 1) as l:
                for u in range(1, UNITS):
                    step(l, u)
                step(l + 1, 0)
            for u in range(1, UNITS):
                step(LAYERS - 1, u, u < UNITS - 1, u < UNITS - 2)
            last = LAYERS * UNITS - 1
            meansq(last)
            residual(last, (UNITS - 1) * UC, (last + 1) * 4)

            cS.link(V.tensor_tensor(lnt[:], h_tok[:], h_tok[:], ALU.mult))
            cS.link(V.tensor_reduce(lnv[:], lnt[:], AX.X, ALU.add))
            v.wait_ge(s_h0, 2)
            cS.link(V.tensor_scalar(lnv[:], lnv[:], 1.0 / DM, EPS, ALU.mult, ALU.add))
            v.sem_inc(s_h0, 3)
            v.wait_ge(s_h0, 6)
            for c in range(CHUNKS):
                ins = V.scalar_tensor_tensor(lnt[:, c, :], h_tok[:, c, :], lnv[:, c:c + 1], bc[2][:, c // 2, :],
                                             ALU.mult, ALU.mult)
            cS.link(ins)
            V.tensor_tensor(x_tok[:], x_tok[:], lnt[:], ALU.add).then_inc(s_out, 1)
            v.wait_ge(s_out, 1)


class Norm:

    def __init__(self, nc, sb, sem, shared, mod, j, bk, w, r, per, tag, keep=False):
        self.keep, held = keep, CHUNKS if keep else UC
        self.nc, self.shared, self.mod, self.j = nc, shared, mod, j
        self.bk, self.w, self.r, self.per = bk, w, r, per
        self.bns, self.bna = sb(f"{tag}_bns", [P, held, 6]), sb(f"{tag}_bna", [P, held, 2])
        self.var, self.rstd = sb(f"{tag}_var", [P, held]), sb(f"{tag}_rstd", [P, held])
        self.xn, self.hT = sb(f"{tag}_xn", [P, UC, DM]), sb(f"{tag}_hT", [P, UNIT])
        self.modu = sb(f"{tag}_modu", [P, 2, BATCH if keep else 2])
        self.s_var, self.s_rstd, self.s_xn, self.s_mod = (sem(f"{tag}_{n}") for n in ("var", "rstd", "xn", "mod"))

    def vector(self, v, u, link):
        self.stats(v, u, link)
        self.scale(v, u)

    def stats(self, v, u, link, units=1):
        V, x, own = self.nc.vector, self.shared.x_tok, u * UC if self.keep else 0
        for c in range(units * UC):
            ins = V.bn_stats(self.bns[:, own + c, :], x[:, u * UC + c, :])
        link(ins)
        seqs = slice(2 * u, 2 * (u + units)) if self.keep else bass.ds(2 * u, 2)
        to = seqs if self.keep else slice(0, 2)
        V.tensor_scalar(self.modu[:, 0, to], self.mod[:, self.j + 1, seqs], 1.0, None, ALU.add)
        V.tensor_scalar(self.modu[:, 1, to], self.mod[:, self.j, seqs], 0.0, None, ALU.add).then_inc(self.s_mod, 1)
        for c in range(units * UC):
            ins = V.bn_aggr(self.bna[:, own + c, :], self.bns[:, own + c, :])
        link(ins)
        own = slice(own, own + units * UC)
        V.tensor_scalar(self.var[:, own], self.bna[:, own, 1], EPS, None, ALU.add).then_inc(self.s_var, 1)

    def scale(self, v, u, rstd_turn=None):
        V, x, own = self.nc.vector, self.shared.x_tok, u * UC if self.keep else 0
        v.wait_ge(self.s_rstd, u + 1 if rstd_turn is None else rstd_turn)
        for c in range(UC):
            ins = V.tensor_scalar(self.xn[:, c, :], x[:, u * UC + c, :], self.bna[:, own + c, 0:1],
                                  self.rstd[:, bass.ds(own + c, 1)], ALU.subtract, ALU.mult)
        ins.then_inc(self.s_xn, 1)

    def gpsimd(self, g, u, units=1, turn=None):
        g.wait_ge(self.s_var, u + 1 if turn is None else turn)
        own = slice(u * UC, (u + units) * UC) if self.keep else slice(0, UC)
        self.nc.gpsimd.tensor_tensor(self.rstd[:, own], self.var[:, own], self.shared.mhalf[:, 0:units * UC],
                                     ALU.pow).then_inc(self.s_rstd, 1)

    def tensor(self, pe, u, turn=None):
        pe.wait_ge(self.s_xn, u + 1)
        pe.wait_ge(self.r, (u * self.per if turn is None else turn) + FREE)
        for c in range(UC):
            ins = pe.transpose(self.bk[:, c * P:(c + 1) * P], self.xn[:, c, :], self.shared.ident[:])
        ins.then_inc(self.w, 1)

    def scalar(self, act, u, turn=None):
        act.wait_ge(self.s_mod, u + 1 if turn is None or first(u) else 2)
        act.wait_ge(self.w, (u * self.per if turn is None else turn) + 1)
        for b in range(2):
            own = bass.ds((2 * u if self.keep else 0) + b, 1)
            ins = self.nc.scalar.activation(self.hT[:, b * SEQ:(b + 1) * SEQ], self.bk[:, b * SEQ:(b + 1) * SEQ],
                                            ACT.Identity, bias=self.modu[:, 1, own], scale=self.modu[:, 0, own])
        ins.then_inc(self.r, 1)


def split3(V, link, parts, src, tmp):
    link(V.tensor_copy(parts[0], src))
    link(V.tensor_tensor(tmp, src, parts[0], ALU.subtract))
    link(V.tensor_copy(parts[1], tmp))
    return V.tensor_tensor(parts[2], tmp, parts[1], ALU.subtract)


def mixture(nc, ctx, bank, shared, mo, tag):
    sb, sem0 = allocators(nc, ctx)
    sem = lambda n: sem0(f"{tag}_{n}")
    PGate, PUp, PCo, PAcc, PM = bank[0:2], bank[2:4], bank[4:6], bank[6], bank[7]
    (s_var, s_rstd, s_xn, s_mod, s_xT, s_hT, s_lgw, s_mix, s_down, s_lg, s_ex, s_co, s_cow, s_coT, s_chain) = (
        sem(n) for n in "var rstd xn mod xT hT lgw mix down lg ex co cow coT chain".split())
    gate_w, gate_r = [sem("gate_w0"), sem("gate_w1")], [sem("gate_r0"), sem("gate_r1")]
    up_w, up_r = [sem("up_w0"), sem("up_w1")], [sem("up_r0"), sem("up_r1")]
    co_w, co_r = [sem("co_w0"), sem("co_w1")], [sem("co_r0"), sem("co_r1")]
    acc_r = sem("acc_r")
    G, R = mo.groups, mo.routed
    turns = [(G + 1) // 2, G // 2]
    cturns = [(R + 1) // 2, R // 2]
    bns, bna = sb(f"{tag}_bns", [P, CHUNKS, 6]), sb(f"{tag}_bna", [P, CHUNKS, 2])
    var, rstd = sb(f"{tag}_var", [P, CHUNKS]), sb(f"{tag}_rstd", [P, CHUNKS])
    xn, hT = sb(f"{tag}_xn", [P, CHUNKS, DM]), sb(f"{tag}_hT", [P, UNITS, UNIT])
    shift = sb(f"{tag}_shift", [P, 2, BATCH])
    lg = sb(f"{tag}_lg", [P, CHUNKS, EXPERTS])
    top = sb(f"{tag}_top", [P, CHUNKS, 8])
    idx = sb(f"{tag}_idx", [P, CHUNKS, 8], U32)
    idf = sb(f"{tag}_idf", [P, CHUNKS, 8])
    ex = sb(f"{tag}_ex", [P, CHUNKS, EXPERTS + 1])
    z, z2, z3 = (sb(f"{tag}_z{i}", [P, CHUNKS]) for i in range(3))
    wt = [sb(f"{tag}_wt{i}", [P, CHUNKS]) for i in range(2)]
    oh = [sb(f"{tag}_oh{i}", [P, CHUNKS, EXPERTS]) for i in range(2)]
    cop = sb(f"{tag}_cop", [P, CHUNKS, P], BF16)
    coT = sb(f"{tag}_coT", [P, UNITS, UNIT], BF16)
    sg = [sb(f"{tag}_sg{i}", [P, UNIT]) for i in range(2)]
    it = [sb(f"{tag}_it{i}", [P, UNIT]) for i in range(2)]
    res = sb(f"{tag}_res", [P, UC, DM])
    turned = (*PGate, *PUp)
    block = ctx.enter_context(nc.Block())

    @block.sync
    def _(sp):
        for free in (*gate_r, *up_r, *co_r, acc_r, s_down):
            sp.sem_inc(free, FREE)

    @block.gpsimd
    def _(g):
        nc.gpsimd.memset(cop[:].bitcast(F32), 0.0).then_inc(s_co, 1)
        g.wait_ge(s_var, 1)
        nc.gpsimd.tensor_tensor(rstd[:], var[:], shared.mhalf[:], ALU.pow).then_inc(s_rstd, 1)

    @block.tensor
    def _(pe):
        def gate_up(u, g):
            b = g % 2
            for bk, w, r, wt_ in ((PGate[b], gate_w[b], gate_r[b], mo.gate), (PUp[b], up_w[b], up_r[b], mo.up)):
                pe.wait_ge(r, u * turns[b] + g // 2 + FREE)
                pe.matmul(bk[:], wt_[:, g, :], hT[:, u, :], start=True, stop=True).then_inc(w, 1)

        def coefficients(u, g):
            b = g % 2
            pe.wait_ge(co_r[b], u * cturns[b] + g // 2 + FREE)
            pe.matmul(PCo[b][:], mo.sel[:, g, :], coT[:, u, :], start=True, stop=True).then_inc(co_w[b], 1)

        def down(u, g):
            pe.wait_ge(s_mix, u * G + g + 1)
            if g == 0:
                pe.wait_ge(acc_r, u + FREE)
            for c in range(UC):
                ins = pe.matmul(PAcc[:, c * P:(c + 1) * P], it[g % 2][:, c * P:(c + 1) * P], mo.down[:, g, :],
                                start=(g == 0 and c == 0), stop=(g == G - 1), skip_group_check=True)
            ins.then_inc(s_down, 1)

        for u in range(UNITS):
            pe.wait_ge(s_xn, u + 1)
            for c in range(UC):
                ins = pe.transpose(turned[u][:, c * P:(c + 1) * P], xn[:, u * UC + c, :], shared.ident[:])
            ins.then_inc(s_xT, 1)
        for u in range(UNITS):
            pe.wait_ge(s_hT, u + 1)
            for c in range(UC):
                k = u * UC + c
                ins = pe.matmul(PM[:, k * EXPERTS:(k + 1) * EXPERTS], hT[:, u, c * P:(c + 1) * P], mo.router[:],
                                start=True, stop=True)
        ins.then_inc(s_lgw, 1)
        gate_up(0, 0)
        gate_up(0, 1)
        pe.wait_ge(s_co, 2)
        for k in range(CHUNKS):
            half = PCo[k // 8][:].bitcast(BF16)
            ins = pe.transpose(half[:, k % 8 * P:(k % 8 + 1) * P], cop[:, k, :], shared.identb[:])
            if k % 8 == 7:
                ins.then_inc(s_cow, 1)
        pe.wait_ge(s_coT, 2)

        def experts(u, last):
            for g in range(G):
                if g < R:
                    coefficients(u, g)
                if g >= 1:
                    down(u, g - 1)
                if g >= 1 and g + 1 < G:
                    gate_up(u, g + 1)
            if not last:
                gate_up(u + 1, 0)
            down(u, G - 1)
            if not last:
                gate_up(u + 1, 1)

        with pe.Fori(0, UNITS - 1) as u:
            experts(u, False)
        experts(UNITS - 1, True)

    @block.scalar
    def _(act):
        act.wait_ge(s_mod, 1)
        for u in range(UNITS):
            act.wait_ge(s_xT, u + 1)
            for b in range(2):
                s = 2 * u + b
                ins = nc.scalar.activation(hT[:, u, b * SEQ:(b + 1) * SEQ], turned[u][:, b * SEQ:(b + 1) * SEQ],
                                           ACT.Identity, bias=shift[:, 1, s:s + 1], scale=shift[:, 0, s:s + 1])
            ins.then_inc(s_hT, 1)
        act.wait_ge(s_lg, 1)
        nc.scalar.activation(ex[:], ex[:], ACT.Exp).then_inc(s_ex, 1)
        with act.Fori(0, UNITS) as u:
            for g in range(G):
                b = g % 2
                act.wait_ge(gate_w[b], u * turns[b] + g // 2 + 1)
                act.wait_ge(up_r[b], u * turns[b] + g // 2 + FREE)
                nc.scalar.activation(sg[b][:], PGate[b][:], ACT.Silu).then_inc(gate_r[b], 1)

    @block.vector
    def _(v):
        V = nc.vector
        first_links = 2 + 15 + (4 if mo.norm else 0)
        ch = Chain(v, s_chain, first_links)
        link = ch.link
        ch.start(0)
        for c in range(CHUNKS):
            ins = V.bn_stats(bns[:, c, :], shared.x_tok[:, c, :])
        link(ins)
        V.tensor_scalar(shift[:, 0, :], mo.mod[:, 4, :], 1.0, None, ALU.add)
        V.tensor_scalar(shift[:, 1, :], mo.mod[:, 3, :], 0.0, None, ALU.add).then_inc(s_mod, 1)
        for c in range(CHUNKS):
            ins = V.bn_aggr(bna[:, c, :], bns[:, c, :])
        link(ins)
        V.tensor_scalar(var[:], bna[:, :, 1], EPS, None, ALU.add).then_inc(s_var, 1)
        v.wait_ge(s_rstd, 1)
        for c in range(CHUNKS):
            ins = V.tensor_scalar(xn[:, c, :], shared.x_tok[:, c, :], bna[:, c, 0:1], rstd[:, c:c + 1],
                                  ALU.subtract, ALU.mult)
            if c % UC == UC - 1:
                ins.then_inc(s_xn, 1)
        v.wait_ge(shared.s_w2, 16 * shared.late)
        v.wait_ge(s_lgw, 1)
        link(V.tensor_copy(lg[:].rearrange("p c e -> p (c e)"), PM[:, 0:CHUNKS * EXPERTS]))
        for c in range(CHUNKS):
            ins = V.max(top[:, c, :], lg[:, c, :])
        link(ins)
        V.tensor_tensor(ex[:, :, EXPERTS], top[:, :, 1], top[:, :, 0], ALU.subtract)
        V.tensor_tensor(ex[:, :, 0:EXPERTS], lg[:], top[:, :, 0:1].to_broadcast([P, CHUNKS, EXPERTS]),
                        ALU.subtract).then_inc(s_lg, 1)
        for c in range(CHUNKS):
            ins = V.max_index(idx[:, c, :], top[:, c, :], lg[:, c, :])
        link(ins)
        link(V.tensor_copy(idf[:], idx[:]))
        for k in range(2):
            link(V.tensor_tensor(oh[k][:], shared.iota[:, None, :].to_broadcast([P, CHUNKS, EXPERTS]),
                                 idf[:, :, k:k + 1].to_broadcast([P, CHUNKS, EXPERTS]), ALU.is_equal))
        v.wait_ge(s_ex, 1)
        link(V.tensor_reduce(z[:], ex[:, :, 0:EXPERTS], AX.X, ALU.add))
        link(V.reciprocal(wt[0][:], z[:]))
        link(V.tensor_tensor(wt[1][:], wt[0][:], ex[:, :, EXPERTS], ALU.mult))
        if mo.norm:
            link(V.scalar_tensor_tensor(z2[:], wt[0][:], 1e-9, wt[1][:], ALU.add, ALU.add))
            link(V.reciprocal(z3[:], z2[:]))
            for k in range(2):
                link(V.tensor_tensor(wt[k][:], wt[k][:], z3[:], ALU.mult))
        for k in range(2):
            link(V.tensor_tensor(oh[k][:], oh[k][:], wt[k][:, :, None].to_broadcast([P, CHUNKS, EXPERTS]), ALU.mult))
        link(V.tensor_tensor(oh[0][:], oh[0][:], oh[1][:], ALU.add))
        v.wait_ge(s_co, 1)
        split3(V, link, [cop[:, :, k * EXPERTS:(k + 1) * EXPERTS] for k in range(PARTS)],
               oh[0][:], oh[1][:]).then_inc(s_co, 1)
        for k in range(2):
            v.wait_ge(s_cow, k + 1)
            V.tensor_copy(coT[:, 2 * k:2 * k + 2, :].rearrange("p u t -> p (u t)"),
                          PCo[k][:].bitcast(BF16)).then_inc(s_coT, 1)
        ch.end()
        ch = Chain(v, s_chain, R + 1, first_links)
        link = ch.link
        with v.Fori(0, UNITS) as u:
            ch.start(u)
            for g in range(G):
                b = g % 2
                v.wait_ge(up_w[b], u * turns[b] + g // 2 + 1)
                v.wait_ge(gate_r[b], u * turns[b] + g // 2 + 1 + FREE)
                v.wait_ge(s_down, u * G + max(g - 1, 0) + FREE)
                V.tensor_tensor(it[b][:], sg[b][:], PUp[b][:], ALU.mult).then_inc(up_r[b], 1)
                v.wait_ge(up_r[b], u * turns[b] + g // 2 + 1 + FREE)
                if g < R:
                    v.wait_ge(co_w[b], u * cturns[b] + g // 2 + 1)
                    link(V.tensor_tensor(it[b][:], it[b][:], PCo[b][:], ALU.mult))
                    v.sem_inc(co_r[b], 1)
                v.sem_inc(s_mix, 1)
            residual(v, V, link, u, shared, mo.gate_bc, res, PAcc, s_down, (u + 1) * G + FREE, acc_r, u + 1)
            ch.end()


def residual(v, V, link, u, shared, gate_bc, res, bk, s_done, value, r, r_value, bias=None):
    v.wait_ge(s_done, value)
    acc = bk[:].rearrange("p (c d) -> p c d", d=DM)
    if bias is not None:
        link(V.tensor_tensor(res[:], acc, bias[:, None, :].to_broadcast([P, UC, DM]), ALU.add))
        acc = res[:]
    for b in range(2):
        ins = V.tensor_tensor(res[:, 2 * b:2 * b + 2, :], acc[:, 2 * b:2 * b + 2, :],
                              gate_bc[:, 2 * u + b, None, :].to_broadcast([P, 2, DM]), ALU.mult)
    ins.then_inc(r, 1)
    v.wait_ge(r, r_value + FREE)
    x = shared.x_tok[:, bass.ds(u * UC, UC), :]
    link(V.tensor_tensor(x, x, res[:], ALU.add))


def attention(nc, ctx, bank, shared):
    sb, sem = allocators(nc, ctx)
    PS, PT, PO, PX, PZ = bank[0:2], bank[2:4], bank[4:6], bank[6], bank[7]
    ps_w, ps_r = [sem("ps_w0"), sem("ps_w1")], [sem("ps_r0"), sem("ps_r1")]
    pt_w, pt_r = [sem("pt_w0"), sem("pt_w1")], [sem("pt_r0"), sem("pt_r1")]
    px_w, px_r, pz_w, pz_r = sem("px_w"), sem("px_r"), sem("pz_w"), sem("pz_r")
    po_r = [sem("po_r0"), sem("po_r1")]
    s_zero, s_par, s_vn, s_vp, s_mp, s_pv, s_on, s_qs, s_ks, s_chain, s_gchain = (
        sem(f"at_{n}") for n in "zero par vn vp mp pv on qs ks chain gchain".split())
    s_st = [sem("at_st0"), sem("at_st1")]
    LEADX, XT = 4, 12
    SCALE = float(AD) ** -0.5
    GH = 8
    QH = 4
    SEQG = AH // GH
    SLOTS_Q, SLOTS_K = (0, 0, 0, 1, 1, 2), (0, 1, 2, 0, 1, 0)
    LOADS = 16 * len(SLOTS_Q)
    ROWS = 96
    norm = Norm(nc, sb, sem, shared, shared.mod[1], 0, PX, px_w, px_r, XT, "at", keep=True)
    hT = norm.hT
    wq = sb("wq", [P, 2, DM])
    qk = [sb("qT", [P, UNIT]), sb("kT", [P, UNIT])]
    parts = sb("parts", [P, 2 * PARTS, UNIT], BF16)
    zero = sb("zero", [P, SEQ])
    rest = [sb("qrest", [P, SEQ]), sb("krest", [P, SEQ])]
    stack = [sb(f"stack{b}", [P, AH, 2, SEQ], BF16) for b in range(2)]
    bq = sb("bq", [P, 1])
    Vn = sb("Vn", [P, UC, DM])
    Vp = sb("Vp", [P, UC, AH, 32])
    mx = sb("mx", [P, 2, QH])
    mt = sb("mt", [P, 2, QH])
    mp = sb("mp", [P, 2, P], BF16)
    mT = [sb(f"mT{i}", [P, SEQ], BF16) for i in range(2)]
    Pt = [sb(f"Pt{i}", [P, 2, SEQ]) for i in range(GH)]
    OT = sb("OT", [P, 4, SEQ])
    rec = sb("rec", [P, AH])
    on = sb("on", [P, 2, DM])
    oT = sb("oT", [P, SEQ])
    res = sb("at_res", [P, 2, DM])
    block = ctx.enter_context(nc.Block())

    def turn(eng, g, h):
        i = g * GH + h
        return i, i % 2, i // 2

    @block.sync
    def _(sp):
        for free in (*ps_r, *pt_r, *po_r, px_r, pz_r):
            sp.sem_inc(free, FREE)
        sp.wait_ge(s_zero, 2)

        def stacks(n, b):
            sp.wait_ge(s_qs, 2 * n + b + 1)
            sp.wait_ge(s_ks, 2 * n + b + 1)
            for s, (q, k) in enumerate(zip(SLOTS_Q, SLOTS_K)):
                two = slice(q, PARTS + k + 1, PARTS + k - q)
                sp.dma_start(stack[b][AD * s:AD * s + AD, :, :, :],
                             parts[:, two, b * SEQ:(b + 1) * SEQ]).then_inc(s_st[b], 16)

        for b in range(2):
            stacks(0, b)
        with sp.Fori(0, UNITS - 1) as u:
            for b in range(2):
                stacks(u + 1, b)

    @block.gpsimd
    def _(g):
        def split_k(n, b, link):
            G, s = nc.gpsimd, slice(b * SEQ, (b + 1) * SEQ)
            k, (p0, p1, p2), r = qk[1][:, s], (parts[:, PARTS + j, s] for j in range(PARTS)), rest[1][:]
            link(G.tensor_tensor(p0, k, zero[:], ALU.add))
            link(G.tensor_tensor(r, k, p0, ALU.subtract))
            link(G.tensor_tensor(p1, r, zero[:], ALU.add))
            return G.tensor_tensor(p2, r, p1, ALU.subtract)

        def values(b):
            for c in range(2 * b, 2 * b + 2):
                v = Vn[:, c, :].rearrange("p (h d) -> p h d", d=AD)
                ins = nc.gpsimd.tensor_tensor(Vp[:, c, :, 0:AD], v, zero[:, 0:DM].rearrange("p (h d) -> p h d", d=AD),
                                              ALU.add)
            ins.then_inc(s_vp, 1)

        nc.gpsimd.memset(zero[:], 0.0)
        norm.gpsimd(g, 0)
        norm.gpsimd(g, 1, UNITS - 1, 2)
        nc.gpsimd.memset(stack[1][:].bitcast(F32), 0.0).then_inc(s_zero, 1)
        ch = Chain(g, s_gchain, 2 * 4)
        ch.start(0)
        for b in range(2):
            g.wait_ge(px_r, 3 + FREE)
            ch.link(split_k(0, b, ch.link))
            g.sem_inc(s_ks, 1)
        for b in range(2):
            g.wait_ge(s_vn, 1)
            values(b)
        ch.end()
        with g.Fori(0, UNITS - 1) as u:
            ch.start(u + 1)
            for b in range(2):
                g.wait_ge(px_r, LEADX + u * XT + 3 + FREE)
                g.wait_ge(s_st[b], (u + 1) * LOADS)
                ch.link(split_k(u + 1, b, ch.link))
                g.wait_ge(pt_w[1], u * AH + (b + 1) * GH)
                g.sem_inc(s_ks, 1)
                g.wait_ge(s_vn, u + 2)
                g.wait_ge(s_pv, u * 8 + 4 * (b + 1))
                values(b)
            ch.end()

    @block.tensor
    def _(pe):
        def scores(n, g, h):
            i, bk, before = turn(pe, g, h)
            b, head = g // SEQG, i % AH
            if h == 0:
                pe.wait_ge(s_st[b], (n + 1) * LOADS)
            pe.wait_ge(ps_r[bk], n * AH + before + FREE)
            for c in range(2):
                ins = pe.matmul(PS[bk][:, c * SEQ:(c + 1) * SEQ], stack[b][0:ROWS, head, 0, c * P:(c + 1) * P],
                                stack[b][0:ROWS, head, 1, :], start=True, stop=True)
            ins.then_inc(ps_w[bk], 1)

        def maxima(n, g, q):
            quad = n * 8 + 2 * g + q
            pe.wait_ge(s_mp, quad + 1)
            pe.wait_ge(pz_r, quad + FREE)
            dst = PZ[:, 0:P].bitcast(BF16)
            for c in range(2):
                ins = pe.transpose(dst[:, c * P:(c + 1) * P], mp[:, c, :], shared.identb[:])
            ins.then_inc(pz_w, 1)

        def scores_T(n, g, h):
            i, bk, before = turn(pe, g, h)
            b, head = g // SEQG, i % AH
            if h % QH == 0:
                pe.wait_ge(pz_r, n * 8 + 2 * g + h // QH + 1 + FREE)
            pe.wait_ge(pt_r[bk], n * AH + before + FREE)
            for c in range(2):
                half = slice(c * SEQ, (c + 1) * SEQ)
                pe.matmul(PT[bk][:, half], shared.selm[0:ROWS, h % QH, :], mT[h // QH][0:ROWS, :],
                          start=True, stop=False)
                ins = pe.matmul(PT[bk][:, half], stack[b][0:ROWS, head, 1, c * P:(c + 1) * P],
                                stack[b][0:ROWS, head, 0, :], start=False, stop=True)
            ins.then_inc(pt_w[bk], 1)

        def weigh(n, g, q):
            b, k, i = g // SEQG, g % SEQG, g * GH + q * QH
            for bk in range(2):
                pe.wait_ge(pt_r[bk], n * AH + i // 2 + 2 + FREE)
            if q == 0:
                pe.wait_ge(s_vp, 2 * n + b + 1)
                pe.wait_ge(po_r[k], 2 * n + b + FREE)
            for c in range(2):
                for r in range(QH):
                    ins = pe.matmul(PO[k][32 * r:32 * r + 32, q * SEQ:(q + 1) * SEQ],
                                    Vp[:, 2 * b + c, k * GH + q * QH + r, :], Pt[q * QH + r][:, c, :],
                                    start=(c == 0), stop=(c == 1))
            ins.then_inc(s_pv, 1)

        def turn_o(n, b, c, x):
            if c == 0:
                for k in range(2):
                    pe.wait_ge(po_r[k], 2 * n + b + 1 + FREE)
            pe.wait_ge(px_r, x + c + FREE)
            for q in range(4):
                ins = pe.transpose(PX[:, q * P:(q + 1) * P], OT[:, q, c * P:(c + 1) * P], shared.ident[:])
            ins.then_inc(px_w, 1)

        def turn_on(n, b):
            pe.wait_ge(s_on, (2 * n + b) * 2 + 2)
            for c in range(2):
                ins = pe.transpose(PX[:, c * P:(c + 1) * P], on[:, c, :], shared.ident[:])
            ins.then_inc(px_w, 1)

        def proj(x):
            pe.wait_ge(px_r, x + 3 + FREE)
            for c in range(2):
                ins = pe.matmul(PX[:, c * DM:(c + 1) * DM], oT[:, c * P:(c + 1) * P], shared.wproj[:],
                                start=True, stop=True)
            ins.then_inc(px_w, 1)

        def project(x, k):
            pe.wait_ge(px_r, x + 1 + k + FREE)
            if k < 2:
                pe.matmul(PX[:], wq[:, k, :], hT[:], start=True, stop=True).then_inc(px_w, 1)
            else:
                for c in range(UC):
                    ins = pe.matmul(PX[:, c * DM:(c + 1) * DM], hT[:, c * P:(c + 1) * P],
                                    shared.wqkv[:, 2 * DM:3 * DM], start=True, stop=True)
                ins.then_inc(px_w, 1)

        def segment(n, g, nn, gg, x, before, out=None, more=True):
            for h in range(GH):
                scores_T(n, g, h)
                if gg is not None:
                    scores(nn, gg, h)
                if h == 1 and before is not None:
                    weigh(*before, 1)
                elif h == 2:
                    maxima(n, g, 1)
                elif h == 5:
                    weigh(n, g, 0)
                elif h == 6 and gg is not None:
                    maxima(nn, gg, 0)
                if g == 1 and more:
                    if h == 2:
                        norm.tensor(pe, n + 1, x)
                    elif h in (4, 6):
                        project(x, (h - 4) // 2)
                if g == 2 and more and h == 0:
                    project(x - 4, 2)
                if out is not None:
                    if h in (2, 4):
                        turn_o(*out, h // 2 - 1, x)
                    elif h == 6:
                        turn_on(*out)
            if out is not None:
                proj(x)

        norm.tensor(pe, 0, 0)
        pe.wait_ge(s_par, 1)
        for k in range(3):
            project(0, k)
        for h in range(GH):
            scores(0, 0, h)
            if h == 5:
                maxima(0, 0, 0)
        segment(0, 0, 0, 1, 0, None)
        with pe.Fori(0, UNITS - 1) as u:
            x = u * XT + LEADX
            segment(u, 1, u, 2, x, (u, 0))
            segment(u, 2, u, 3, x + 4, (u, 1), (u, 0))
            segment(u, 3, u + 1, 0, x, (u, 2))
            segment(u + 1, 0, u + 1, 1, x + 8, (u, 3), (u, 1))
        u, x = UNITS - 1, (UNITS - 1) * XT + LEADX
        segment(u, 1, u, 2, x, (u, 0), more=False)
        segment(u, 2, u, 3, x, (u, 1), (u, 0), more=False)
        segment(u, 3, u, None, x, (u, 2), more=False)
        weigh(u, 3, 1)
        for c in range(2):
            turn_o(u, 1, c, x + 4)
        turn_on(u, 1)
        proj(x + 4)

    @block.scalar
    def _(act):
        def evacuate(x, k):
            bias, scale = ((bq[:, 0:1], SCALE), (shared.bqk[:, 1:2], 1.0))[k]
            act.wait_ge(px_w, x + 2 + k)
            nc.scalar.activation(qk[k][:], PX[:], ACT.Identity, bias=bias, scale=scale).then_inc(px_r, 1)

        def sums(n, g, after):
            k = g % SEQG
            act.wait_ge(s_pv, n * 8 + 2 * g + 2)
            if after is not None:
                act.wait_ge(px_w, after)
            nc.scalar.activation(OT[:, 2 * k:2 * k + 2, :].rearrange("p g t -> p (g t)"), PO[k][:],
                                 ACT.Identity).then_inc(po_r[k], 1)

        def turned(x):
            act.wait_ge(px_w, x + 3)
            nc.scalar.activation(oT[:], PX[:, 0:SEQ], ACT.Identity).then_inc(px_r, 1)

        def segment(n, g, x, before=None, after=None, out=None, more=True):
            for h in range(GH):
                i, bk, earlier = turn(act, g, h)
                act.wait_ge(pt_w[bk], n * AH + earlier + 1)
                if before is not None and h % QH == 0:
                    act.wait_ge(s_pv, n * 8 + i // QH - 1)
                nc.scalar.activation(Pt[h][:].rearrange("p c t -> p (c t)"), PT[bk][:],
                                     ACT.Exp).then_inc(pt_r[bk], 1)
                if h == 1 and before is not None:
                    sums(*before, after)
                if out is not None and h == 7:
                    turned(x)
                if g == 1 and more:
                    if h == 3:
                        norm.scalar(act, n + 1, x)
                    elif h in (5, 7):
                        if h == 5:
                            act.wait_ge(s_qs, 2 * n + 2)
                            act.wait_ge(s_ks, 2 * n + 2)
                        evacuate(x, (h - 5) // 2)

        act.wait_ge(s_par, 1)
        norm.scalar(act, 0, 0)
        for k in range(2):
            evacuate(0, k)
        segment(0, 0, 0)
        with act.Fori(0, UNITS - 1) as u:
            x = u * XT + LEADX
            segment(u, 1, x, (u, 0), x)
            segment(u, 2, x + 4, (u, 1), None, (u, 0))
            segment(u, 3, x, (u, 2), x + 6)
            segment(u + 1, 0, x + 8, (u, 3), None, (u, 1))
        u, x = UNITS - 1, (UNITS - 1) * XT + LEADX
        segment(u, 1, x, (u, 0), x, more=False)
        segment(u, 2, x, (u, 1), None, (u, 0), more=False)
        segment(u, 3, x, (u, 2), x + 2, more=False)
        sums(u, 3, None)
        turned(x + 4)

    @block.vector
    def _(v):
        V = nc.vector

        def split_q(b, link):
            s = slice(b * SEQ, (b + 1) * SEQ)
            link(split3(V, link, [parts[:, j, s] for j in range(PARTS)], qk[0][:, s], rest[0][:]))

        def release_q(n, b):
            v.wait_ge(pt_w[1], (n - 1) * AH + (b + 1) * GH)
            v.sem_inc(s_qs, 1)

        def reduce(n, g, h):
            i, bk, before = turn(v, g, h)
            v.wait_ge(ps_w[bk], n * AH + before + 1)
            return V.tensor_reduce(mx[:, :, h % QH], PS[bk][:].rearrange("p (c t) -> p c t", c=2), AX.X,
                                   ALU.max).then_inc(ps_r[bk], 1)

        def maxima(n, g, q, link):
            v.wait_ge(ps_r[1], n * AH + (g * GH + (q + 1) * QH) // 2 + FREE)
            if not (g == 0 and q == 0 and isinstance(n, int)):
                v.wait_ge(pz_w, n * 8 + 2 * g + q)
            split3(V, link, [mp[:, :, k * QH:(k + 1) * QH] for k in range(PARTS)], mx[:], mt[:]).then_inc(s_mp, 1)

        def maxima_T(n, g, q):
            v.wait_ge(pz_w, n * 8 + 2 * g + q + 1)
            V.tensor_copy(mT[q][:], PZ[:, 0:P].bitcast(BF16)).then_inc(pz_r, 1)

        def add_bias(x):
            v.wait_ge(px_w, x + 4)
            V.tensor_tensor(Vn[:], PX[:].rearrange("p (c d) -> p c d", d=DM),
                            shared.bv[:, None, :].to_broadcast([P, UC, DM]), ALU.add).then_inc(px_r, 1)
            v.wait_ge(px_r, x + 4 + FREE)
            v.sem_inc(s_vn, 1)

        def normalise(n, b, c, x, link):
            o = PX[:].rearrange("p (h d) -> p h d", d=32)
            v.wait_ge(px_w, x + c + 1)
            link(V.reciprocal(rec[:], o[:, :, AD]))
            V.tensor_tensor(on[:, c, :].rearrange("p (h d) -> p h d", d=AD), o[:, :, 0:AD],
                            rec[:, :, None].to_broadcast([P, AH, AD]), ALU.mult).then_inc(px_r, 1)
            v.wait_ge(px_r, x + c + 1 + FREE)
            v.sem_inc(s_on, 1)

        def add(n, b, x, link):
            v.wait_ge(px_w, x + 4)
            V.tensor_tensor(res[:], PX[:, 0:SEQ].rearrange("p (c d) -> p c d", d=DM),
                            shared.bp[:, None, :].to_broadcast([P, 2, DM]), ALU.add).then_inc(px_r, 1)
            v.wait_ge(px_r, x + 4 + FREE)
            link(V.tensor_tensor(res[:], res[:], shared.bc[4][:, 2 * n + b, None, :].to_broadcast([P, 2, DM]),
                                 ALU.mult))
            xs = shared.x_tok[:, bass.ds(n * UC + 2 * b, 2), :]
            link(V.tensor_tensor(xs, xs, res[:], ALU.add))

        def segment(n, g, nn, gg, x, link, out=None, more=False):
            for h in range(GH):
                if gg is not None:
                    reduce(nn, gg, h)
                    if h % QH == QH - 1:
                        maxima(nn, gg, h // QH, link)
                if h == 2:
                    maxima_T(n, g, 1)
                elif h == 6 and gg is not None:
                    maxima_T(nn, gg, 0)
                if out is not None:
                    if h in (2, 4):
                        normalise(*out, h // 2 - 1, x, link)
                    elif h == 7:
                        add(*out, x, link)
                if more:
                    if g == 1 and h == 0:
                        norm.scale(v, n + 1, 2)
                    elif g == 1 and h == 7:
                        v.wait_ge(px_r, x + 2 + FREE)
                        v.wait_ge(s_st[0], (n + 1) * LOADS)
                        split_q(0, link)
                        release_q(n + 1, 0)
                    elif g == 2 and h == 0:
                        v.wait_ge(s_vp, 2 * n + 2)
                        add_bias(x - 4)
                    elif g == 3 and h == 6:
                        v.wait_ge(s_st[1], (n + 1) * LOADS)
                        split_q(1, link)
                    elif g == 0 and h == 0:
                        release_q(n, 1)

        LEAD, BODY = 2 * LN_LINKS + 4 * 2 + 3 * 4, 4 * 2 + 3 * 8 + 2 * 4
        for k in range(2):
            V.tensor_copy(wq[:, k, :].rearrange("p (c h) -> p c h", c=AD),
                          shared.wqkv[:, k * DM:(k + 1) * DM].rearrange("p (h c) -> p c h", c=AD))
        V.tensor_scalar(bq[:], shared.bqk[:, 0:1], SCALE, None, ALU.mult).then_inc(s_par, 1)
        V.memset(mp[:], 0.0)
        V.memset(Vp[:], 0.0)
        ch = Chain(v, s_chain, LEAD)
        ch.start(0)
        norm.stats(v, 0, ch.link)
        V.memset(stack[0][:].bitcast(F32), 0.0).then_inc(s_zero, 1)
        V.memset(Vp[:, :, :, AD], 1.0)
        norm.scale(v, 0)
        norm.stats(v, 1, ch.link, UNITS - 1)
        v.wait_ge(px_r, 2 + FREE)
        for b in range(2):
            split_q(b, ch.link)
            v.sem_inc(s_qs, 1)
        add_bias(0)
        for h in range(GH):
            reduce(0, 0, h)
            if h % QH == QH - 1:
                maxima(0, 0, h // QH, ch.link)
            if h == 5:
                maxima_T(0, 0, 0)
        segment(0, 0, 0, 1, 0, ch.link)
        ch.end()
        ch = Chain(v, s_chain, BODY, LEAD)
        with v.Fori(0, UNITS - 1) as u:
            x = u * XT + LEADX
            ch.start(u)
            segment(u, 1, u, 2, x, ch.link, more=True)
            segment(u, 2, u, 3, x + 4, ch.link, (u, 0), more=True)
            segment(u, 3, u + 1, 0, x, ch.link, more=True)
            segment(u + 1, 0, u + 1, 1, x + 8, ch.link, (u, 1), more=True)
            ch.end()
        u, x = UNITS - 1, (UNITS - 1) * XT + LEADX
        ch.start(u)
        segment(u, 1, u, 2, x, ch.link)
        segment(u, 2, u, 3, x, ch.link, (u, 0))
        segment(u, 3, u, None, x, ch.link)
        for c in range(2):
            normalise(u, 1, c, x + 4, ch.link)
        add(u, 1, x + 4, ch.link)


def store(nc, ctx, shared, out):
    s_out = ctx.enter_context(nc.semaphore("s_store"))
    block = ctx.enter_context(nc.Block())

    @block.sync
    def _(sp):
        sp.dma_start(out.rearrange("b (i p) d -> p (b i) d", p=P), shared.x_tok[:]).then_inc(s_out, 16)
        sp.wait_ge(s_out, 16)


LN_LINKS = 2

def first(m):
    return isinstance(m, int) and m == 0


KA, KB, KP = 14 + 4 + 8, 1, 1


class Chain:

    def __init__(self, eng, sem, per, base=0):
        self.eng, self.sem, self.per, self.base = eng, sem, per, base

    def start(self, n):
        self.n, self.k = n, 0

    def link(self, ins):
        self.k += 1
        ins.then_inc(self.sem, 1)
        self.eng.wait_ge(self.sem, self.n * self.per + self.base + self.k)

    def end(self):
        assert self.k == self.per, self.k


_INS = {"x": "L0_attn_x", "W_in": "L0_attn_W_in", "conv_w": "L0_attn_conv_w", "conv_b": "L0_attn_conv_b",
        "dt_bias": "L0_attn_dt_bias", "A_log": "L0_attn_A_log", "D": "L0_attn_D",
        "gate_norm_w": "L0_attn_gate_norm_w", "W_out": "L0_attn_W_out", "block_norm_w": "L0_attn_block_norm_w",
        "final_norm_w": "L0_attn_final_norm_w", "c0": "L0_c", "wmod0": "L0_wmod", "c1": "L1_c", "wmod1": "L1_wmod"}


_INS.update({
    "router0": "L0_ffn_router_w", "gate0": "L0_ffn_gate_w", "up0": "L0_ffn_up_w", "down0": "L0_ffn_down_w",
    "sgate0": "L0_ffn_shared_gate_w", "sup0": "L0_ffn_shared_up_w", "sdown0": "L0_ffn_shared_down_w",
    "w_qkv": "L1_attn_w_qkv", "b_qkv": "L1_attn_b_qkv", "w_proj": "L1_attn_w_proj", "b_proj": "L1_attn_b_proj",
    "router1": "L1_ffn_router_w", "gate1": "L1_ffn_wg_r", "up1": "L1_ffn_wu_r", "down1": "L1_ffn_wd_r",
    "sgate1": "L1_ffn_wg_s", "sup1": "L1_ffn_wu_s", "sdown1": "L1_ffn_wd_s"})


def kernel(**inputs):
    import numpy as np
    import concourse.bacc as bacc
    from concourse.bass_utils import run_bass_kernel_spmd

    nc = bacc.Bacc("TRN2", target_bir_lowering=False, num_devices=1)
    arrays, args = {}, {}
    for arg, name in _INS.items():
        a = np.ascontiguousarray(inputs[name])
        arrays[f"in_{arg}"] = a
        args[arg] = nc.dram_tensor(f"in_{arg}", a.shape, mybir.dt.from_np(a.dtype), kind="ExternalInput").ap()
    args["out"] = nc.dram_tensor("out_x", (BATCH, SEQ, DM), F32, kind="ExternalOutput").ap()
    program(nc, **args)
    r = run_bass_kernel_spmd(nc, [arrays], core_ids=[0])
    return r.results[0]["out_x"]
```

```python
from contextlib import ExitStack

import concourse.bass as bass
from concourse import mybir

P = 128
F32 = mybir.dt.float32
BF16 = mybir.dt.bfloat16
U32 = mybir.dt.uint32
ALU = mybir.AluOpType
ACT = mybir.ActivationFunctionType
AX = mybir.AxisListType

BATCH, SEQ, DM = 8, 256, 128
CHUNK = 128
CHUNKS = BATCH * SEQ // CHUNK
UNIT = 512
UC = UNIT // CHUNK
UNITS = BATCH * SEQ // UNIT
LAYERS = 4
DI, HEADS, HD, NS = 256, 8, 32, 128
ZOFF, XOFF, DTOFF, DPROJ = 0, DI, 2 * DI + 2 * NS, 2 * DI + 2 * NS + HEADS
EXPERTS, AH, AD = 16, 16, 8
PARTS = 3
EPS = 1e-5
GTAPS = (3,)
VTAPS = tuple(g for g in range(4) if g not in GTAPS)
PCW, PCB, PGW, PBN, PD_, PDTB, PA_, PLEN = 0, 16, 20, 22, 23, 25, 33, 41
FREE = 1


def program(nc, x, W_in, conv_w, conv_b, dt_bias, A_log, D, gate_norm_w, W_out, block_norm_w, final_norm_w,
            c0, wmod0, c1, wmod1, router0, gate0, up0, down0, sgate0, sup0, sdown0, w_qkv, b_qkv, w_proj, b_proj,
            router1, gate1, up1, down1, sgate1, sup1, sdown1, out):
    with ExitStack() as whole:
        sb, sem = allocators(nc, whole)
        bank = [whole.enter_context(nc.psum_tensor(f"bank{i}", [P, 512], F32)) for i in range(8)]
        shared = Shared(sb, sem)
        with ExitStack() as ctx:
            mamba(nc, ctx, bank, shared, x, W_in, conv_w, conv_b, dt_bias, A_log, D, gate_norm_w, W_out,
                  block_norm_w, final_norm_w, c0, wmod0, c1, wmod1,
                  (router0, gate0, up0, down0, sgate0, sup0, sdown0, w_qkv, b_qkv, w_proj, b_proj,
                   router1, gate1, up1, down1, sgate1, sup1, sdown1))
        with ExitStack() as ctx_pr:
            pr = Projections(nc, *allocators(nc, ctx_pr), shared)
            with ExitStack() as ctx:
                mixture(nc, ctx, bank, shared, shared.moe0, "f0", True, pr)
            with ExitStack() as ctx:
                attention(nc, ctx, bank, shared, pr)
        with ExitStack() as ctx:
            mixture(nc, ctx, bank, shared, shared.moe1, "f1", False)
        with ExitStack() as ctx:
            store(nc, ctx, shared, out)


def allocators(nc, ctx):
    def sb(name, shape, dt=F32):
        return ctx.enter_context(nc.sbuf_tensor(name, shape, dt))

    def sem(name):
        return ctx.enter_context(nc.semaphore(name))

    return sb, sem


class Moe:

    def __init__(self, sb, name, f, norm, mod, gate_bc):
        self.f, self.norm, self.mod, self.gate_bc = f, norm, mod, gate_bc
        self.per = P // f
        self.routed = EXPERTS // self.per
        self.groups = self.routed + 1
        self.router = sb(f"{name}_router", [P, EXPERTS])
        self.gate = sb(f"{name}_gate", [P, self.groups, P])
        self.up = sb(f"{name}_up", [P, self.groups, P])
        self.down = sb(f"{name}_down", [P, self.groups, DM])
        self.sel = sb(f"{name}_sel", [P, self.routed, P], BF16)


class Shared:

    def __init__(self, sb, sem):
        self.ident = sb("ident", [P, P])
        self.identb = sb("identb", [P, P], BF16)
        self.mhalf = sb("mhalf", [P, CHUNKS])
        self.iota = sb("iota", [P, EXPERTS])
        self.x_tok = sb("x_tok", [P, CHUNKS, DM])
        self.mod = [sb(f"mod{i}", [P, 6, BATCH]) for i in range(2)]
        self.bc = [sb(f"bc{i}", [P, BATCH, DM]) for i in range(6)]
        self.moe0 = Moe(sb, "moe0", 64, False, self.mod[0], self.bc[3])
        self.moe1 = Moe(sb, "moe1", 32, True, self.mod[1], self.bc[5])
        self.wqkv = sb("wqkv", [P, 3 * DM])
        self.wproj = sb("wproj", [P, DM])
        self.bqk = sb("bqk", [P, 2])
        self.bv = sb("bv", [P, DM])
        self.bp = sb("bp", [P, DM])
        self.selm = sb("selm", [P, AH // 4, P], BF16)
        self.bns = sb("bns_next", [P, CHUNKS, 6])
        self.s_w2 = sem("s_w2")


def mamba(nc, ctx, bank, shared, x, W_in, conv_w, conv_b, dt_bias, A_log, D, gate_norm_w, W_out, block_norm_w,
          final_norm_w, c0, wmod0, c1, wmod1, later):
    XPROJ_AT, TAP_AT, VTAPS_AT = (1, 2, 3, 4), (1, 2, 3, 4), (2, 3, 4, 6)
    sb, sem = allocators(nc, ctx)
    PA, PDk, PG, PM, PY = bank[0:2], bank[2:4], bank[4], bank[5], bank[6:8]

    ident, identb, mhalf, x_tok, mod, bc = (shared.ident, shared.identb, shared.mhalf, shared.x_tok, shared.mod,
                                            shared.bc)
    ones = sb("ones", [P, P])
    triu = sb("triu", [P, P])
    maskneg = sb("maskneg", [P, 4, CHUNK], BF16)
    selh = sb("selh", [P, HEADS, P], BF16)
    negsel = sb("negsel", [P, HEADS, P], BF16)
    selq = sb("selq", [P, 2, P], BF16)

    wi_all = sb("wi_all", [P, LAYERS, DPROJ])
    wo_all = sb("wo_all", [P, LAYERS, 2, DM])
    par = sb("par", [P, LAYERS, PLEN])
    fnw = sb("fnw", [P, 1])
    cT = [sb(f"cT{i}", [P, BATCH]) for i in range(2)]
    wmod = [sb(f"wmod{i}", [P, 6, P]) for i in range(2)]
    wi = sb("wi", [P, DPROJ])
    wo = sb("wo", [P, 2, DM])
    pla = sb("pla", [P, PLEN])
    plb = sb("plb", [P, PLEN])

    h_tok = sb("h_tok", [P, CHUNKS, DM])
    modt = sb("modt", [P, 2, BATCH])

    sq = sb("sq", [P, UC, DM])
    ss = sb("ss", [P, UC])
    ms = sb("ms", [P, UC])
    rs = sb("rs", [P, UC])
    hn = sb("hn", [P, UC, DM])
    hnT = sb("hnT", [P, UNIT])
    cv = [sb(f"cv{g}", [P, UNIT]) for g in range(4)]
    prod = [[sb(f"prod{i}_{k}", [P, UNIT]) for k in range(3)] for i in range(len(GTAPS))]
    feat = [[sb(f"feat{p}_{g}", [P, UNIT]) for g in range(4)] for p in range(2)]
    sz = [sb(f"sz{p}", [P, 2, UNIT]) for p in range(2)]
    va = [sb(f"va{i}", [P, UC * HEADS]) for i in range(8)]
    dts = sb("dts", [P, UC, HEADS])
    av = sb("av", [P, UC * HEADS])
    ct = sb("ct", [P, 2, UC * HEADS])
    cp = sb("cp", [P, UC, P], BF16)
    edec = sb("edec", [P, UC, HEADS])
    cTs = [sb(f"cTs{p}", [P, UNIT], BF16) for p in range(2)]
    dtx = [sb(f"dtx{p}", [P, UC, DI]) for p in range(2)]
    dtxd = [sb(f"dtxd{p}", [P, 2, DI]) for p in range(2)]
    Btok = [sb(f"Btok{p}", [P, 2, NS]) for p in range(2)]
    Gs = [sb(f"Gs{p}", [P, UC, CHUNK]) for p in range(2)]
    Ssb = sb("Ssb", [P, 2, DI])
    Ei = sb("Ei", [P, 2, 2, CHUNK])
    yi = sb("yi", [P, 2, 2, CHUNK])
    eb = [sb(f"eb{i}", [P, 4, CHUNK]) for i in range(2)]
    yts = [sb(f"yt{p}", [P, 2, UNIT]) for p in range(2)]
    gsq = sb("gsq", [P, 2, UNIT])
    ms2 = sb("ms2", [P, UC])
    rs2 = sb("rs2", [P, UC])

    pa_w, pa_r = [sem("pa_w0"), sem("pa_w1")], [sem("pa_r0"), sem("pa_r1")]
    pd_w, pd_r = [sem("pd_w0"), sem("pd_w1")], [sem("pd_r0"), sem("pd_r1")]
    pg_w, pg_r = sem("pg_w"), sem("pg_r")
    pm_w, pm_r = sem("pm_w"), sem("pm_r")
    s_lc, s_x, s_ld, s_setup, s_const, s_mod, s_modps, s_h0, s_par, s_wa, s_wb = (
        sem(f"s_{n}") for n in "lc x ld setup const mod modps h0 par wa wb".split())
    s_ms, s_rs, s_hn, s_acc, s_gt, s_feat, s_v, s_e, s_a, s_cp, s_diff, s_edec, s_dtxd = (
        sem(f"s_{n}") for n in "ms rs hn acc gt feat v e a cp diff edec dtxd".split())
    s_M, s_y = sem("s_M"), sem("s_y")
    s_yt, s_yo, s_g, s_gsq, s_ssq, s_ms2, s_rs2, s_fin, s_finr = (
        sem(f"s_{n}") for n in "yt yo g gsq ssq ms2 rs2 fin finr".split())
    dchA, dchB, dchP, dchS, dchG = (sem(f"dch{n}") for n in "ABPSG")
    BASE = 6

    def pd_turn(i):
        c, q = i // 2, i % 2
        return c if q == 1 or c == 0 else c + 1

    def at(eng, s, per, n, m):
        eng.wait_ge(s, n * per + m)

    lnv = sb("lnv", [P, CHUNKS])
    fs, fr = sb("fs", [P, CHUNKS]), sb("fr", [P, CHUNKS])
    bns = sb("bns", [P, CHUNKS, 6])
    bna = sb("bna", [P, CHUNKS, 2])
    lnt = sb("lnt", [P, CHUNKS, DM])
    gtmp = sb("gtmp", [P, 4, BATCH])

    def bcsrc(j):
        return (modt[:, 0, :], mod[0][:, 0, :], modt[:, 1, :], mod[0][:, 5, :], mod[1][:, 2, :], mod[1][:, 5, :])[j]

    LOADS_C = 5
    LOADS = 2 + 4 + 7 + 2 + HEADS

    ctx.enter_context(nc.allow_non_contiguous_dma(reason="a few small vectors, laid over partitions"))
    block = ctx.enter_context(nc.Block())

    @block.sync
    def _(sp):
        for free in (*pd_r, s_y):
            sp.sem_inc(free, FREE)
        for t, w, c_, w_ in ((cT[0], wmod[0], c0, wmod0), (cT[1], wmod[1], c1, wmod1)):
            sp.dma_start(t[:], c_.rearrange("b k -> k b")).then_inc(s_lc, 16)
            sp.dma_start(w[:], w_.rearrange("k (j d) -> k j d", j=6)).then_inc(s_lc, 16)
        sp.dma_start(fnw[:], final_norm_w.rearrange("(p o) -> p o", o=1)).then_inc(s_lc, 16)
        sp.dma_start(x_tok[:], x.rearrange("b (i p) d -> p (b i) d", p=P)).then_inc(s_x, 16)
        sp.dma_start(wi_all[:], W_in.rearrange("l k n -> k l n")).then_inc(s_ld, 16)
        for g in range(4):
            sp.dma_start(par[:, :, PCW + 4 * g:PCW + 4 * g + 4],
                         conv_w[:, g * P:(g + 1) * P, :].rearrange("l p k -> p l k")).then_inc(s_ld, 16)
        for t, k, src in ((PCB, 4, conv_b), (PGW, 2, gate_norm_w), (PBN, 1, block_norm_w)):
            for g in range(k):
                sp.dma_start(par[:, :, t + g], src[:, g * P:(g + 1) * P].rearrange("l p -> p l")).then_inc(s_ld, 16)
        sp.dma_start(par[:, :, PDTB:PDTB + 8], dt_bias.partition_broadcast(P)).then_inc(s_ld, 16)
        sp.dma_start(par[:, :, PA_:PA_ + 8], A_log.partition_broadcast(P)).then_inc(s_ld, 16)
        for h in range(HEADS):
            sp.dma_start(par[32 * (h % 4):32 * (h % 4) + 32, :, PD_ + h // 4],
                         D[:, h].partition_broadcast(32)).then_inc(s_ld, 16)
        sp.dma_start(wo_all[:].rearrange("p l q d -> p (l q) d"),
                     W_out.rearrange("l (q p) d -> p (l q) d", q=2)).then_inc(s_ld, 16)
        (router0, gate0, up0, down0, sgate0, sup0, sdown0, w_qkv, b_qkv, w_proj, b_proj,
         router1, gate1, up1, down1, sgate1, sup1, sdown1) = later
        m0, m1, r0, r1 = shared.moe0, shared.moe1, shared.moe0.routed, shared.moe1.routed
        late = [
            (m0.router[:], router0), (m1.router[:], router1),
            (m0.gate[:, 0:r0, :].rearrange("p g (e f) -> p (g e) f", f=m0.f), gate0.rearrange("e h f -> h e f")),
            (m0.up[:, 0:r0, :].rearrange("p g (e f) -> p (g e) f", f=m0.f), up0.rearrange("e h f -> h e f")),
            (m0.down[:, 0:r0, :], down0.rearrange("(g e) f d -> (e f) g d", g=r0)),
            (m0.gate[:, r0, :], sgate0), (m0.up[:, r0, :], sup0), (m0.down[:, r0, :], sdown0),
            (shared.wqkv[:], w_qkv), (shared.wproj[:], w_proj),
            *((shared.bqk[AH * c:AH * c + AH, :], b_qkv[0:2 * DM].rearrange("(k h c) -> c h k", k=2, c=AD)[c])
              for c in range(AD)),
            (shared.bv[:], b_qkv[2 * DM:3 * DM].partition_broadcast(P)),
            (shared.bp[:], b_proj.partition_broadcast(P)),
            (m1.gate[:, 0:r1, :].rearrange("p g (e f) -> p (g e) f", f=m1.f), gate1.rearrange("e h f -> h e f")),
            (m1.up[:, 0:r1, :].rearrange("p g (e f) -> p (g e) f", f=m1.f), up1.rearrange("e h f -> h e f")),
            (m1.down[:, 0:r1, :], down1.rearrange("(g e) f d -> (e f) g d", g=r1)),
            (m1.gate[:, r1, :].rearrange("p (n f) -> p n f", n=2), sgate1.rearrange("n h f -> h n f")),
            (m1.up[:, r1, :].rearrange("p (n f) -> p n f", n=2), sup1.rearrange("n h f -> h n f")),
            (m1.down[:, r1, :], sdown1.rearrange("n f d -> (n f) d")),
        ]
        shared.late = len(late)
        for dst, src in late:
            sp.dma_start(dst, src).then_inc(shared.s_w2, 16)
        sp.wait_ge(shared.s_w2, 16 * len(late))

    @block.gpsimd
    def _(g):
        def select(t, fill, base, pattern, op=ALU.not_equal, step=1):
            return nc.gpsimd.affine_select(out=t[:], in_=t[:], compare_op=op, fill=fill, base=base,
                                           pattern=pattern, channel_multiplier=step)

        for t, v in ((mhalf, -0.5), (ident, 0.0), (identb, 0.0)):
            last = nc.gpsimd.memset(t[:], v)
        last.then_inc(s_setup, 1)
        g.wait_ge(s_setup, 1)
        for t in (ident, identb):
            last = select(t, 1.0, 0, [[-1, P]])
        last.then_inc(s_const, 1)
        g.wait_ge(s_h0, 1)
        nc.gpsimd.tensor_tensor(lnv[:], lnv[:], mhalf[:], ALU.pow).then_inc(s_h0, 1)
        for t, v in ((ones, 1.0), (triu, 1.0), (maskneg, 0.0), (selh, 0.0), (selq, 0.0), (cp, 0.0)):
            last = nc.gpsimd.memset(t[:], v)
        last.then_inc(s_setup, 1)
        g.wait_ge(s_setup, 2)
        select(triu, 0.0, 0, [[1, P]], ALU.is_ge, -1)
        select(maskneg, -1e30, 0, [[0, 4], [1, CHUNK]], ALU.is_ge, -1)
        for k in range(PARTS):
            select(selh, 1.0, -HEADS * k, [[-1, HEADS], [0, P]])
            select(selq, 1.0, -HEADS * k, [[-4, 2], [-1, 4], [0, HD]]).then_inc(s_setup, 1)
            g.wait_ge(s_setup, 3 + k)
        nc.gpsimd.tensor_scalar(negsel[:], selh[:], -1.0, 0.0, ALU.mult, ALU.add).then_inc(s_const, 1)

        def later_constants():
            for t in (shared.moe0.sel, shared.moe1.sel, shared.selm):
                last = nc.gpsimd.memset(t[:], 0.0)
            last.then_inc(s_setup, 1)
            g.wait_ge(s_setup, 6)
            for k in range(PARTS):
                for mo in (shared.moe0, shared.moe1):
                    select(mo.sel, 1.0, -EXPERTS * k, [[-mo.per, mo.routed], [-1, mo.per], [0, mo.f]])
                select(shared.selm, -1.0, -(AH // 4) * k, [[-1, AH // 4], [0, P]]).then_inc(s_setup, 1)
                g.wait_ge(s_setup, 7 + k)
            nc.gpsimd.iota(shared.iota[:], pattern=[[1, EXPERTS]], base=0, channel_multiplier=0,
                           allow_small_or_imprecise_dtypes=True)

        def A(m):
            at(g, s_ms, 1, m, 1)
            nc.gpsimd.tensor_tensor(rs[:], ms[:], mhalf[:, 0:UC], ALU.pow).then_inc(s_rs, 1)

        def A2(m, p):
            g.wait_ge(pa_r[0], m * 5 + BASE + 5)
            at(g, s_edec, 1, m, 1)
            src = dtx[p][:].rearrange("p (b i) (h d) -> p b i h d", i=2, h=HEADS)[:, :, 0]
            dst = dtxd[p][:].rearrange("p b (h d) -> p b h d", h=HEADS)
            e = edec[:].rearrange("p (b i) h -> p b i h", i=2)[:, :, 0]
            for b in range(2):
                ins = nc.gpsimd.tensor_tensor(dst[:, b], src[:, b], e[:, b, :, None].to_broadcast([P, HEADS, HD]),
                                              ALU.mult)
            ins.then_inc(s_dtxd, 1)

        def taps(m, k):
            group = GTAPS[k]
            b, acc = (1 + group) % 2, cv[group][:].rearrange("p (b t) -> p b t", b=2)
            g.wait_ge(pa_r[b], m * 5 + (1 + group) // 2 + BASE + 1)
            for s in (1, 2, 3):
                t = prod[k][s - 1][:].rearrange("p (b t) -> p b t", b=2)
                ins = nc.gpsimd.tensor_tensor(acc[:, :, s:], acc[:, :, s:], t[:, :, :SEQ - s], ALU.add)
                if s < 3:
                    cG.link(ins)
                else:
                    ins.then_inc(s_gt, 1)

        def all_taps(m):
            cG.start(m)
            for k in range(len(GTAPS)):
                taps(m, k)
            cG.end()

        def gate(n, p):
            yt = yts[p]
            at(g, s_yt, 1, n, 1)
            odd = yt[:].rearrange("p q (b i t) -> p q b i t", b=2, i=2)[:, :, :, 1, :]
            nc.gpsimd.tensor_tensor(odd, odd, yi[:].rearrange("p b q t -> p q b t"), ALU.add).then_inc(s_yo, 1)
            at(g, s_yo, 1, n, 1)
            g.wait_ge(pa_r[0], n * 5 + 4 + BASE)
            nc.gpsimd.tensor_tensor(yt[:], yt[:], sz[p][:], ALU.mult).then_inc(s_g, 1)

        def C(n):
            at(g, s_ms2, 1, n, 1)
            nc.gpsimd.tensor_tensor(rs2[:], ms2[:], mhalf[:, 0:UC], ALU.pow).then_inc(s_rs2, 1)

        def step(n, p, more=True, more2=True):
            if more2:
                A(n + 2)
            if not first(n):
                C(n - 1)
            if more:
                all_taps(n + 1)
            gate(n, p)
            if more:
                A2(n + 1, 1 - p)

        def finish(k):
            own = slice(k * UC, k * UC + UC)
            g.wait_ge(s_fin, k + 1)
            nc.gpsimd.tensor_tensor(fr[:, own], fs[:, own], mhalf[:, 0:UC], ALU.pow).then_inc(s_finr, 1)

        cG = Chain(g, dchG, 2 * len(GTAPS))
        A(0)
        all_taps(0)
        A(1)
        A2(0, 0)
        step(0, 0)
        later_constants()
        with g.Fori(0, LAYERS - 1) as l:
            for u in range(1, UNITS + 1):
                step(l * UNITS + u, u % 2)
        for u in range(1, UNITS):
            step((LAYERS - 1) * UNITS + u, u % 2, u < UNITS - 1, u < UNITS - 2)
            if u < UNITS - 1:
                finish(u - 1)
        finish(UNITS - 2)
        C(LAYERS * UNITS - 1)
        finish(UNITS - 1)

    @block.tensor
    def _(pe):
        pe.wait_ge(s_mod, 1)
        for i in range(2):
            for j in range(6):
                ins = pe.matmul(PY[i][:, j * BATCH:(j + 1) * BATCH], wmod[i][:, j, :], cT[i][:],
                                start=True, stop=True)
            ins.then_inc(s_modps, 1)
        pe.wait_ge(s_const, 1)
        pe.wait_ge(s_mod, 2)
        for j in range(6):
            for half in range(2):
                k = 2 * j + half
                if k >= 2:
                    pe.wait_ge(pa_r[half], j)
                for b in range(4):
                    src = bcsrc(j)[:, 4 * half + b:4 * half + b + 1]
                    ins = pe.matmul(PA[half][:, b * DM:(b + 1) * DM], src.to_broadcast([P, P]), ident[:],
                                    start=True, stop=True)
                ins.then_inc(pa_w[half], 1)

        def pa_turn(m, k):
            b = k % 2
            pe.wait_ge(pa_r[b], m * 5 + k // 2 + BASE)
            return PA[b], pa_w[b]

        def A1(m):
            bk, w = pa_turn(m, 0)
            at(pe, s_hn, 1, m, 1)
            for c in range(UC):
                ins = pe.transpose(bk[:, c * P:(c + 1) * P], hn[:, c, :], ident[:])
            ins.then_inc(w, 1)

        def dt(m):
            pe.wait_ge(pa_r[0], m * 5 + BASE + 1)
            at(pe, pm_r, 3, m, 0)
            for c in range(UC):
                ins = pe.matmul(PM[:, c * HEADS:(c + 1) * HEADS], hnT[:, c * P:(c + 1) * P],
                                wi[:, DTOFF:DPROJ], start=True, stop=True)
            ins.then_inc(pm_w, 1)

        def proj(m, k, off):
            bk, w = pa_turn(m, k)
            pe.matmul(bk[:], wi[:, off:off + P], hnT[:], start=True, stop=True).then_inc(w, 1)

        def xproj(m, g):
            proj(m, 1 + g, XOFF + g * P)

        def zproj(m, q):
            proj(m, 5 + q, ZOFF + q * P)

        def cum(m):
            if first(m):
                pe.wait_ge(s_const, 2)
            at(pe, s_a, 1, m, 1)
            at(pe, pm_r, 3, m, 1)
            if not (isinstance(m, int) and m < 2):
                at(pe, s_ms2, 1, m - 2, 1)
            pe.matmul(PM[:, 0:UC * HEADS], triu[:], av[:], start=True, stop=True)
            pe.matmul(PM[:, UC * HEADS:2 * UC * HEADS], ones[:], av[:], start=True, stop=True).then_inc(pm_w, 1)

        def cTr(m):
            at(pe, s_cp, 1, m, 1)
            at(pe, pm_r, 3, m, 2)
            dst = PM[:, 0:UNIT // 2].bitcast(BF16)
            for c in range(UC):
                ins = pe.transpose(dst[:, c * P:(c + 1) * P], cp[:, c, :], identb[:])
            ins.then_inc(pm_w, 1)

        def A3(m, p):
            f = feat[p]
            at(pe, s_feat, 4, m, 4)
            for j in range(2):
                bk, w = pa_turn(m, 7 + j)
                for i in range(2):
                    for q in range(2):
                        c = 2 * j + i
                        ins = pe.transpose(bk[:, i * DI + q * P:i * DI + (q + 1) * P],
                                           f[q][:, c * P:(c + 1) * P], ident[:])
                ins.then_inc(w, 1)
            bk, w = pa_turn(m, 9)
            for b in range(2):
                ins = pe.transpose(bk[:, b * P:(b + 1) * P], f[2][:, 2 * b * P:(2 * b + 1) * P], ident[:])
            ins.then_inc(w, 1)
            at(pe, pg_r, 4, m, 0)
            for c in range(UC):
                cs = slice(c * P, (c + 1) * P)
                ins = pe.matmul(PG[:, cs], f[2][:, cs], f[3][:, cs], start=True, stop=True)
            ins.then_inc(pg_w, 1)

        def S(n, p):
            pe.wait_ge(pa_r[1], n * 5 + BASE + 5)
            at(pe, s_dtxd, 1, n, 1)
            at(pe, pg_r, 4, n, 1)
            for b in range(2):
                ins = pe.matmul(PG[:, b * DI:(b + 1) * DI], Btok[p][:, b, :], dtxd[p][:, b, :],
                                start=True, stop=True)
            ins.then_inc(pg_w, 1)

        def inter(n, p):
            at(pe, pg_r, 4, n, 2)
            for b in range(2):
                cs = slice((2 * b + 1) * P, (2 * b + 2) * P)
                for q in range(2):
                    k = 2 * b + q
                    ins = pe.matmul(PG[:, k * P:(k + 1) * P], Ssb[:, b, q * P:(q + 1) * P], feat[p][3][:, cs],
                                    start=True, stop=True)
            ins.then_inc(pg_w, 1)

        def Einter(n, p):
            at(pe, pd_r[0], 5, n, 1 + FREE)
            for b in range(2):
                cs = slice((2 * b + 1) * P, (2 * b + 2) * P)
                for q in range(2):
                    k = 2 * b + q
                    ins = pe.matmul(PDk[0][:, k * P:(k + 1) * P], selq[:, q, :], cTs[p][:, cs],
                                    start=True, stop=True)
            ins.then_inc(pd_w[0], 1)

        def decay(n, p, i):
            c, q = i // 2, i % 2
            cs = slice(c * P, (c + 1) * P)
            if i == 0:
                at(pe, pm_r, 3, n, 3)
            at(pe, pd_r[q], 5 - q, n, pd_turn(i) + FREE)
            bk = PDk[q]
            pe.matmul(bk[:], identb[:], maskneg[:].rearrange("p h t -> p (h t)"), start=True, stop=False)
            for r in range(4):
                pe.matmul(bk[:, r * P:(r + 1) * P], selh[:, 4 * q + r, :], cTs[p][:, cs],
                          start=False, stop=False, skip_group_check=True)
            ins = pe.matmul(bk[:], cTs[p][:, cs], negsel[:, 4 * q:4 * q + 4, :].rearrange("k h t -> k (h t)"),
                            start=False, stop=True)
            ins.then_inc(pd_w[q], 1)

        def y(n, p, i):
            c, q = i // 2, i % 2
            at(pe, s_M, 8, n, i + 1)
            if i == 0 and not first(n):
                at(pe, s_yt, 1, n - 1, 1)
            for r in range(4):
                h = 4 * q + r
                ins = pe.matmul(PY[q][32 * r:32 * r + 32, c * P:(c + 1) * P],
                                dtx[p][:, c, h * HD:(h + 1) * HD], eb[q][:, r, :], start=True, stop=True)
            ins.then_inc(s_y, 1)

        def outp(n, p, l, turn):
            yt = yts[p]
            at(pe, s_g, 1, n, 1)
            pe.wait_ge(pg_r, turn)
            at(pe, s_wb, 1, l, 1)
            for c in range(UC):
                cs = slice(c * P, (c + 1) * P)
                for q in range(2):
                    ins = pe.matmul(PG[:, cs], yt[:, q, cs], wo[:, q, :], start=(q == 0), stop=(q == 1))
            ins.then_inc(pg_w, 1)

        def sumsq(n, turn):
            at(pe, s_gsq, 1, n, 1)
            pe.wait_ge(pm_r, turn)
            for c in range(UC):
                cs = slice(c * P, (c + 1) * P)
                for q in range(2):
                    ins = pe.matmul(PM[:, c:c + 1], gsq[:, q, cs], ones[:, 0:1],
                                    start=(q == 0), stop=(q == 1))
            ins.then_inc(s_ssq, 1)

        pe.wait_ge(s_wa, 1)
        A1(0)
        dt(0)
        for g in range(4):
            xproj(0, g)
        cum(0)
        cTr(0)
        zproj(0, 0)
        zproj(0, 1)
        decay(0, 0, 0)
        decay(0, 0, 1)
        A3(0, 0)
        A1(1)

        def step(l, u, more=True, more2=True):
            n, p = l * UNITS + u, u % 2
            for i in range(8):
                if i == 0:
                    Einter(n, p)
                    if more:
                        if u == UNITS - 1:
                            pe.wait_ge(s_wa, l + 2)
                        dt(n + 1)
                if i == 0:
                    S(n, p)
                if i == 1:
                    inter(n, p)
                if i == 3:
                    if first(n):
                        pe.wait_ge(pg_r, 3)
                        pe.sem_inc(pg_w, 1)
                    else:
                        outp(n - 1, 1 - p, l if u > 0 else l - 1, n * 4 + 3)
                if i == 2 and not first(n):
                    sumsq(n - 1, (n + 1) * 3 + 1 if more else n * 3 + 3)
                if more:
                    if i in XPROJ_AT:
                        xproj(n + 1, XPROJ_AT.index(i))
                    if i == 5:
                        cum(n + 1)
                    if i == 6:
                        zproj(n + 1, 0)
                    if i == 7:
                        cTr(n + 1)
                    if i == 6:
                        zproj(n + 1, 1)
                y(n, p, i)
                if i < 6:
                    decay(n, p, i + 2)
            if more:
                decay(n + 1, 1 - p, 0)
                decay(n + 1, 1 - p, 1)
                A3(n + 1, 1 - p)
            if more2:
                A1(n + 2)

        step(0, 0)
        with pe.Fori(0, LAYERS - 1) as l:
            for u in range(1, UNITS):
                step(l, u)
            step(l + 1, 0)
        for u in range(1, UNITS):
            step(LAYERS - 1, u, u < UNITS - 1, u < UNITS - 2)
        outp(LAYERS * UNITS - 1, 1, LAYERS - 1, LAYERS * UNITS * 4)
        pe.wait_ge(s_ms2, LAYERS * UNITS - 1)
        sumsq(LAYERS * UNITS - 1, LAYERS * UNITS * 3)

    @block.scalar
    def _(act):
        act.wait_ge(s_lc, 16 * LOADS_C)
        for i in range(2):
            ins = nc.scalar.activation(cT[i][:], cT[i][:], ACT.Silu)
        ins.then_inc(s_mod, 1)
        act.wait_ge(s_ld, 16 * LOADS)
        nc.scalar.activation(par[:, :, PA_:PA_ + 8], par[:, :, PA_:PA_ + 8], ACT.Exp).then_inc(s_par, 1)
        for k in range(12):
            half = k % 2
            act.wait_ge(pa_w[half], k // 2 + 1)
            nc.scalar.activation(bc[k // 2][:, 4 * half:4 * half + 4, :].rearrange("p b d -> p (b d)"),
                                 PA[half][:], ACT.Identity).then_inc(pa_r[half], 1)

        def hnT_copy(m):
            act.wait_ge(pa_w[0], m * 5 + BASE + 1)
            nc.scalar.activation(hnT[:], PA[0][:], ACT.Identity).then_inc(pa_r[0], 1)

        def tap(m, g, l):
            b, k = (1 + g) % 2, (1 + g) // 2
            if not first(m):
                at(act, s_feat, 4, m - 1, g + 1)
            if g == 0:
                act.wait_ge(s_wa, l + 1)
            act.wait_ge(pa_w[b], m * 5 + k + BASE + 1)
            if g in GTAPS:
                for s in (1, 2, 3):
                    j = PCW + 4 * g + 3 - s
                    nc.scalar.activation(prod[GTAPS.index(g)][s - 1][:], PA[b][:], ACT.Identity,
                                         scale=pla[:, j:j + 1])
            nc.scalar.activation(cv[g][:], PA[b][:], ACT.Identity, bias=pla[:, PCB + g:PCB + g + 1],
                                 scale=pla[:, PCW + 4 * g + 3:PCW + 4 * g + 4]
                                 ).then_inc(pa_r[b] if g in GTAPS else s_acc, 1)

        def silus(m, p):
            for g in range(4):
                b, k = (1 + g) % 2, (1 + g) // 2
                if g in GTAPS:
                    at(act, s_gt, len(GTAPS), m, GTAPS.index(g) + 1)
                else:
                    act.wait_ge(pa_r[b], m * 5 + k + BASE + 1)
                nc.scalar.activation(feat[p][g][:], cv[g][:], ACT.Silu).then_inc(s_feat, 1)
            for q in range(2):
                b, k = (5 + q) % 2, (5 + q) // 2
                act.wait_ge(pa_w[b], m * 5 + k + BASE + 1)
                nc.scalar.activation(sz[p][:, q, :], PA[b][:], ACT.Silu).then_inc(pa_r[b], 1)

        def tail(m, p):
            act.wait_ge(pa_w[1], m * 5 + 5 + BASE)
            nc.scalar.activation(Btok[p][:].rearrange("p b n -> p (b n)"), PA[1][:, 0:2 * NS],
                                 ACT.Identity).then_inc(pa_r[1], 1)
            at(act, pg_w, 4, m, 1)
            nc.scalar.activation(Gs[p][:].rearrange("p c t -> p (c t)"), PG[:], ACT.Identity).then_inc(pg_r, 1)

        def expv(m):
            at(act, s_v, 1, m, 1)
            nc.scalar.activation(va[2][:], va[1][:], ACT.Exp, scale=-1.0).then_inc(s_e, 1)

        def expd(m):
            at(act, s_dtxd, 1, m, 0)
            at(act, s_diff, 1, m, 1)
            nc.scalar.activation(edec[:].rearrange("p c h -> p (c h)"), va[7][:], ACT.Exp).then_inc(s_edec, 1)

        def Eint(n):
            at(act, pd_w[0], 5, n, 2)
            nc.scalar.activation(Ei[:].rearrange("p b q t -> p (b q t)"), PDk[0][:], ACT.Exp).then_inc(pd_r[0], 1)

        def Scopy(n):
            at(act, pg_w, 4, n, 2)
            nc.scalar.activation(Ssb[:].rearrange("p b d -> p (b d)"), PG[:], ACT.Identity).then_inc(pg_r, 1)

        def E(n, i):
            c, q = i // 2, i % 2
            at(act, pd_w[q], 5 - q, n, pd_turn(i) + 1)
            at(act, s_y, 8, n, max(i - 1, 0) + FREE)
            nc.scalar.activation(eb[q][:].rearrange("p h t -> p (h t)"), PDk[q][:], ACT.Exp).then_inc(pd_r[q], 1)

        def square(n, p):
            yt = yts[p]
            at(act, s_g, 1, n, 1)
            nc.scalar.activation(gsq[:], yt[:], ACT.Square).then_inc(s_gsq, 1)

        hnT_copy(0)
        expv(0)
        for g in range(4):
            tap(0, g, 0)
        expd(0)
        silus(0, 0)
        E(0, 0)
        E(0, 1)
        tail(0, 0)
        hnT_copy(1)

        def step(l, u, more=True, more2=True):
            n, p = l * UNITS + u, u % 2
            for i in range(8):
                if i == 0:
                    Eint(n)
                if i == 0:
                    Scopy(n)
                if i == 1 and not first(n):
                    square(n - 1, 1 - p)
                if more:
                    if i == 1:
                        expv(n + 1)
                    if i in TAP_AT:
                        tap(n + 1, TAP_AT.index(i), l + 1 if u == UNITS - 1 else l)
                if i < 6:
                    E(n, i + 2)
            if more:
                expd(n + 1)
                silus(n + 1, 1 - p)
                E(n + 1, 0)
                E(n + 1, 1)
                tail(n + 1, 1 - p)
            if more2:
                hnT_copy(n + 2)

        step(0, 0)
        with act.Fori(0, LAYERS - 1) as l:
            for u in range(1, UNITS):
                step(l, u)
            step(l + 1, 0)
        for u in range(1, UNITS):
            step(LAYERS - 1, u, u < UNITS - 1, u < UNITS - 2)
        square(LAYERS * UNITS - 1, 1)

    @block.vector
    def _(v):
        V = nc.vector
        cA, cB, cP, cS = Chain(v, dchA, KA), Chain(v, dchB, KB), Chain(v, dchP, KP), Chain(v, dchS, 0)
        cS.start(0)
        v.wait_ge(s_x, 16)
        for c in range(CHUNKS):
            ins = V.bn_stats(bns[:, c, :], x_tok[:, c, :])
        cS.link(ins)
        V.memset(gtmp[:], 0.0)
        for c in range(CHUNKS):
            ins = V.bn_aggr(bna[:, c, :], bns[:, c, :])
        cS.link(ins)
        V.tensor_scalar(lnv[:], bna[:, :, 1], EPS, None, ALU.add).then_inc(s_h0, 1)
        for i in range(2):
            v.wait_ge(s_modps, i + 1)
            cS.link(V.tensor_copy(mod[i][:].rearrange("p j b -> p (j b)"), PY[i][:, 0:6 * BATCH]))
        for i in range(2):
            two = mod[i][:, 2:6:3, :]
            cS.link(V.tensor_scalar(gtmp[:, 0:2, :], two, 0.0, 2.0, ALU.is_ge, ALU.mult))
            cS.link(V.scalar_tensor_tensor(gtmp[:, 2:4, :], two, -1.0, two, ALU.mult, ALU.max))
            cS.link(V.tensor_scalar(gtmp[:, 2:4, :], gtmp[:, 2:4, :], 0.25, None, ALU.max))
            cS.link(V.scalar_tensor_tensor(two, gtmp[:, 0:2, :], -1.0, gtmp[:, 2:4, :], ALU.add, ALU.mult))
        cS.link(V.tensor_scalar(modt[:, 0, :], mod[0][:, 1, :], 1.0, None, ALU.add))
        v.wait_ge(s_lc, 16 * LOADS_C)
        V.tensor_scalar(modt[:, 1, :], mod[0][:, 2, :], fnw[:, 0:1], None, ALU.mult).then_inc(s_mod, 1)
        v.wait_ge(s_h0, 2)
        for c in range(CHUNKS):
            ins = V.tensor_scalar(lnt[:, c, :], x_tok[:, c, :], bna[:, c, 0:1], lnv[:, c:c + 1],
                                  ALU.subtract, ALU.mult)
        cS.link(ins)

        def scaled(u):
            def rows(t):
                return t[:, 2 * u:2 * u + 2, None, :].to_broadcast([P, 2, 2, DM])
            h, t = (t[:, UC * u:UC * u + UC, :].rearrange("p (b i) d -> p b i d", i=2) for t in (h_tok, lnt))
            v.wait_ge(pa_r[u // 2], 2)
            cS.link(V.tensor_tensor(h, t, rows(bc[0]), ALU.mult))
            cS.link(V.tensor_tensor(h, h, rows(bc[1]), ALU.add))

        def fold_a(l):
            if not first(l):
                v.wait_ge(pa_w[0], l * UNITS * 5 - 1 + BASE)
                at(v, s_acc, UNITS * len(VTAPS), l, 0)
                for g in GTAPS:
                    v.wait_ge(pa_r[(1 + g) % 2], (l * UNITS - 1) * 5 + (1 + g) // 2 + BASE + 1)
            V.tensor_copy(pla[:], par[:, l, :]).then_inc(s_par, 1)
            v.wait_ge(s_par, 2 * l + 2)
            V.tensor_scalar(wi[:], wi_all[:, l, :], pla[:, PBN:PBN + 1], None, ALU.mult).then_inc(s_wa, 1)

        def fold_b(l):
            V.tensor_copy(plb[:], par[:, l, :]).then_inc(s_par, 1)
            v.wait_ge(s_par, 2 * l + 3)
            for q in range(2):
                ins = V.tensor_scalar(wo[:, q, :], wo_all[:, l, q, :], plb[:, PGW + q:PGW + q + 1], None, ALU.mult)
            ins.then_inc(s_wb, 1)
            v.wait_ge(s_wb, l + 1)

        def A1a(m, hs):
            cP.start(m)
            for c in range(UC):
                ins = V.tensor_tensor_reduce(out=sq[:, c, :], in0=h_tok[:, hs + c, :], in1=h_tok[:, hs + c, :],
                                             scale=1.0, scalar=0.0, op0=ALU.mult, op1=ALU.add,
                                             accum_out=ss[:, c:c + 1])
            cP.link(ins)
            V.tensor_scalar(ms[:], ss[:], 1.0 / DM, EPS, ALU.mult, ALU.add).then_inc(s_ms, 1)

        def A1b(m, hs):
            if not first(m):
                v.wait_ge(pa_w[0], m * 5 - 4 + BASE)
            at(v, s_rs, 1, m, 1)
            for c in range(UC):
                ins = V.tensor_scalar(hn[:, c, :], h_tok[:, hs + c, :], rs[:, c:c + 1], None, ALU.mult)
            ins.then_inc(s_hn, 1)

        def by_head(t):
            return t.rearrange("p (c h) -> p c h", h=HEADS)

        def dt_bias_add(m):
            cA.start(m)
            at(v, pm_w, 3, m, 1)
            V.tensor_tensor(by_head(va[0][:]), by_head(PM[:, 0:UC * HEADS]),
                            pla[:, None, PDTB:PDTB + 8].to_broadcast([P, UC, HEADS]), ALU.add).then_inc(pm_r, 1)
            at(v, pm_r, 3, m, 1)
            V.scalar_tensor_tensor(va[1][:], va[0][:], -1.0, va[0][:], ALU.mult, ALU.max).then_inc(s_v, 1)

        def softplus(m):
            e, s, s2, p = va[2][:], va[4][:], va[5][:], va[6][:]
            at(v, s_e, 1, m, 1)
            cA.link(V.tensor_scalar(va[3][:], e, 2.0, None, ALU.add))
            cA.link(V.reciprocal(va[3][:], va[3][:]))
            cA.link(V.tensor_tensor(s, e, va[3][:], ALU.mult))
            cA.link(V.tensor_tensor(s2, s, s, ALU.mult))
            cA.link(V.tensor_scalar(p, s2, 1.0 / 15, None, ALU.mult))
            for k in (13, 11, 9, 7, 5, 3):
                cA.link(V.scalar_tensor_tensor(p, p, 1.0 / k, s2, ALU.add, ALU.mult))
            cA.link(V.scalar_tensor_tensor(p, p, 1.0, s, ALU.add, ALU.mult))
            cA.link(V.tensor_scalar(va[0][:], va[0][:], 0.0, None, ALU.max))
            cA.link(V.scalar_tensor_tensor(dts[:].rearrange("p c h -> p (c h)"), p, 2.0, va[0][:],
                                           ALU.mult, ALU.add))
            V.scalar_tensor_tensor(by_head(av[:]), dts[:], -1.0,
                                   pla[:, None, PA_:PA_ + 8].to_broadcast([P, UC, HEADS]),
                                   ALU.mult, ALU.mult).then_inc(s_a, 1)

        def split(m):
            at(v, pm_w, 3, m, 2)
            cA.link(V.tensor_copy(ct[:].rearrange("p k c -> p (k c)"), PM[:, 0:2 * UC * HEADS]))
            v.sem_inc(pm_r, 1)
            r = va[3][:]
            split3(V, cA.link, [cp[:, :, k * HEADS:(k + 1) * HEADS] for k in range(PARTS)],
                   by_head(ct[:, 0, :]), by_head(r)).then_inc(s_cp, 1)
            V.tensor_tensor(va[7][:], ct[:, 1, :], ct[:, 0, :], ALU.subtract).then_inc(s_diff, 1)

        def cT_copy(m, p):
            at(v, pm_w, 3, m, 3)
            V.tensor_copy(cTs[p][:], PM[:, 0:UNIT // 2].bitcast(BF16)).then_inc(pm_r, 1)

        def taps(m, g):
            b, k = (1 + g) % 2, (1 + g) // 2
            at(v, s_acc, len(VTAPS), m, VTAPS.index(g) + 1)
            src = PA[b][:].rearrange("p (b t) -> p b t", b=2)
            acc = cv[g][:].rearrange("p (b t) -> p b t", b=2)
            for s in (1, 2, 3):
                j = PCW + 4 * g + 3 - s
                ins = V.scalar_tensor_tensor(acc[:, :, s:], src[:, :, :SEQ - s], pla[:, j:j + 1], acc[:, :, s:],
                                             ALU.mult, ALU.add)
                if s < 3:
                    cA.link(ins)
                else:
                    ins.then_inc(pa_r[b], 1)

        def v_taps(m, g):
            if g in VTAPS:
                taps(m, g)

        def dtx_(m, p):
            for j in range(2):
                b, k = (7 + j) % 2, (7 + j) // 2
                v.wait_ge(pa_w[b], m * 5 + k + BASE + 1)
                V.tensor_tensor(dtx[p][:, 2 * j:2 * j + 2, :].rearrange("p c (h d) -> p (c h) d", h=HEADS),
                                PA[b][:].rearrange("p (c d) -> p c d", d=HD),
                                dts[:, 2 * j:2 * j + 2, :].rearrange("p c h -> p (c h)")[:, :, None]
                                .to_broadcast([P, 2 * HEADS, HD]), ALU.mult).then_inc(pa_r[b], 1)
            cA.end()

        def M(n, p, i):
            c, q = i // 2, i % 2
            if i == 0:
                at(v, pg_r, 4, n, 1)
            at(v, pd_r[q], 5 - q, n, pd_turn(i) + 1 + FREE)
            V.tensor_tensor(eb[q][:], eb[q][:], Gs[p][:, c, None, :].to_broadcast([P, 4, CHUNK]),
                            ALU.mult).then_inc(s_M, 1)

        def yinter(n):
            if not first(n):
                at(v, s_yo, 1, n - 1, 1)
            at(v, pg_w, 4, n, 3)
            at(v, pd_r[0], 5, n, 2 + FREE)
            V.tensor_tensor(yi[:].rearrange("p b q t -> p (b q t)"), PG[:], Ei[:].rearrange("p b q t -> p (b q t)"),
                            ALU.mult).then_inc(pg_r, 1)

        def gate(n, p):
            yt = yts[p]
            for q in range(2):
                at(v, s_y, 8, n, 7 + q + FREE)
                ins = V.scalar_tensor_tensor(yt[:, q, :], feat[p][q][:], plb[:, PD_ + q:PD_ + q + 1], PY[q][:],
                                             ALU.mult, ALU.add)
            ins.then_inc(s_yt, 1)

        def meansq(n):
            at(v, s_ssq, 1, n, 1)
            V.tensor_scalar(ms2[:], PM[:, 0:UC], 1.0 / DI, EPS, ALU.mult, ALU.add).then_inc(s_ms2, 1)

        def residual(n, hs, turn):
            cB.start(n)
            at(v, s_rs2, 1, n, 1)
            v.wait_ge(pg_w, turn + 1)
            for c in range(UC):
                ins = V.scalar_tensor_tensor(h_tok[:, hs + c, :], PG[:, c * P:(c + 1) * P], rs2[:, c:c + 1],
                                             h_tok[:, hs + c, :], ALU.mult, ALU.add)
            cB.link(ins)
            v.sem_inc(pg_r, 1)
            cB.end()

        scaled(0)
        A1a(0, 0)
        v.wait_ge(s_ld, 16 * LOADS)
        fold_a(0)
        A1b(0, 0)
        dt_bias_add(0)
        softplus(0)
        for g in VTAPS:
            taps(0, g)
        split(0)
        cT_copy(0, 0)
        for u in range(1, UNITS):
            scaled(u)
        A1a(1, UC)
        dtx_(0, 0)
        fold_b(0)
        A1b(1, UC)

        def finish_a(k):
            for c in range(UC):
                i = k * UC + c
                ins = V.tensor_tensor_reduce(out=sq[:, c, :], in0=h_tok[:, i, :], in1=h_tok[:, i, :], scale=1.0,
                                             scalar=0.0, op0=ALU.mult, op1=ALU.add, accum_out=fs[:, i:i + 1])
            cS.link(ins)
            own = slice(k * UC, k * UC + UC)
            V.tensor_scalar(fs[:, own], fs[:, own], 1.0 / DM, EPS, ALU.mult, ALU.add).then_inc(s_fin, 1)

        def finish_b(k):
            own = slice(k * UC, k * UC + UC)
            v.wait_ge(s_finr, k + 1)
            for c in range(UC):
                i = k * UC + c
                ins = V.scalar_tensor_tensor(lnt[:, i, :], h_tok[:, i, :], fr[:, i:i + 1], bc[2][:, i // 2, :],
                                             ALU.mult, ALU.mult)
            cS.link(ins)
            cS.link(V.tensor_tensor(x_tok[:, own, :], x_tok[:, own, :], lnt[:, own, :], ALU.add))
            for c in range(UC):
                V.bn_stats(shared.bns[:, k * UC + c, :], x_tok[:, k * UC + c, :])

        def step(l, u, more=True, more2=True):
            n, p = l * UNITS + u, u % 2
            if more and u == UNITS - 1:
                fold_a(l + 1)
            for i in range(8):
                M(n, p, i)
                if i == 2:
                    yinter(n)
                if i == 4:
                    if first(n):
                        v.sem_inc(pg_r, 1)
                    else:
                        meansq(n - 1)
                if more:
                    if i == 0:
                        dt_bias_add(n + 1)
                    if i == 2:
                        softplus(n + 1)
                    if i == 5:
                        split(n + 1)
                    if i in VTAPS_AT:
                        v_taps(n + 1, VTAPS_AT.index(i))
                    if i == 7:
                        cT_copy(n + 1, 1 - p)
                if more2:
                    if i == 0:
                        A1a(n + 2, (u + 2) % UNITS * UC)
                    if i == 3:
                        A1b(n + 2, (u + 2) % UNITS * UC)
                if i == 6 and not first(n):
                    residual(n - 1, (u - 1) % UNITS * UC, n * 4 + 3)
                    if u == 0:
                        fold_b(l)
            gate(n, p)
            if more:
                dtx_(n + 1, 1 - p)

        step(0, 0)
        with v.Fori(0, LAYERS - 1) as l:
            for u in range(1, UNITS):
                step(l, u)
            step(l + 1, 0)
        for u in range(1, UNITS):
            step(LAYERS - 1, u, u < UNITS - 1, u < UNITS - 2)
            if u > 1:
                finish_b(u - 2)
            finish_a(u - 1)
        last = LAYERS * UNITS - 1
        meansq(last)
        finish_b(2)
        residual(last, (UNITS - 1) * UC, (last + 1) * 4)
        finish_a(3)
        finish_b(3)


class Norm:

    def __init__(self, nc, sb, sem, shared, mod, j, w, r, tag):
        self.nc, self.shared, self.mod, self.j = nc, shared, mod, j
        self.w, self.r = w, r
        self.bna, self.shift = sb(f"{tag}_bna", [P, CHUNKS, 2]), sb(f"{tag}_shift", [P, 2, BATCH])
        self.var, self.rstd = sb(f"{tag}_var", [P, CHUNKS]), sb(f"{tag}_rstd", [P, CHUNKS])
        self.xn, self.hT = sb(f"{tag}_xn", [P, UC, DM]), sb(f"{tag}_hT", [P, UNIT])
        self.s_var, self.s_rstd, self.s_xn, self.s_shift = (sem(f"{tag}_{n}") for n in ("var", "rstd", "xn", "shift"))

    def stats(self, v, link, lo, hi):
        V, seqs, own = self.nc.vector, slice(2 * lo, 2 * hi), slice(UC * lo, UC * hi)
        V.tensor_scalar(self.shift[:, 0, seqs], self.mod[:, self.j + 1, seqs], 1.0, None, ALU.add)
        V.tensor_scalar(self.shift[:, 1, seqs], self.mod[:, self.j, seqs], 0.0, None,
                        ALU.add).then_inc(self.s_shift, 1)
        for c in range(UC * lo, UC * hi):
            ins = V.bn_aggr(self.bna[:, c, :], self.shared.bns[:, c, :])
        link(ins)
        V.tensor_scalar(self.var[:, own], self.bna[:, own, 1], EPS, None, ALU.add).then_inc(self.s_var, 1)

    def scale(self, v, u, part):
        V, x = self.nc.vector, self.shared.x_tok
        v.wait_ge(self.s_rstd, part)
        for c in range(UC):
            i = u * UC + c
            ins = V.tensor_scalar(self.xn[:, c, :], x[:, i, :], self.bna[:, i, 0:1], self.rstd[:, bass.ds(i, 1)],
                                  ALU.subtract, ALU.mult)
        ins.then_inc(self.s_xn, 1)

    def gpsimd(self, g, part, lo, hi):
        own = slice(UC * lo, UC * hi)
        g.wait_ge(self.s_var, part)
        self.nc.gpsimd.tensor_tensor(self.rstd[:, own], self.var[:, own], self.shared.mhalf[:, own],
                                     ALU.pow).then_inc(self.s_rstd, 1)

    def tensor(self, pe, u, bk, turn):
        pe.wait_ge(self.s_xn, u + 1)
        pe.wait_ge(self.r, turn + FREE)
        for c in range(UC):
            ins = pe.transpose(bk[:, c * P:(c + 1) * P], self.xn[:, c, :], self.shared.ident[:])
        ins.then_inc(self.w, 1)

    def scalar(self, act, u, bk, turn, part):
        act.wait_ge(self.s_shift, part)
        act.wait_ge(self.w, turn + 1)
        for b in range(2):
            own = bass.ds(2 * u + b, 1)
            ins = self.nc.scalar.activation(self.hT[:, b * SEQ:(b + 1) * SEQ], bk[:, b * SEQ:(b + 1) * SEQ],
                                            ACT.Identity, bias=self.shift[:, 1, own], scale=self.shift[:, 0, own])
        ins.then_inc(self.r, 1)


def split3(V, link, parts, src, tmp):
    link(V.tensor_copy(parts[0], src))
    link(V.tensor_tensor(tmp, src, parts[0], ALU.subtract))
    link(V.tensor_copy(parts[1], tmp))
    return V.tensor_tensor(parts[2], tmp, parts[1], ALU.subtract)


def mixture(nc, ctx, bank, shared, mo, tag, more, pr=None):
    sb, sem0 = allocators(nc, ctx)
    sem = lambda n: sem0(f"{tag}_{n}")
    PGate, PUp, PCo, PAcc, PM = bank[0:2], bank[2:4], bank[4:6], bank[6], bank[7]
    (s_var, s_rstd, s_xn, s_mod, s_xT, s_hT, s_lgw, s_mix, s_down, s_lg, s_ex, s_co, s_cow, s_coT, s_chain) = (
        sem(n) for n in "var rstd xn mod xT hT lgw mix down lg ex co cow coT chain".split())
    gate_w, gate_r = [sem("gate_w0"), sem("gate_w1")], [sem("gate_r0"), sem("gate_r1")]
    up_w, up_r = [sem("up_w0"), sem("up_w1")], [sem("up_r0"), sem("up_r1")]
    co_w, co_r = [sem("co_w0"), sem("co_w1")], [sem("co_r0"), sem("co_r1")]
    acc_r = sem("acc_r")
    G, R = mo.groups, mo.routed
    BUFS = 3
    turns = [(G + 1) // 2, G // 2]
    cturns = [(R + 1) // 2, R // 2]
    bna = sb(f"{tag}_bna", [P, CHUNKS, 2])
    var, rstd = sb(f"{tag}_var", [P, CHUNKS]), sb(f"{tag}_rstd", [P, CHUNKS])
    xn, hT = sb(f"{tag}_xn", [P, CHUNKS, DM]), sb(f"{tag}_hT", [P, UNITS, UNIT])
    shift = sb(f"{tag}_shift", [P, 2, BATCH])
    lg = sb(f"{tag}_lg", [P, CHUNKS, EXPERTS])
    top = sb(f"{tag}_top", [P, CHUNKS, 8])
    idx = sb(f"{tag}_idx", [P, CHUNKS, 8], U32)
    idf = sb(f"{tag}_idf", [P, CHUNKS, 8])
    ex = sb(f"{tag}_ex", [P, CHUNKS, EXPERTS + 1])
    z, z2, z3 = (sb(f"{tag}_z{i}", [P, CHUNKS]) for i in range(3))
    wt = [sb(f"{tag}_wt{i}", [P, CHUNKS]) for i in range(2)]
    oh = [sb(f"{tag}_oh{i}", [P, CHUNKS, EXPERTS]) for i in range(2)]
    cop = sb(f"{tag}_cop", [P, CHUNKS, P], BF16)
    coT = sb(f"{tag}_coT", [P, UNITS, UNIT], BF16)
    sg = [sb(f"{tag}_sg{i}", [P, UNIT]) for i in range(2)]
    it = [sb(f"{tag}_it{i}", [P, UNIT]) for i in range(BUFS)]
    res = sb(f"{tag}_res", [P, UC, DM])
    COVERS = (slice(0, UC), slice(UC, CHUNKS))
    turned = (*PGate, *PUp)
    block = ctx.enter_context(nc.Block())

    @block.sync
    def _(sp):
        for free in (*gate_r, *up_r, *co_r, acc_r):
            sp.sem_inc(free, FREE)
        sp.sem_inc(s_down, BUFS)
        if pr is not None:
            pr.start_sync(sp)

    @block.gpsimd
    def _(g):
        nc.gpsimd.memset(cop[:].bitcast(F32), 0.0).then_inc(s_co, 1)
        for k, own in enumerate(COVERS):
            g.wait_ge(s_var, k + 1)
            nc.gpsimd.tensor_tensor(rstd[:, own], var[:, own], shared.mhalf[:, own], ALU.pow).then_inc(s_rstd, 1)
        if pr is not None:
            pr.start_gpsimd(g)

    @block.tensor
    def _(pe):
        def gate_up(u, g):
            b = g % 2
            for bk, w, r, wt_ in ((PGate[b], gate_w[b], gate_r[b], mo.gate), (PUp[b], up_w[b], up_r[b], mo.up)):
                pe.wait_ge(r, u * turns[b] + g // 2 + FREE)
                pe.matmul(bk[:], wt_[:, g, :], hT[:, u, :], start=True, stop=True).then_inc(w, 1)

        def coefficients(u, g):
            b = g % 2
            pe.wait_ge(co_r[b], u * cturns[b] + g // 2 + FREE)
            pe.matmul(PCo[b][:], mo.sel[:, g, :], coT[:, u, :], start=True, stop=True).then_inc(co_w[b], 1)

        def down(u, g):
            pe.wait_ge(s_mix, u * G + g + 1)
            if g == 0:
                pe.wait_ge(acc_r, u + FREE)
            for c in range(UC):
                ins = pe.matmul(PAcc[:, c * P:(c + 1) * P], it[g % BUFS][:, c * P:(c + 1) * P], mo.down[:, g, :],
                                start=(g == 0 and c == 0), stop=(g == G - 1), skip_group_check=True)
            ins.then_inc(s_down, 1)

        for u in range(UNITS):
            pe.wait_ge(s_xn, u + 1)
            for c in range(UC):
                ins = pe.transpose(turned[u][:, c * P:(c + 1) * P], xn[:, u * UC + c, :], shared.ident[:])
            ins.then_inc(s_xT, 1)
        for u in range(UNITS):
            pe.wait_ge(s_hT, u + 1)
            for c in range(UC):
                k = u * UC + c
                ins = pe.matmul(PM[:, k * EXPERTS:(k + 1) * EXPERTS], hT[:, u, c * P:(c + 1) * P], mo.router[:],
                                start=True, stop=True)
        ins.then_inc(s_lgw, 1)
        gate_up(0, 0)
        gate_up(0, 1)
        pe.wait_ge(s_co, 2)
        for k in range(CHUNKS):
            half = PCo[k // 8][:].bitcast(BF16)
            ins = pe.transpose(half[:, k % 8 * P:(k % 8 + 1) * P], cop[:, k, :], shared.identb[:])
            if k % 8 == 7:
                ins.then_inc(s_cow, 1)
        pe.wait_ge(s_coT, 2)
        coefficients(0, 0)

        def experts(u, last):
            for g in range(G):
                if 1 <= g < R:
                    coefficients(u, g)
                if g >= 1:
                    down(u, g - 1)
                if g >= 1 and g + 1 < G:
                    gate_up(u, g + 1)
                if last and pr is not None:
                    pr.start_tensor(pe, PM, g)
            if not last:
                gate_up(u + 1, 0)
                coefficients(u + 1, 0)
            down(u, G - 1)
            if not last:
                gate_up(u + 1, 1)

        with pe.Fori(0, UNITS - 1) as u:
            experts(u, False)
        experts(UNITS - 1, True)

    @block.scalar
    def _(act):
        act.wait_ge(s_mod, 1)
        for u in range(UNITS):
            act.wait_ge(s_xT, u + 1)
            for b in range(2):
                s = 2 * u + b
                ins = nc.scalar.activation(hT[:, u, b * SEQ:(b + 1) * SEQ], turned[u][:, b * SEQ:(b + 1) * SEQ],
                                           ACT.Identity, bias=shift[:, 1, s:s + 1], scale=shift[:, 0, s:s + 1])
            ins.then_inc(s_hT, 1)
        act.wait_ge(s_lg, 1)
        nc.scalar.activation(ex[:], ex[:], ACT.Exp).then_inc(s_ex, 1)

        def silus(u, last):
            for g in range(G):
                b = g % 2
                act.wait_ge(gate_w[b], u * turns[b] + g // 2 + 1)
                act.wait_ge(up_r[b], u * turns[b] + g // 2 + FREE)
                nc.scalar.activation(sg[b][:], PGate[b][:], ACT.Silu).then_inc(gate_r[b], 1)
                if last and pr is not None:
                    pr.start_scalar(act, PM, g)

        with act.Fori(0, UNITS - 1) as u:
            silus(u, False)
        silus(UNITS - 1, True)

    @block.vector
    def _(v):
        V = nc.vector
        first_links = len(COVERS) + 15 + (4 if mo.norm else 0)
        ch = Chain(v, s_chain, first_links)
        link = ch.link
        ch.start(0)
        for k, own in enumerate(COVERS):
            for c in range(own.start, own.stop):
                ins = V.bn_aggr(bna[:, c, :], shared.bns[:, c, :])
            link(ins)
            V.tensor_scalar(var[:, own], bna[:, own, 1], EPS, None, ALU.add).then_inc(s_var, 1)
            if k == 0:
                V.tensor_scalar(shift[:, 0, :], mo.mod[:, 4, :], 1.0, None, ALU.add)
                V.tensor_scalar(shift[:, 1, :], mo.mod[:, 3, :], 0.0, None, ALU.add).then_inc(s_mod, 1)
        for c in range(CHUNKS):
            if c in (0, UC):
                v.wait_ge(s_rstd, 1 if c == 0 else 2)
            ins = V.tensor_scalar(xn[:, c, :], shared.x_tok[:, c, :], bna[:, c, 0:1], rstd[:, c:c + 1],
                                  ALU.subtract, ALU.mult)
            if c % UC == UC - 1:
                ins.then_inc(s_xn, 1)
        v.wait_ge(shared.s_w2, 16 * shared.late)
        v.wait_ge(s_lgw, 1)
        link(V.tensor_copy(lg[:].rearrange("p c e -> p (c e)"), PM[:, 0:CHUNKS * EXPERTS]))
        for c in range(CHUNKS):
            ins = V.max(top[:, c, :], lg[:, c, :])
        link(ins)
        V.tensor_tensor(ex[:, :, EXPERTS], top[:, :, 1], top[:, :, 0], ALU.subtract)
        V.tensor_tensor(ex[:, :, 0:EXPERTS], lg[:], top[:, :, 0:1].to_broadcast([P, CHUNKS, EXPERTS]),
                        ALU.subtract).then_inc(s_lg, 1)
        for c in range(CHUNKS):
            ins = V.max_index(idx[:, c, :], top[:, c, :], lg[:, c, :])
        link(ins)
        link(V.tensor_copy(idf[:], idx[:]))
        for k in range(2):
            link(V.tensor_tensor(oh[k][:], shared.iota[:, None, :].to_broadcast([P, CHUNKS, EXPERTS]),
                                 idf[:, :, k:k + 1].to_broadcast([P, CHUNKS, EXPERTS]), ALU.is_equal))
        v.wait_ge(s_ex, 1)
        link(V.tensor_reduce(z[:], ex[:, :, 0:EXPERTS], AX.X, ALU.add))
        link(V.reciprocal(wt[0][:], z[:]))
        link(V.tensor_tensor(wt[1][:], wt[0][:], ex[:, :, EXPERTS], ALU.mult))
        if mo.norm:
            link(V.scalar_tensor_tensor(z2[:], wt[0][:], 1e-9, wt[1][:], ALU.add, ALU.add))
            link(V.reciprocal(z3[:], z2[:]))
            for k in range(2):
                link(V.tensor_tensor(wt[k][:], wt[k][:], z3[:], ALU.mult))
        for k in range(2):
            link(V.tensor_tensor(oh[k][:], oh[k][:], wt[k][:, :, None].to_broadcast([P, CHUNKS, EXPERTS]), ALU.mult))
        link(V.tensor_tensor(oh[0][:], oh[0][:], oh[1][:], ALU.add))
        v.wait_ge(s_co, 1)
        split3(V, link, [cop[:, :, k * EXPERTS:(k + 1) * EXPERTS] for k in range(PARTS)],
               oh[0][:], oh[1][:]).then_inc(s_co, 1)
        for k in range(2):
            v.wait_ge(s_cow, k + 1)
            V.tensor_copy(coT[:, 2 * k:2 * k + 2, :].rearrange("p u t -> p (u t)"),
                          PCo[k][:].bitcast(BF16)).then_inc(s_coT, 1)
        ch.end()

        def mix(u, g, link):
            b, t = g % 2, it[g % BUFS]
            v.wait_ge(up_w[b], u * turns[b] + g // 2 + 1)
            v.wait_ge(gate_r[b], u * turns[b] + g // 2 + 1 + FREE)
            before = g - BUFS if g >= BUFS else (G - 1) - (G - 1 - g) % BUFS - G
            v.wait_ge(s_down, u * G + before + 1 + BUFS)
            V.tensor_tensor(t[:], sg[b][:], PUp[b][:], ALU.mult).then_inc(up_r[b], 1)
            v.wait_ge(up_r[b], u * turns[b] + g // 2 + 1 + FREE)
            if g < R:
                v.wait_ge(co_w[b], u * cturns[b] + g // 2 + 1)
                link(V.tensor_tensor(t[:], t[:], PCo[b][:], ALU.mult))
                v.sem_inc(co_r[b], 1)
            v.sem_inc(s_mix, 1)

        def add(u, link):
            v.wait_ge(s_down, (u + 1) * G + BUFS)
            for b in range(2):
                ins = V.tensor_tensor(res[:, 2 * b:2 * b + 2, :],
                                      PAcc[:, 2 * b * DM:(2 * b + 2) * DM].rearrange("p (c d) -> p c d", d=DM),
                                      mo.gate_bc[:, 2 * u + b, None, :].to_broadcast([P, 2, DM]), ALU.mult)
            ins.then_inc(acc_r, 1)
            v.wait_ge(acc_r, u + 1 + FREE)
            x = shared.x_tok[:, bass.ds(u * UC, UC), :]
            link(V.tensor_tensor(x, x, res[:], ALU.add))
            if more:
                for c in range(UC):
                    V.bn_stats(shared.bns[:, bass.ds(u * UC + c, 1), :].rearrange("p o s -> p (o s)"),
                               shared.x_tok[:, u * UC + c, :])

        ch = Chain(v, s_chain, 1, first_links)
        ch.start(0)
        mix(0, 0, ch.link)
        ch.end()
        ch = Chain(v, s_chain, R + 1, first_links + 1)
        with v.Fori(0, UNITS - 1) as u:
            ch.start(u)
            for g in range(1, G):
                mix(u, g, ch.link)
            mix(u + 1, 0, ch.link)
            add(u, ch.link)
            ch.end()
        u = UNITS - 1
        ch.start(u)
        if pr is not None:
            pr.start_vector(v, PM, 0)
        for g in range(1, G):
            mix(u, g, ch.link)
            if pr is not None:
                pr.start_vector(v, PM, g)
        add(u, ch.link)


class Projections:

    TURNS = 4
    SLOTS_Q, SLOTS_K = (0, 0, 0, 1, 1, 2), (0, 1, 2, 0, 1, 0)
    LOADS = 16 * len(SLOTS_Q)
    ROWS = 96
    SCALE = float(AD) ** -0.5
    LINKS = 1 + 4 * 2

    def __init__(self, nc, sb, sem, shared):
        self.nc, self.shared = nc, shared
        self.px_w, self.px_r = sem("px_w"), sem("px_r")
        self.s_zero, self.s_par, self.s_vn, self.s_vp, self.s_qs, self.s_ks, self.s_chain, self.s_gchain = (
            sem(f"pr_{n}") for n in "zero par vn vp qs ks chain gchain".split())
        self.s_st = [sem("pr_st0"), sem("pr_st1")]
        self.norm = Norm(nc, sb, sem, shared, shared.mod[1], 0, self.px_w, self.px_r, "at")
        self.wq = sb("wq", [P, 2, DM])
        self.qk = [sb("qT", [P, UNIT]), sb("kT", [P, UNIT])]
        self.parts = sb("parts", [P, 2 * PARTS, UNIT], BF16)
        self.zero = sb("zero", [P, SEQ])
        self.rest = [sb("qrest", [P, SEQ]), sb("krest", [P, SEQ])]
        self.stack = [sb(f"stack{b}", [P, AH, 2, SEQ], BF16) for b in range(2)]
        self.bq = sb("bq", [P, 1])
        self.Vn = sb("Vn", [P, UC, DM])
        self.Vp = sb("Vp", [P, UC, AH, 32])

    def stacks(self, sp, n, b):
        sp.wait_ge(self.s_qs, 2 * n + b + 1)
        sp.wait_ge(self.s_ks, 2 * n + b + 1)
        for s, (q, k) in enumerate(zip(self.SLOTS_Q, self.SLOTS_K)):
            two = slice(q, PARTS + k + 1, PARTS + k - q)
            sp.dma_start(self.stack[b][AD * s:AD * s + AD, :, :, :],
                         self.parts[:, two, b * SEQ:(b + 1) * SEQ]).then_inc(self.s_st[b], 16)

    def start_sync(self, sp):
        sp.sem_inc(self.px_r, FREE)
        sp.wait_ge(self.s_zero, 1)
        for b in range(2):
            self.stacks(sp, 0, b)
        for b in range(2):
            sp.wait_ge(self.s_st[b], self.LOADS)

    def split_k(self, b, link):
        G, s = self.nc.gpsimd, slice(b * SEQ, (b + 1) * SEQ)
        k, (p0, p1, p2), r = self.qk[1][:, s], (self.parts[:, PARTS + j, s] for j in range(PARTS)), self.rest[1][:]
        link(G.tensor_tensor(p0, k, self.zero[:], ALU.add))
        link(G.tensor_tensor(r, k, p0, ALU.subtract))
        link(G.tensor_tensor(p1, r, self.zero[:], ALU.add))
        link(G.tensor_tensor(p2, r, p1, ALU.subtract))

    def values(self, b):
        for c in range(2 * b, 2 * b + 2):
            v = self.Vn[:, c, :].rearrange("p (h d) -> p h d", d=AD)
            ins = self.nc.gpsimd.tensor_tensor(self.Vp[:, c, :, 0:AD], v,
                                               self.zero[:, 0:DM].rearrange("p (h d) -> p h d", d=AD), ALU.add)
        ins.then_inc(self.s_vp, 1)

    def start_gpsimd(self, g):
        G = self.nc.gpsimd
        for t in self.stack:
            G.memset(t[:].bitcast(F32), 0.0)
        G.memset(self.zero[:], 0.0)
        G.memset(self.Vp[:], 0.0).then_inc(self.s_zero, 1)
        g.wait_ge(self.s_zero, 1)
        G.memset(self.Vp[:, :, :, AD], 1.0)
        self.norm.gpsimd(g, 1, 0, 1)
        ch = Chain(g, self.s_gchain, 2 * 4)
        ch.start(0)
        for b in range(2):
            g.wait_ge(self.px_r, 3 + FREE)
            self.split_k(b, ch.link)
            g.sem_inc(self.s_ks, 1)
        ch.end()
        for b in range(2):
            g.wait_ge(self.s_vn, 1)
            self.values(b)

    def project(self, pe, bk, x, k):
        hT = self.norm.hT
        pe.wait_ge(self.px_r, x + 1 + k + FREE)
        if k < 2:
            pe.matmul(bk[:], self.wq[:, k, :], hT[:], start=True, stop=True).then_inc(self.px_w, 1)
        else:
            for c in range(UC):
                ins = pe.matmul(bk[:, c * DM:(c + 1) * DM], hT[:, c * P:(c + 1) * P],
                                self.shared.wqkv[:, 2 * DM:3 * DM], start=True, stop=True)
            ins.then_inc(self.px_w, 1)

    def start_tensor(self, pe, bk, g):
        if g == 2:
            self.norm.tensor(pe, 0, bk, 0)
        elif g == 3:
            pe.wait_ge(self.s_par, 1)
        if g in (3, 4, 5):
            self.project(pe, bk, 0, g - 3)

    def evacuate(self, act, bk, x, k):
        bias, scale = ((self.bq[:, 0:1], self.SCALE), (self.shared.bqk[:, 1:2], 1.0))[k]
        act.wait_ge(self.px_w, x + 2 + k)
        self.nc.scalar.activation(self.qk[k][:], bk[:], ACT.Identity, bias=bias, scale=scale).then_inc(self.px_r, 1)

    def start_scalar(self, act, bk, g):
        if g == 3:
            act.wait_ge(self.s_par, 1)
            self.norm.scalar(act, 0, bk, 0, 1)
        elif g in (4, 5):
            self.evacuate(act, bk, 0, g - 4)

    def split_q(self, b, link):
        s = slice(b * SEQ, (b + 1) * SEQ)
        link(split3(self.nc.vector, link, [self.parts[:, j, s] for j in range(PARTS)], self.qk[0][:, s],
                    self.rest[0][:]))

    def add_bias(self, v, bk, x):
        v.wait_ge(self.px_w, x + 4)
        self.nc.vector.tensor_tensor(self.Vn[:], bk[:].rearrange("p (c d) -> p c d", d=DM),
                                     self.shared.bv[:, None, :].to_broadcast([P, UC, DM]),
                                     ALU.add).then_inc(self.px_r, 1)
        v.wait_ge(self.px_r, x + 4 + FREE)
        v.sem_inc(self.s_vn, 1)

    def start_vector(self, v, bk, g):
        V = self.nc.vector
        if g == 0:
            self.ch = Chain(v, self.s_chain, self.LINKS)
            self.ch.start(0)
            for k in range(2):
                V.tensor_copy(self.wq[:, k, :].rearrange("p (c h) -> p c h", c=AD),
                              self.shared.wqkv[:, k * DM:(k + 1) * DM].rearrange("p (h c) -> p c h", c=AD))
            V.tensor_scalar(self.bq[:], self.shared.bqk[:, 0:1], self.SCALE, None, ALU.mult).then_inc(self.s_par, 1)
            self.norm.stats(v, self.ch.link, 0, 1)
        elif g == 1:
            self.norm.scale(v, 0, 1)
        elif g == 5:
            v.wait_ge(self.px_r, 2 + FREE)
            for b in range(2):
                self.split_q(b, self.ch.link)
                v.sem_inc(self.s_qs, 1)
            self.ch.end()
        elif g == 6:
            self.add_bias(v, bk, 0)


def attention(nc, ctx, bank, shared, pr):
    sb, sem = allocators(nc, ctx)
    PS, PT, PO, PX, PZ = bank[0:2], bank[2:4], bank[4:6], bank[6], bank[7]
    ps_w, ps_r = [sem("ps_w0"), sem("ps_w1")], [sem("ps_r0"), sem("ps_r1")]
    pt_w, pt_r = [sem("pt_w0"), sem("pt_w1")], [sem("pt_r0"), sem("pt_r1")]
    px_w, px_r, pz_w, pz_r = pr.px_w, pr.px_r, sem("pz_w"), sem("pz_r")
    po_r = [sem("po_r0"), sem("po_r1")]
    s_mp, s_pv, s_on, s_chain = (sem(f"at_{n}") for n in "mp pv on chain".split())
    norm, stack, ROWS, LOADS, s_st = pr.norm, pr.stack, pr.ROWS, pr.LOADS, pr.s_st
    LEADX, XT = pr.TURNS, 12
    GH = 8
    QH = 4
    SEQG = AH // GH
    mx = sb("mx", [P, 2, QH])
    mt = sb("mt", [P, 2, QH])
    mp = sb("mp", [P, 2, P], BF16)
    mT = [sb(f"mT{i}", [P, SEQ], BF16) for i in range(2)]
    Pt = [sb(f"Pt{i}", [P, 2, SEQ]) for i in range(GH)]
    OT = sb("OT", [P, 4, SEQ])
    rec = sb("rec", [P, AH])
    on = sb("on", [P, 2, DM])
    oT = sb("oT", [P, SEQ])
    res = sb("at_res", [P, 2, DM])
    block = ctx.enter_context(nc.Block())

    def turn(eng, g, h):
        i = g * GH + h
        return i, i % 2, i // 2

    @block.sync
    def _(sp):
        for free in (*ps_r, *pt_r, *po_r, pz_r):
            sp.sem_inc(free, FREE)
        with sp.Fori(0, UNITS - 1) as u:
            for b in range(2):
                pr.stacks(sp, u + 1, b)

    @block.gpsimd
    def _(g):
        norm.gpsimd(g, 2, 1, UNITS)
        ch = Chain(g, pr.s_gchain, 2 * 4)
        with g.Fori(0, UNITS - 1) as u:
            ch.start(u + 1)
            for b in range(2):
                g.wait_ge(px_r, LEADX + u * XT + 3 + FREE)
                g.wait_ge(s_st[b], (u + 1) * LOADS)
                pr.split_k(b, ch.link)
                g.wait_ge(pt_w[1], u * AH + (b + 1) * GH)
                g.sem_inc(pr.s_ks, 1)
                g.wait_ge(pr.s_vn, u + 2)
                g.wait_ge(s_pv, u * 8 + 4 * (b + 1))
                pr.values(b)
            ch.end()

    @block.tensor
    def _(pe):
        def scores(n, g, h):
            i, bk, before = turn(pe, g, h)
            b, head = g // SEQG, i % AH
            if h == 0:
                pe.wait_ge(s_st[b], (n + 1) * LOADS)
            pe.wait_ge(ps_r[bk], n * AH + before + FREE)
            for c in range(2):
                ins = pe.matmul(PS[bk][:, c * SEQ:(c + 1) * SEQ], stack[b][0:ROWS, head, 0, c * P:(c + 1) * P],
                                stack[b][0:ROWS, head, 1, :], start=True, stop=True)
            ins.then_inc(ps_w[bk], 1)

        def maxima(n, g, q):
            quad = n * 8 + 2 * g + q
            pe.wait_ge(s_mp, quad + 1)
            pe.wait_ge(pz_r, quad + FREE)
            dst = PZ[:, 0:P].bitcast(BF16)
            for c in range(2):
                ins = pe.transpose(dst[:, c * P:(c + 1) * P], mp[:, c, :], shared.identb[:])
            ins.then_inc(pz_w, 1)

        def scores_T(n, g, h):
            i, bk, before = turn(pe, g, h)
            b, head = g // SEQG, i % AH
            if h % QH == 0:
                pe.wait_ge(pz_r, n * 8 + 2 * g + h // QH + 1 + FREE)
            pe.wait_ge(pt_r[bk], n * AH + before + FREE)
            for c in range(2):
                half = slice(c * SEQ, (c + 1) * SEQ)
                pe.matmul(PT[bk][:, half], shared.selm[0:ROWS, h % QH, :], mT[h // QH][0:ROWS, :],
                          start=True, stop=False)
                ins = pe.matmul(PT[bk][:, half], stack[b][0:ROWS, head, 1, c * P:(c + 1) * P],
                                stack[b][0:ROWS, head, 0, :], start=False, stop=True)
            ins.then_inc(pt_w[bk], 1)

        def weigh(n, g, q):
            b, k, i = g // SEQG, g % SEQG, g * GH + q * QH
            for bk in range(2):
                pe.wait_ge(pt_r[bk], n * AH + i // 2 + 2 + FREE)
            if q == 0:
                pe.wait_ge(pr.s_vp, 2 * n + b + 1)
                pe.wait_ge(po_r[k], 2 * n + b + FREE)
            for c in range(2):
                for r in range(QH):
                    ins = pe.matmul(PO[k][32 * r:32 * r + 32, q * SEQ:(q + 1) * SEQ],
                                    pr.Vp[:, 2 * b + c, k * GH + q * QH + r, :], Pt[q * QH + r][:, c, :],
                                    start=(c == 0), stop=(c == 1))
            ins.then_inc(s_pv, 1)

        def turn_o(n, b, c, x):
            if c == 0:
                for k in range(2):
                    pe.wait_ge(po_r[k], 2 * n + b + 1 + FREE)
            pe.wait_ge(px_r, x + c + FREE)
            for q in range(4):
                ins = pe.transpose(PX[:, q * P:(q + 1) * P], OT[:, q, c * P:(c + 1) * P], shared.ident[:])
            ins.then_inc(px_w, 1)

        def turn_on(n, b):
            pe.wait_ge(s_on, (2 * n + b) * 2 + 2)
            for c in range(2):
                ins = pe.transpose(PX[:, c * P:(c + 1) * P], on[:, c, :], shared.ident[:])
            ins.then_inc(px_w, 1)

        def proj(x):
            pe.wait_ge(px_r, x + 3 + FREE)
            for c in range(2):
                ins = pe.matmul(PX[:, c * DM:(c + 1) * DM], oT[:, c * P:(c + 1) * P], shared.wproj[:],
                                start=True, stop=True)
            ins.then_inc(px_w, 1)

        def segment(n, g, nn, gg, x, before, out=None, more=True):
            for h in range(GH):
                scores_T(n, g, h)
                if gg is not None:
                    scores(nn, gg, h)
                if h == 0 and before is not None:
                    weigh(*before, 1)
                elif h == 2:
                    maxima(n, g, 1)
                elif h == 7:
                    weigh(n, g, 0)
                elif h == 6 and gg is not None:
                    maxima(nn, gg, 0)
                if g == 1 and more:
                    if h == 2:
                        norm.tensor(pe, n + 1, PX, x)
                    elif h in (5, 7):
                        pr.project(pe, PX, x, (h - 5) // 2)
                if g == 2 and more and h == 0:
                    pr.project(pe, PX, x - 4, 2)
                if out is not None:
                    if h in (2, 4):
                        turn_o(*out, h // 2 - 1, x)
                    elif h == 6:
                        turn_on(*out)
            if out is not None:
                proj(x)

        for h in range(GH):
            scores(0, 0, h)
            if h == 5:
                maxima(0, 0, 0)
        segment(0, 0, 0, 1, 0, None)
        with pe.Fori(0, UNITS - 1) as u:
            x = u * XT + LEADX
            segment(u, 1, u, 2, x, (u, 0))
            segment(u, 2, u, 3, x + 4, (u, 1), (u, 0))
            segment(u, 3, u + 1, 0, x, (u, 2))
            segment(u + 1, 0, u + 1, 1, x + 8, (u, 3), (u, 1))
        u, x = UNITS - 1, (UNITS - 1) * XT + LEADX
        segment(u, 1, u, 2, x, (u, 0), more=False)
        segment(u, 2, u, 3, x, (u, 1), (u, 0), more=False)
        segment(u, 3, u, None, x, (u, 2), more=False)
        weigh(u, 3, 1)
        for c in range(2):
            turn_o(u, 1, c, x + 4)
        turn_on(u, 1)
        proj(x + 4)

    @block.scalar
    def _(act):
        def sums(n, g, after):
            k = g % SEQG
            act.wait_ge(s_pv, n * 8 + 2 * g + 2)
            if after is not None:
                act.wait_ge(px_w, after)
            nc.scalar.activation(OT[:, 2 * k:2 * k + 2, :].rearrange("p g t -> p (g t)"), PO[k][:],
                                 ACT.Identity).then_inc(po_r[k], 1)

        def turned(x):
            act.wait_ge(px_w, x + 3)
            nc.scalar.activation(oT[:], PX[:, 0:SEQ], ACT.Identity).then_inc(px_r, 1)

        def segment(n, g, x, before=None, after=None, out=None, more=True):
            for h in range(GH):
                i, bk, earlier = turn(act, g, h)
                act.wait_ge(pt_w[bk], n * AH + earlier + 1)
                if before is not None and h % QH == 0:
                    act.wait_ge(s_pv, n * 8 + i // QH - 1)
                nc.scalar.activation(Pt[h][:].rearrange("p c t -> p (c t)"), PT[bk][:],
                                     ACT.Exp).then_inc(pt_r[bk], 1)
                if h == 1 and before is not None:
                    sums(*before, after)
                if out is not None and h == 7:
                    turned(x)
                if g == 1 and more:
                    if h == 3:
                        norm.scalar(act, n + 1, PX, x, 2)
                    elif h in (5, 7):
                        if h == 5:
                            act.wait_ge(pr.s_qs, 2 * n + 2)
                            act.wait_ge(pr.s_ks, 2 * n + 2)
                        pr.evacuate(act, PX, x, (h - 5) // 2)

        segment(0, 0, 0)
        with act.Fori(0, UNITS - 1) as u:
            x = u * XT + LEADX
            segment(u, 1, x, (u, 0), x)
            segment(u, 2, x + 4, (u, 1), None, (u, 0))
            segment(u, 3, x, (u, 2), x + 6)
            segment(u + 1, 0, x + 8, (u, 3), None, (u, 1))
        u, x = UNITS - 1, (UNITS - 1) * XT + LEADX
        segment(u, 1, x, (u, 0), x, more=False)
        segment(u, 2, x, (u, 1), None, (u, 0), more=False)
        segment(u, 3, x, (u, 2), x + 2, more=False)
        sums(u, 3, None)
        turned(x + 4)

    @block.vector
    def _(v):
        V = nc.vector

        def release_q(n, b):
            v.wait_ge(pt_w[1], (n - 1) * AH + (b + 1) * GH)
            v.sem_inc(pr.s_qs, 1)

        def reduce(n, g, h):
            i, bk, before = turn(v, g, h)
            v.wait_ge(ps_w[bk], n * AH + before + 1)
            return V.tensor_reduce(mx[:, :, h % QH], PS[bk][:].rearrange("p (c t) -> p c t", c=2), AX.X,
                                   ALU.max).then_inc(ps_r[bk], 1)

        def maxima(n, g, q, link):
            v.wait_ge(ps_r[1], n * AH + (g * GH + (q + 1) * QH) // 2 + FREE)
            if not (g == 0 and q == 0 and isinstance(n, int)):
                v.wait_ge(pz_w, n * 8 + 2 * g + q)
            split3(V, link, [mp[:, :, k * QH:(k + 1) * QH] for k in range(PARTS)], mx[:], mt[:]).then_inc(s_mp, 1)

        def maxima_T(n, g, q):
            v.wait_ge(pz_w, n * 8 + 2 * g + q + 1)
            V.tensor_copy(mT[q][:], PZ[:, 0:P].bitcast(BF16)).then_inc(pz_r, 1)

        def normalise(n, b, c, x, link):
            o = PX[:].rearrange("p (h d) -> p h d", d=32)
            v.wait_ge(px_w, x + c + 1)
            link(V.reciprocal(rec[:], o[:, :, AD]))
            V.tensor_tensor(on[:, c, :].rearrange("p (h d) -> p h d", d=AD), o[:, :, 0:AD],
                            rec[:, :, None].to_broadcast([P, AH, AD]), ALU.mult).then_inc(px_r, 1)
            v.wait_ge(px_r, x + c + 1 + FREE)
            v.sem_inc(s_on, 1)

        def add(n, b, x, link):
            v.wait_ge(px_w, x + 4)
            V.tensor_tensor(res[:], PX[:, 0:SEQ].rearrange("p (c d) -> p c d", d=DM),
                            shared.bp[:, None, :].to_broadcast([P, 2, DM]), ALU.add).then_inc(px_r, 1)
            v.wait_ge(px_r, x + 4 + FREE)
            link(V.tensor_tensor(res[:], res[:], shared.bc[4][:, 2 * n + b, None, :].to_broadcast([P, 2, DM]),
                                 ALU.mult))
            xs = shared.x_tok[:, bass.ds(n * UC + 2 * b, 2), :]
            link(V.tensor_tensor(xs, xs, res[:], ALU.add))
            for c in range(2):
                i = n * UC + 2 * b + c
                V.bn_stats(shared.bns[:, bass.ds(i, 1), :].rearrange("p o s -> p (o s)"), shared.x_tok[:, i, :])

        def segment(n, g, nn, gg, x, link, out=None, more=False):
            for h in range(GH):
                if gg is not None:
                    reduce(nn, gg, h)
                    if h % QH == QH - 1:
                        maxima(nn, gg, h // QH, link)
                if h == 2:
                    maxima_T(n, g, 1)
                elif h == 6 and gg is not None:
                    maxima_T(nn, gg, 0)
                if out is not None:
                    if h in (2, 4):
                        normalise(*out, h // 2 - 1, x, link)
                    elif h == 7:
                        add(*out, x, link)
                if more:
                    if g == 1 and h == 0:
                        norm.scale(v, n + 1, 2)
                    elif g == 1 and h == 7:
                        v.wait_ge(px_r, x + 2 + FREE)
                        v.wait_ge(s_st[0], (n + 1) * LOADS)
                        pr.split_q(0, link)
                        release_q(n + 1, 0)
                    elif g == 2 and h == 0:
                        v.wait_ge(pr.s_vp, 2 * n + 2)
                        pr.add_bias(v, PX, x - 4)
                    elif g == 3 and h == 6:
                        v.wait_ge(s_st[1], (n + 1) * LOADS)
                        pr.split_q(1, link)
                    elif g == 0 and h == 0:
                        release_q(n, 1)

        LEAD, BODY = 1 + 3 * 4, 4 * 2 + 3 * 8 + 2 * 4
        V.memset(mp[:], 0.0)
        ch = Chain(v, s_chain, LEAD)
        ch.start(0)
        norm.stats(v, ch.link, 1, UNITS)
        for h in range(GH):
            reduce(0, 0, h)
            if h % QH == QH - 1:
                maxima(0, 0, h // QH, ch.link)
            if h == 5:
                maxima_T(0, 0, 0)
        segment(0, 0, 0, 1, 0, ch.link)
        ch.end()
        ch = Chain(v, s_chain, BODY, LEAD)
        with v.Fori(0, UNITS - 1) as u:
            x = u * XT + LEADX
            ch.start(u)
            segment(u, 1, u, 2, x, ch.link, more=True)
            segment(u, 2, u, 3, x + 4, ch.link, (u, 0), more=True)
            segment(u, 3, u + 1, 0, x, ch.link, more=True)
            segment(u + 1, 0, u + 1, 1, x + 8, ch.link, (u, 1), more=True)
            ch.end()
        u, x = UNITS - 1, (UNITS - 1) * XT + LEADX
        ch.start(u)
        segment(u, 1, u, 2, x, ch.link)
        segment(u, 2, u, 3, x, ch.link, (u, 0))
        segment(u, 3, u, None, x, ch.link)
        for c in range(2):
            normalise(u, 1, c, x + 4, ch.link)
        add(u, 1, x + 4, ch.link)


def store(nc, ctx, shared, out):
    s_out = ctx.enter_context(nc.semaphore("s_store"))
    block = ctx.enter_context(nc.Block())

    @block.sync
    def _(sp):
        sp.dma_start(out.rearrange("b (i p) d -> p (b i) d", p=P), shared.x_tok[:]).then_inc(s_out, 16)
        sp.wait_ge(s_out, 16)


def first(m):
    return isinstance(m, int) and m == 0


KA, KB, KP = 14 + 4 + 2 * len(VTAPS), 1, 1


class Chain:

    def __init__(self, eng, sem, per, base=0):
        self.eng, self.sem, self.per, self.base = eng, sem, per, base

    def start(self, n):
        self.n, self.k = n, 0

    def link(self, ins):
        self.k += 1
        ins.then_inc(self.sem, 1)
        self.eng.wait_ge(self.sem, self.n * self.per + self.base + self.k)

    def end(self):
        assert self.k == self.per, self.k


INPUTS = {"x": "L0_attn_x", "W_in": "L0_attn_W_in", "conv_w": "L0_attn_conv_w", "conv_b": "L0_attn_conv_b",
        "dt_bias": "L0_attn_dt_bias", "A_log": "L0_attn_A_log", "D": "L0_attn_D",
        "gate_norm_w": "L0_attn_gate_norm_w", "W_out": "L0_attn_W_out", "block_norm_w": "L0_attn_block_norm_w",
        "final_norm_w": "L0_attn_final_norm_w", "c0": "L0_c", "wmod0": "L0_wmod", "c1": "L1_c", "wmod1": "L1_wmod",
        "router0": "L0_ffn_router_w", "gate0": "L0_ffn_gate_w", "up0": "L0_ffn_up_w", "down0": "L0_ffn_down_w",
        "sgate0": "L0_ffn_shared_gate_w", "sup0": "L0_ffn_shared_up_w", "sdown0": "L0_ffn_shared_down_w",
        "w_qkv": "L1_attn_w_qkv", "b_qkv": "L1_attn_b_qkv", "w_proj": "L1_attn_w_proj", "b_proj": "L1_attn_b_proj",
        "router1": "L1_ffn_router_w", "gate1": "L1_ffn_wg_r", "up1": "L1_ffn_wu_r", "down1": "L1_ffn_wd_r",
        "sgate1": "L1_ffn_wg_s", "sup1": "L1_ffn_wu_s", "sdown1": "L1_ffn_wd_s"}


def kernel(**inputs):
    import numpy as np
    import concourse.bacc as bacc
    from concourse.bass_utils import run_bass_kernel_spmd

    nc = bacc.Bacc("TRN2", target_bir_lowering=False, num_devices=1)
    arrays, args = {}, {}
    for arg, name in INPUTS.items():
        a = np.ascontiguousarray(inputs[name])
        arrays[f"in_{arg}"] = a
        args[arg] = nc.dram_tensor(f"in_{arg}", a.shape, mybir.dt.from_np(a.dtype), kind="ExternalInput").ap()
    args["out"] = nc.dram_tensor("out_x", (BATCH, SEQ, DM), F32, kind="ExternalOutput").ap()
    program(nc, **args)
    r = run_bass_kernel_spmd(nc, [arrays], core_ids=[0])
    return r.results[0]["out_x"]
```
